# Optimizing a Trainium2 kernel written in Bass

```python
import numpy as np
import jax
import jax.numpy as jnp

def _softmax(x, axis=-1):
    return jax.nn.softmax(x, axis=axis)

def _gelu(x):
    return jax.nn.gelu(x, approximate=True)

def _silu(x):
    return jax.nn.silu(x)

def _sigmoid(x):
    return jax.nn.sigmoid(x)

def _layernorm(x, axis=-1, eps=1e-05):
    m = jnp.mean(x, axis=axis, keepdims=True)
    v = jnp.var(x, axis=axis, keepdims=True)
    return (x - m) / jnp.sqrt(v + eps)

def _scatter_add(tgt, idx, src, axis=0):
    return tgt.at[idx].add(src)

def _segment_sum(src, seg, n):
    return jax.ops.segment_sum(src, seg, n)
kernel_name = 'mk_decoder_postln_d1_seqx_r4_90c8bb'

def setup_inputs(seed: int=0):
    np.random.seed(seed)
    _w = jnp.asarray

    def _rec_inputs():
        import jax
        import jax.numpy as jnp
        _rk = jax.random.key(seed)
        x = -0.000125 + 0.9999 * jax.random.normal(jax.random.fold_in(_rk, 1), (4, 512, 256), jnp.float32)
        _lenS = 512 - jax.random.randint(jax.random.fold_in(_rk, 7), (4,), 0, max(1, 512 // 4) + 1, jnp.int32)
        _lenS2 = 512 - jax.random.randint(jax.random.fold_in(_rk, 8), (4,), 0, max(1, 512 // 4) + 1, jnp.int32)
        _ctx_1024P = jax.random.normal(jax.random.fold_in(_rk, 11), (4, 16, 256), jnp.float32)
        _ctx_1024c = jax.random.dirichlet(jax.random.fold_in(_rk, 511), 0.3 * jnp.ones((16,), jnp.float32), (4, 512))
        _ctx_1024t = jnp.einsum('bsk,bkd->bsd', _ctx_1024c, _ctx_1024P)
        _ctx_1024t = _ctx_1024t * jax.lax.rsqrt(jnp.mean(jnp.square(_ctx_1024t)) + 1e-12) * 0.953939
        ctx_1024 = -1.52775e-05 + 0.999936 * (_ctx_1024t + 0.3 * jax.random.normal(jax.random.fold_in(_rk, 611), (4, 512, 256), jnp.float32))
        return (x, ctx_1024)
    x, ctx_1024 = _rec_inputs()

    def _L0_attn_setup():
        import jax, jax.numpy as jnp
        import numpy as np
        B, T, D, H, K, V, F = (4, 1024, 256, 8, 128, 128, 1024)
        EPS = 1e-05

        def layernorm(x, w, b):
            m = jnp.mean(x, -1, keepdims=True)
            v = jnp.var(x, -1, keepdims=True)
            return (x - m) * jax.lax.rsqrt(v + EPS) * w + b

        def l2norm(x):
            return x * jax.lax.rsqrt(jnp.sum(x * x, -1, keepdims=True) + 1e-06)

        def gdn_recurrence(q, k, v, alpha, beta):
            qT = jnp.moveaxis(q, 1, 0)
            kT = jnp.moveaxis(k, 1, 0)
            vT = jnp.moveaxis(v, 1, 0)
            aT = jnp.moveaxis(alpha, 1, 0)
            bT = jnp.moveaxis(beta, 1, 0)

            def step(S, inp):
                q_t, k_t, v_t, a_t, b_t = inp
                kS = jnp.einsum('bhk,bhkv->bhv', k_t, S)
                bk = (b_t[..., None] * k_t)[..., :, None]
                S = a_t[..., None, None] * (S - bk * kS[..., None, :]) + bk * v_t[..., None, :]
                o = jnp.einsum('bhk,bhkv->bhv', q_t, S)
                return (S, o)
            S0 = jnp.zeros((q.shape[0], H, K, V), q.dtype)
            _, oT = jax.lax.scan(step, S0, (qT, kT, vT, aT, bT))
            return jnp.moveaxis(oT, 0, 1)
        key = jax.random.key(seed)
        ks = jax.random.split(key, 12)
        s = 0.02
        return {'x': jax.random.normal(ks[0], (B, T, D), jnp.float32), 'Wq': jax.random.normal(ks[1], (D, H * K), jnp.float32) * s, 'Wk': jax.random.normal(ks[2], (D, H * K), jnp.float32) * s, 'Wv': jax.random.normal(ks[3], (D, H * V), jnp.float32) * s, 'Wb': jax.random.normal(ks[4], (D, H), jnp.float32) * s, 'Wa': jax.random.normal(ks[5], (D, H), jnp.float32) * s, 'Wo': jax.random.normal(ks[6], (H * V, D), jnp.float32) * s, 'ln1_w': jnp.ones((D,), jnp.float32), 'ln1_b': jnp.zeros((D,), jnp.float32), 'ln2_w': jnp.ones((D,), jnp.float32), 'ln2_b': jnp.zeros((D,), jnp.float32), 'W1': jax.random.normal(ks[7], (D, F), jnp.float32) * s, 'b1': jnp.zeros((F,), jnp.float32), 'W2': jax.random.normal(ks[8], (F, D), jnp.float32) * s, 'b2': jnp.zeros((D,), jnp.float32)}
    _L0_attn_all = _L0_attn_setup()
    _L0_attn_in = {k: v for k, v in _L0_attn_all.items() if k in ('Wq', 'Wk', 'Wv', 'Wb', 'Wa', 'Wo', 'ln1_w', 'ln1_b', 'ln2_w', 'ln2_b', 'W1', 'b1', 'W2', 'b2')}
    del _L0_attn_all

    def _L0_xattn_setup():
        import math
        import jax, jax.numpy as jnp
        import numpy as np
        B, L, D = (8, 1024, 256)
        H = 8
        DK = D // H
        K_FACTOR = 2
        key = jax.random.key(seed)
        ks = jax.random.split(key, 11)
        s = 0.02
        return {'queries': jax.random.normal(ks[0], (B, L, D), dtype=jnp.float32), 'keys': jax.random.normal(ks[1], (B, L, D), dtype=jnp.float32), 'values': jax.random.normal(ks[2], (B, L, D), dtype=jnp.float32), 'Wq': jax.random.normal(ks[3], (D, H * DK), dtype=jnp.float32) * s, 'bq': jnp.zeros((H * DK,), dtype=jnp.float32), 'Wk': jax.random.normal(ks[4], (D, H * DK), dtype=jnp.float32) * s, 'bk': jnp.zeros((H * DK,), dtype=jnp.float32), 'Wv': jax.random.normal(ks[5], (D, H * DK), dtype=jnp.float32) * s, 'bv': jnp.zeros((H * DK,), dtype=jnp.float32), 'Wo': jax.random.normal(ks[6], (H * DK, D), dtype=jnp.float32) * s, 'bo': jnp.zeros((D,), dtype=jnp.float32)}
    _L0_xattn_all = _L0_xattn_setup()
    _L0_xattn_in = {k: v for k, v in _L0_xattn_all.items() if k in ('Wq', 'bq', 'Wk', 'bk', 'Wv', 'bv', 'Wo', 'bo')}
    del _L0_xattn_all

    def _L0_ffn_setup():
        import jax, jax.numpy as jnp
        import numpy as np
        H, E, DFF = (256, 8, 1024)
        key = jax.random.key(seed)
        ks = jax.random.split(key, 7)
        s = lambda *shape: 1.0 / np.sqrt(shape[-2] if len(shape) > 1 else shape[-1])
        x = jax.random.normal(ks[0], (2, 512, H), dtype=jnp.float32)
        Wr = jax.random.normal(ks[1], (H, E), dtype=jnp.float32) * (1.0 / np.sqrt(H))
        br = jnp.zeros((E,), dtype=jnp.float32)
        W1 = jax.random.normal(ks[2], (E, H, DFF), dtype=jnp.float32) * (1.0 / np.sqrt(H))
        b1 = jnp.zeros((E, DFF), dtype=jnp.float32)
        W2 = jax.random.normal(ks[3], (E, DFF, H), dtype=jnp.float32) * (1.0 / np.sqrt(DFF))
        b2 = jnp.zeros((E, H), dtype=jnp.float32)
        return {'x': x, 'Wr': Wr, 'br': br, 'W1': W1, 'b1': b1, 'W2': W2, 'b2': b2}
    _L0_ffn_all = _L0_ffn_setup()
    _L0_ffn_in = {k: v for k, v in _L0_ffn_all.items() if k in ('Wr', 'br', 'W1', 'b1', 'W2', 'b2')}
    del _L0_ffn_all
    return {'x': x, 'ctx_1024': ctx_1024, 'L0_attn_Wq': _L0_attn_in['Wq'], 'L0_attn_Wk': _L0_attn_in['Wk'], 'L0_attn_Wv': _L0_attn_in['Wv'], 'L0_attn_Wb': _L0_attn_in['Wb'], 'L0_attn_Wa': _L0_attn_in['Wa'], 'L0_attn_Wo': _L0_attn_in['Wo'], 'L0_attn_ln1_w': _L0_attn_in['ln1_w'], 'L0_attn_ln1_b': _L0_attn_in['ln1_b'], 'L0_attn_ln2_w': _L0_attn_in['ln2_w'], 'L0_attn_ln2_b': _L0_attn_in['ln2_b'], 'L0_attn_W1': _L0_attn_in['W1'], 'L0_attn_b1': _L0_attn_in['b1'], 'L0_attn_W2': _L0_attn_in['W2'], 'L0_attn_b2': _L0_attn_in['b2'], 'L0_xattn_Wq': _L0_xattn_in['Wq'], 'L0_xattn_bq': _L0_xattn_in['bq'], 'L0_xattn_Wk': _L0_xattn_in['Wk'], 'L0_xattn_bk': _L0_xattn_in['bk'], 'L0_xattn_Wv': _L0_xattn_in['Wv'], 'L0_xattn_bv': _L0_xattn_in['bv'], 'L0_xattn_Wo': _L0_xattn_in['Wo'], 'L0_xattn_bo': _L0_xattn_in['bo'], 'L0_ffn_Wr': _L0_ffn_in['Wr'], 'L0_ffn_br': _L0_ffn_in['br'], 'L0_ffn_W1': _L0_ffn_in['W1'], 'L0_ffn_b1': _L0_ffn_in['b1'], 'L0_ffn_W2': _L0_ffn_in['W2'], 'L0_ffn_b2': _L0_ffn_in['b2']}

def reference(x, ctx_1024, L0_attn_Wq, L0_attn_Wk, L0_attn_Wv, L0_attn_Wb, L0_attn_Wa, L0_attn_Wo, L0_attn_ln1_w, L0_attn_ln1_b, L0_attn_ln2_w, L0_attn_ln2_b, L0_attn_W1, L0_attn_b1, L0_attn_W2, L0_attn_b2, L0_xattn_Wq, L0_xattn_bq, L0_xattn_Wk, L0_xattn_bk, L0_xattn_Wv, L0_xattn_bv, L0_xattn_Wo, L0_xattn_bo, L0_ffn_Wr, L0_ffn_br, L0_ffn_W1, L0_ffn_b1, L0_ffn_W2, L0_ffn_b2):
    import jax
    import jax.numpy as jnp

    def _L0_attn_ref(x, Wq, Wk, Wv, Wb, Wa, Wo, ln1_w, ln1_b, ln2_w, ln2_b, W1, b1, W2, b2):
        import jax, jax.numpy as jnp
        import numpy as np
        B, T, D, H, K, V, F = (4, 1024, 256, 8, 128, 128, 1024)
        EPS = 1e-05

        def layernorm(x, w, b):
            m = jnp.mean(x, -1, keepdims=True)
            v = jnp.var(x, -1, keepdims=True)
            return (x - m) * jax.lax.rsqrt(v + EPS) * w + b

        def l2norm(x):
            return x * jax.lax.rsqrt(jnp.sum(x * x, -1, keepdims=True) + 1e-06)

        def gdn_recurrence(q, k, v, alpha, beta):
            qT = jnp.moveaxis(q, 1, 0)
            kT = jnp.moveaxis(k, 1, 0)
            vT = jnp.moveaxis(v, 1, 0)
            aT = jnp.moveaxis(alpha, 1, 0)
            bT = jnp.moveaxis(beta, 1, 0)

            def step(S, inp):
                q_t, k_t, v_t, a_t, b_t = inp
                kS = jnp.einsum('bhk,bhkv->bhv', k_t, S)
                bk = (b_t[..., None] * k_t)[..., :, None]
                S = a_t[..., None, None] * (S - bk * kS[..., None, :]) + bk * v_t[..., None, :]
                o = jnp.einsum('bhk,bhkv->bhv', q_t, S)
                return (S, o)
            S0 = jnp.zeros((q.shape[0], H, K, V), q.dtype)
            _, oT = jax.lax.scan(step, S0, (qT, kT, vT, aT, bT))
            return jnp.moveaxis(oT, 0, 1)
        b, t, _ = x.shape
        n = layernorm(x, ln1_w, ln1_b)
        q = l2norm(jax.nn.silu(n @ Wq).reshape(b, t, H, K))
        k = l2norm(jax.nn.silu(n @ Wk).reshape(b, t, H, K))
        v = jax.nn.silu(n @ Wv).reshape(b, t, H, V)
        beta = jax.nn.sigmoid(n @ Wb)
        alpha = jax.nn.sigmoid(n @ Wa)
        o = gdn_recurrence(q, k, v, alpha, beta).reshape(b, t, H * V) @ Wo
        x = x + o
        h = layernorm(x, ln2_w, ln2_b)
        x = x + (jax.nn.gelu(h @ W1 + b1, approximate=False) @ W2 + b2)
        return x

    def _L0_xattn_ref(queries, keys, values, Wq, bq, Wk, bk, Wv, bv, Wo, bo):
        import math
        import jax, jax.numpy as jnp
        import numpy as np
        B, L, D = (8, 1024, 256)
        H = 8
        DK = D // H
        K_FACTOR = 2
        b, l, _ = queries.shape
        q = (queries @ Wq + bq).reshape(b, l, H, DK)
        k = (keys @ Wk + bk).reshape(b, l, H, DK)
        v = (values @ Wv + bv).reshape(b, l, H, DK)
        qT = q.transpose(0, 2, 3, 1)
        kT = k.transpose(0, 2, 3, 1)
        vT = v.transpose(0, 2, 3, 1)
        q_fft = jnp.fft.rfft(qT, axis=-1)
        k_fft = jnp.fft.rfft(kT, axis=-1)
        corr = jnp.fft.irfft(q_fft * jnp.conj(k_fft), n=l, axis=-1)
        top_k = int(K_FACTOR * math.log(l))
        weights, delay = jax.lax.top_k(corr, top_k)
        tmp_corr = jax.nn.softmax(weights, axis=-1)
        tmp_values = jnp.concatenate([vT, vT], axis=-1)
        init_index = jnp.arange(l)
        delay_k = jnp.moveaxis(delay, -1, 0)
        corr_k = jnp.moveaxis(tmp_corr, -1, 0)

        def step(acc, dc):
            d_i, c_i = dc
            idx = init_index[None, None, None, :] + d_i[..., None]
            pattern = jnp.take_along_axis(tmp_values, idx, axis=-1)
            return (acc + pattern * c_i[..., None], None)
        agg, _ = jax.lax.scan(step, jnp.zeros_like(vT), (delay_k, corr_k))
        out = agg.transpose(0, 3, 1, 2).reshape(b, l, H * DK)
        return out @ Wo + bo

    def _L0_ffn_ref(x, Wr, br, W1, b1, W2, b2):
        import jax, jax.numpy as jnp
        import numpy as np
        H, E, DFF = (256, 8, 1024)
        B, S, Hd = x.shape
        n_exp = W1.shape[0]
        xt = x.reshape(-1, Hd)
        logits = xt @ Wr + br
        probs = jax.nn.softmax(logits, axis=-1)
        gate = jnp.max(probs, axis=-1)
        idx = jnp.argmax(probs, axis=-1)
        h1 = jnp.maximum(jnp.einsum('th,ehf->etf', xt, W1) + b1[:, None, :], 0.0)
        ye = jnp.einsum('etf,efh->eth', h1, W2) + b2[:, None, :]
        onehot = jax.nn.one_hot(idx, n_exp, dtype=xt.dtype)
        y = jnp.einsum('te,eth->th', onehot, ye) * gate[:, None]
        return y.reshape(B, S, Hd)
    x = _layernorm(x + _L0_attn_ref(x, L0_attn_Wq, L0_attn_Wk, L0_attn_Wv, L0_attn_Wb, L0_attn_Wa, L0_attn_Wo, L0_attn_ln1_w, L0_attn_ln1_b, L0_attn_ln2_w, L0_attn_ln2_b, L0_attn_W1, L0_attn_b1, L0_attn_W2, L0_attn_b2), axis=-1)
    x = _layernorm(x + _L0_xattn_ref(x, ctx_1024, ctx_1024, L0_xattn_Wq, L0_xattn_bq, L0_xattn_Wk, L0_xattn_bk, L0_xattn_Wv, L0_xattn_bv, L0_xattn_Wo, L0_xattn_bo), axis=-1)
    x = _layernorm(x + _L0_ffn_ref(x, L0_ffn_Wr, L0_ffn_br, L0_ffn_W1, L0_ffn_b1, L0_ffn_W2, L0_ffn_b2), axis=-1)
    return x

_drawn_inputs = setup_inputs


def setup_inputs(seed=0):
    import zlib

    import numpy as np

    out = dict(_drawn_inputs(seed))
    spreads = {'L0_attn_ln1_w': (1.0, 0.6),
     'L0_attn_ln1_b': (0.0, 0.8),
     'L0_attn_ln2_w': (1.0, 0.573),
     'L0_attn_ln2_b': (0.0, 0.511),
     'L0_attn_b1': (0.0, 0.1),
     'L0_attn_b2': (0.0, 0.1),
     'L0_xattn_bq': (0.0, 0.8),
     'L0_xattn_bk': (0.0, 0.8),
     'L0_xattn_bv': (0.0, 0.1),
     'L0_xattn_bo': (0.0, 0.1),
     'L0_ffn_br': (0.0, 0.1),
     'L0_ffn_b1': (0.0, 0.3),
     'L0_ffn_b2': (0.0, 0.1)}
    factors = {'L0_attn_Wq': 8.0,
     'L0_attn_Wk': 8.0,
     'L0_attn_Wv': 6.165,
     'L0_attn_Wb': 8.0,
     'L0_attn_Wa': 8.0,
     'L0_attn_Wo': 5.636}
    for name, (base, spread) in spreads.items():
        noise = np.random.default_rng([zlib.crc32(name.encode()), seed]).standard_normal(out[name].shape)
        drawn = base * np.exp(spread * noise) if base else spread * noise
        out[name] = jnp.asarray(drawn.astype(out[name].dtype))
    for name, factor in factors.items():
        out[name] = (out[name] * factor).astype(out[name].dtype)
    return out
```

```python
from contextlib import ExitStack

import concourse.bass as bass
from concourse import mybir

P = 128
B, T, D = 4, 512, 256
NT = B * T // P
CB = T // P
H, HD = 8, 128
HW = H * HD
GH = 4
NG = H // GH
F = 1024
KD = D // P
FT = F // P
LEVELS = 6
NSC = 5
EPS = 1e-5

F32 = mybir.dt.float32
I32 = mybir.dt.int32
ALU = mybir.AluOpType
ACT = mybir.ActivationFunctionType
AX = mybir.AxisListType.X
ds = bass.ds


def tensors(nc, ctx, prefix):
    def sb(name, shape, dt=F32):
        return ctx.enter_context(nc.sbuf_tensor(prefix + name, shape, dt))

    def ps(name, shape):
        return ctx.enter_context(nc.psum_tensor(prefix + name, shape, F32))

    numbers = []

    def sem(name):
        s = ctx.enter_context(nc.semaphore(prefix + name))
        numbers.append(s.num)
        return s

    def clear():
        runs = []
        for n in sorted(numbers):
            if runs and runs[-1][1] == n:
                runs[-1][1] = n + 1
            else:
                runs.append([n, n + 1])
        with nc.Block() as block:
            @block.sync
            def _(sp):
                for lo, hi in runs:
                    sp.sem_clear(range(lo, hi))

    def start_block():
        ctx.callback(clear)
        return ctx.enter_context(nc.Block())

    return sb, ps, sem, start_block


def wait_apart(eng, sem, value, held):
    if not isinstance(value, int):
        value = eng.to_reg(value)
    eng.wait_ge(*held)
    eng.wait_ge(sem, value)


def project_stage(nc, a, ident, qkv_dram, scal_dram, grow_dram):
    with ExitStack() as ctx:
        sb, ps, sem, start_block = tensors(nc, ctx, "pj_")
        x_all = sb("x_all", [P, NT, D])
        w_qkv = sb("w_qkv", [P, KD, 3 * HW])
        w_gate = sb("w_gate", [P, KD, 2 * H])
        ln_w = sb("ln_w", [P, KD])
        ln_b = sb("ln_b", [P, KD])
        stats = sb("stats", [P, NT, 6])
        meanvar = sb("meanvar", [P, NT, 2])
        rstd = sb("rstd", [P, NT])
        shift = sb("shift", [P, NT])
        z = sb("z", [P, 2, D])
        n_t = sb("n_t", [P, 2, KD, P])
        sig = sb("sig", [P, 6, 512])
        act = sb("act", [P, 2, 3 * HW])
        sq = sb("sq", [P, 2 * HW])
        ss = sb("ss", [P, 2 * H])
        rn = sb("rn", [P, 2, 2 * H])
        half = sb("half", [P, 2 * H])
        gates = sb("gates", [P, NT, 2 * H])
        cumul = sb("cumul", [P, P])
        ones = sb("ones", [P, P])
        keep = sb("keep", [P, NT * H])
        beta = sb("beta", [P, NT * H])
        la = sb("la", [P, NT * H])
        tmp = sb("tmp", [P, NT * H])
        gsum = sb("gsum", [P, NT * H])
        gtot = sb("gtot", [P, NT * H])
        grow = sb("grow", [P, P])
        scal = sb("scal", [P, NT, NSC, H])
        ps_t = [ps(f"t{u}", [P, 512]) for u in range(2)]
        ps_p = [ps(f"p{j}", [P, 512]) for j in range(6)]

        x_loaded, w_loaded, g_loaded = sem("x_loaded"), sem("w_loaded"), sem("g_loaded")
        stats_done, ln_done = sem("stats_done"), sem("ln_done")
        z_ready, zt_done, nt_ready = sem("z_ready"), sem("zt_done"), sem("nt_ready")
        chunk_done, gate_done, gate_read = sem("chunk_done"), sem("gate_done"), sem("gate_read")
        sig_ready, act_ready = sem("sig_ready"), sem("act_ready")
        sq_ready, ss_ready, rn_ready, unit_ready = sem("sq_ready"), sem("ss_ready"), sem("rn_ready"), sem("unit_ready")
        stored = [sem(f"stored{u}") for u in range(2)]
        pow_ready, half_ready = sem("pow_ready"), sem("half_ready")
        const_ready, chain, la_ready = sem("const_ready"), sem("chain"), sem("la_ready")
        beta_ready, ex_ready, ln1p_ready = sem("beta_ready"), sem("ex_ready"), sem("ln1p_ready")
        sums_done, gsum_ready, grow_done, grow_ready = sem("sums_done"), sem("gsum_ready"), sem("grow_done"), sem("grow_ready")
        ediff_ready, eg_ready, scal_ready, out_stored = sem("ediff_ready"), sem("eg_ready"), sem("scal_ready"), sem("out_stored")
        block = start_block()

        @block.sync
        def _(sp):
            sp.dma_start(x_all[:], a["x"].rearrange("(n p) d -> p n d", p=P)).then_inc(x_loaded, 16)
            sp.dma_start(ln_w[:], a["ln1_w"].rearrange("(k p) -> p k", p=P),
                         allow_slow_non_contiguous=True).then_inc(w_loaded, 16)
            sp.dma_start(ln_b[:], a["ln1_b"].rearrange("(k p) -> p k", p=P),
                         allow_slow_non_contiguous=True).then_inc(w_loaded, 16)
            for j, w in enumerate(("Wq", "Wk", "Wv")):
                sp.dma_start(w_qkv[:, :, j * HW:(j + 1) * HW],
                             a[w].rearrange("(k p) m -> p k m", p=P)).then_inc(w_loaded, 16)
            sp.dma_start(w_gate[:, :, 0:H], a["Wb"].rearrange("(k p) m -> p k m", p=P)).then_inc(w_loaded, 16)
            sp.dma_start(w_gate[:, :, H:2 * H], a["Wa"].rearrange("(k p) m -> p k m", p=P)).then_inc(w_loaded, 16)
            sp.dma_start(cumul[:], a["mask_incl"]).then_inc(g_loaded, 16)
            sp.dma_start(keep[:], a["keep"]).then_inc(g_loaded, 16)
            with sp.Fori(0, NT // 2) as it:
                for u in range(2):
                    row = sp.snap(it * 2 * P + u * P)
                    sp.wait_ge(unit_ready, 2 * it + u + 1)
                    sp.dma_start(qkv_dram[ds(row, P), :], act[:, u, :]).then_inc(stored[u], 16)
            sp.wait_ge(grow_ready, 1)
            sp.dma_start(grow_dram, grow[:]).then_inc(out_stored, 16)
            sp.wait_ge(scal_ready, 1)
            sp.dma_start(scal_dram.rearrange("n p c -> p n c"), scal[:].rearrange("p n c h -> p n (c h)")).then_inc(out_stored, 16)
            for u in range(2):
                sp.wait_ge(stored[u], 16 * (NT // 2))
            sp.wait_ge(out_stored, 32)

        @block.vector
        def _(dve):
            dve.wait_ge(x_loaded, 16)
            for n in range(NT):
                nc.vector.bn_stats(stats[:, n, :], x_all[:, n, :]).then_inc(stats_done, 1)
            for n in range(NT):
                dve.wait_ge(stats_done, n + 1)
                nc.vector.bn_aggr(meanvar[:, n, :], stats[:, n, :]).then_inc(stats_done, 1)
            dve.wait_ge(stats_done, 2 * NT)
            dve.wait_ge(ln_done, 1)
            nc.vector.scalar_tensor_tensor(shift[:], meanvar[:, :, 0], -1.0, rstd[:], ALU.mult, ALU.mult).then_inc(ln_done, 1)
            nc.vector.memset(ones[:], 1.0).then_inc(const_ready, 1)
            dve.wait_ge(ln_done, 2)
            for u in range(2):
                nc.vector.tensor_scalar(z[:, u, :], x_all[:, u, :], rstd[:, u:u + 1], shift[:, u:u + 1],
                                        ALU.mult, ALU.add).then_inc(z_ready, 1)

            def tile(it, u, more):
                n = 2 * it + u
                for j in range(6):
                    dve.wait_ge(sig_ready, 6 * n + j + 1)
                    if j == 0 and not (isinstance(it, int) and it == 0):
                        dve.wait_ge(stored[u], 16 * it)
                    nc.vector.tensor_tensor(act[:, u, j * 512:(j + 1) * 512], ps_p[j][:], sig[:, j, :],
                                            ALU.mult).then_inc(act_ready, 1)
                dve.wait_ge(gate_done, n + 1)
                nc.vector.tensor_scalar(gates[:, ds(n, 1), :].rearrange("p a c -> p (a c)"), ps_t[u][:, 256:256 + 2 * H],
                                        1.0, None, ALU.mult).then_inc(gate_read, 1)
                dve.wait_ge(sq_ready, n + 1)
                nc.vector.tensor_reduce(ss[:], sq[:].rearrange("p (h d) -> p h d", d=HD), AX, ALU.add).then_inc(ss_ready, 1)
                dve.wait_ge(ss_ready, n + 1)
                nc.vector.tensor_scalar(rn[:, u, :], ss[:], 1e-6, None, ALU.add).then_inc(rn_ready, 1)
                if more:
                    dve.wait_ge(zt_done, n + 1)
                    nc.vector.tensor_scalar(z[:, u, :], x_all[:, ds(n + 2, 1), :].rearrange("p a d -> p (a d)"),
                                            rstd[:, ds(n + 2, 1)], shift[:, ds(n + 2, 1)],
                                            ALU.mult, ALU.add).then_inc(z_ready, 1)

            for u in range(2):
                tile(0, u, True)
            with dve.Fori(1, NT // 2 - 1) as it:
                for u in range(2):
                    tile(it, u, True)
            for u in range(2):
                tile(NT // 2 - 1, u, False)

            dve.wait_ge(gate_read, NT)
            nc.vector.scalar_tensor_tensor(tmp[:].rearrange("p (n h) -> p n h", h=H), gates[:, :, H:2 * H], -1.0,
                                           gates[:, :, H:2 * H], ALU.mult, ALU.max).then_inc(chain, 1)
            nc.vector.tensor_scalar(la[:].rearrange("p (n h) -> p n h", h=H), gates[:, :, H:2 * H], 0.0, None,
                                    ALU.min).then_inc(la_ready, 1)
            dve.wait_ge(ln1p_ready, 1)
            dve.wait_ge(la_ready, 1)
            nc.vector.tensor_tensor(la[:], la[:], tmp[:], ALU.subtract).then_inc(la_ready, 1)
            dve.wait_ge(sums_done, 1)
            nc.vector.tensor_copy(gsum[:], ps_p[0][:, 0:P]).then_inc(gsum_ready, 1)
            nc.vector.tensor_copy(gtot[:], ps_p[1][:, 0:P]).then_inc(gsum_ready, 1)
            dve.wait_ge(gsum_ready, 2)
            nc.vector.tensor_tensor(tmp[:], gtot[:], gsum[:], ALU.subtract).then_inc(ediff_ready, 1)
            dve.wait_ge(grow_done, 1)
            nc.vector.tensor_copy(grow[:], ps_p[2][:, 0:P]).then_inc(grow_ready, 1)

            def col(c):
                return scal[:, :, c, :]

            def nh(t):
                return t[:].rearrange("p (n h) -> p n h", h=H)

            dve.wait_ge(beta_ready, 1)
            dve.wait_ge(g_loaded, 32)
            nc.vector.tensor_scalar(col(0), nh(beta), 1.0, None, ALU.mult).then_inc(chain, 1)
            nc.vector.tensor_scalar(col(1), nh(beta), -1.0, None, ALU.mult).then_inc(chain, 1)
            nc.vector.tensor_scalar(col(2), nh(gsum), 1.0, None, ALU.mult).then_inc(chain, 1)
            dve.wait_ge(eg_ready, 2)
            nc.vector.tensor_tensor(col(3), nh(gtot), nh(keep), ALU.mult).then_inc(chain, 1)
            nc.vector.tensor_tensor(col(4), nh(tmp), nh(keep), ALU.mult).then_inc(chain, 1)
            dve.wait_ge(chain, 6)
            nc.vector.nop().then_inc(scal_ready, 1)

        @block.gpsimd
        def _(pool):
            nc.gpsimd.memset(half[:], -0.5).then_inc(half_ready, 1)
            pool.wait_ge(half_ready, 1)
            pool.wait_ge(stats_done, 2 * NT)
            nc.gpsimd.tensor_scalar(rstd[:], meanvar[:, :, 1], EPS, None, ALU.add).then_inc(half_ready, 1)
            pool.wait_ge(half_ready, 2)
            nc.gpsimd.tensor_tensor(rstd[:], rstd[:], half[:, 0:NT], ALU.pow).then_inc(ln_done, 1)
            with pool.Fori(0, NT // 2) as it:
                for u in range(2):
                    n = 2 * it + u
                    qk = act[:, u, 0:2 * HW]
                    pool.wait_ge(act_ready, 6 * n + 4)
                    nc.gpsimd.tensor_tensor(sq[:], qk, qk, ALU.mult).then_inc(sq_ready, 1)
                    pool.wait_ge(rn_ready, n + 1)
                    nc.gpsimd.tensor_tensor(rn[:, u, :], rn[:, u, :], half[:], ALU.pow).then_inc(pow_ready, 1)
                    pool.wait_ge(pow_ready, n + 1)
                    nc.gpsimd.tensor_tensor(qk.rearrange("p (h d) -> p h d", d=HD),
                                            qk.rearrange("p (h d) -> p h d", d=HD),
                                            rn[:, u, :].unsqueeze(2).broadcast_to([P, 2 * H, HD]),
                                            ALU.mult).then_inc(unit_ready, 1)

        @block.scalar
        def _(act_e):
            act_e.wait_ge(w_loaded, 16 * 7)
            with act_e.Fori(0, NT // 2) as it:
                for u in range(2):
                    n = 2 * it + u
                    act_e.wait_ge(zt_done, n + 1)
                    for k in range(KD):
                        nc.scalar.activation(n_t[:, u, k, :], ps_t[u][:, k * P:(k + 1) * P], ACT.Identity,
                                             bias=ln_b[:, k:k + 1], scale=ln_w[:, k:k + 1]).then_inc(nt_ready, 1)
                    for j in range(6):
                        act_e.wait_ge(chunk_done, 6 * n + j + 1)
                        nc.scalar.activation(sig[:, j, :], ps_p[j][:], ACT.Sigmoid).then_inc(sig_ready, 1)
            act_e.wait_ge(gate_read, NT)
            nc.scalar.activation(beta[:].rearrange("p (n h) -> p n h", h=H), gates[:, :, 0:H],
                                 ACT.Sigmoid).then_inc(beta_ready, 1)
            act_e.wait_ge(chain, 1)
            nc.scalar.activation(tmp[:], tmp[:], ACT.Exp, scale=-1.0).then_inc(ex_ready, 1)
            act_e.wait_ge(ex_ready, 1)
            nc.scalar.activation(tmp[:], tmp[:], ACT.Ln, bias=1.0).then_inc(ln1p_ready, 1)
            act_e.wait_ge(ediff_ready, 1)
            nc.scalar.activation(gtot[:], gtot[:], ACT.Exp).then_inc(eg_ready, 1)
            nc.scalar.activation(tmp[:], tmp[:], ACT.Exp).then_inc(eg_ready, 1)

        @block.tensor
        def _(pe):
            pe.wait_ge(w_loaded, 16 * 7)

            def transposes(n, u):
                pe.wait_ge(z_ready, n + 1)
                for k in range(KD):
                    last = nc.tensor.transpose(ps_t[u][:, k * P:(k + 1) * P], z[:, u, k * P:(k + 1) * P], ident[:])
                last.then_inc(zt_done, 1)

            def products(it, u, first):
                n = 2 * it + u
                for j in range(6):
                    if j == 0:
                        pe.wait_ge(nt_ready, 2 * n + 2)
                    if not first:
                        pe.wait_ge(act_ready, 6 * n - 6 + j + 1)
                    for k in range(KD):
                        last = nc.tensor.matmul(ps_p[j][:], n_t[:, u, k, :], w_qkv[:, k, j * 512:(j + 1) * 512],
                                                start=(k == 0), stop=(k == KD - 1))
                    last.then_inc(chunk_done, 1)
                for k in range(KD):
                    last = nc.tensor.matmul(ps_t[u][:, 256:256 + 2 * H], n_t[:, u, k, :], w_gate[:, k, :],
                                            start=(k == 0), stop=(k == KD - 1))
                last.then_inc(gate_done, 1)

            def tile(it, u, first=False, last=False):
                n = 2 * it + u
                products(it, u, first)
                if not last:
                    if not first:
                        pe.wait_ge(gate_read, n)
                    transposes(n + 1, 1 - u)

            transposes(0, 0)
            tile(0, 0, first=True)
            tile(0, 1)
            with pe.Fori(1, NT // 2 - 1) as it:
                for u in range(2):
                    tile(it, u)
            tile(NT // 2 - 1, 0)
            tile(NT // 2 - 1, 1, last=True)
            pe.wait_ge(la_ready, 2)
            pe.wait_ge(g_loaded, 32)
            pe.wait_ge(const_ready, 1)
            nc.tensor.matmul(ps_p[0][:, 0:P], cumul[:], la[:], start=True, stop=True)
            nc.tensor.matmul(ps_p[1][:, 0:P], ones[:], la[:], start=True, stop=True).then_inc(sums_done, 1)
            pe.wait_ge(gsum_ready, 2)
            nc.tensor.transpose(ps_p[2][:, 0:P], gsum[:], ident[:]).then_inc(grow_done, 1)


def delta_stage(nc, a, ident, qkv_dram, scal_dram, grow_dram, o_dram):
    with ExitStack() as ctx:
        sb, ps, sem, start_block = tensors(nc, ctx, "dl_")
        qkv = [sb(f"qkv{u}", [P, 3, H, HD]) for u in range(2)]
        gb = [sb(f"gb{u}", [P, H, P]) for u in range(2)]
        sc = [sb(f"sc{u}", [P, NSC, H]) for u in range(2)]
        BETA, NBETA, GSUM, GEND, WDECAY = range(NSC)
        masks = sb("masks", [P, LEVELS, P])
        mask_incl = sb("mask_incl", [P, P])
        mask_strict = sb("mask_strict", [P, P])
        mask_one = sb("mask_one", [P, P])
        zero = sb("zero", [P, 2])

        def pair(name, slots=2):
            return [[sb(f"{name}{u}{g}", [P, GH, P]) for g in range(NG)] for u in range(slots)]

        k_t, q_t, kg_t, qg_t = pair("k_t"), pair("q_t", 1) * 2, pair("kg_t"), pair("qg_t")
        n_mat_t, attn_t, tinv, tinv_t = pair("n_mat_t"), pair("attn_t"), pair("tinv"), pair("tinv_t")
        k_t = pair("k_tt", 1) * 2
        eg, edec, eb = pair("eg", 1)[0], pair("edec", 1)[0], pair("eb", 1)[0]
        ymat, rhs, w, w2, sdec, state = (pair(s, 1)[0] for s in ("ymat", "rhs", "w", "w2", "sdec", "state"))
        o_sb = pair("o_sb", 1)[0]
        bank = [ps(f"m{i}", [P, GH, P]) for i in range(4)]
        xb = [ps(f"x{g}", [P, GH, P]) for g in range(NG)]
        tb = [ps(f"t{g}", [P, GH, P]) for g in range(NG)]

        loaded = [sem(f"loaded{u}") for u in range(2)]
        const_loaded, state_zero = sem("const_loaded"), sem("state_zero")
        kt_done, qt_done, kk_done, kq_done, tinv2_done = (sem(s) for s in ("kt_done", "qt_done", "kk_done", "kq_done", "tinv2_done"))
        x_done, t_done, tt_done = sem("x_done"), sem("t_done"), sem("tt_done")
        ks_done, y_done, o_done, kw_done = sem("ks_done"), sem("y_done"), sem("o_done"), sem("kw_done")
        eg_ready, edec_ready, kt_copied, qt_copied, tinv2_copied = (
            sem(s) for s in ("eg_ready", "edec_ready", "kt_copied", "qt_copied", "tinv2_copied"))
        t_copied, tt_copied, o_copied = sem("t_copied"), sem("tt_copied"), sem("o_copied")
        kg_ready, qg_ready, diff_ready, a_ready, attn_ready, tinv2t_ready = (
            sem(s) for s in ("kg_ready", "qg_ready", "diff_ready", "a_ready", "attn_ready", "tinv2t_ready"))
        ymat_ready, r_ready, w_ready, s_ready = sem("ymat_ready"), sem("r_ready"), sem("w_ready"), sem("s_ready")
        nbm_ready, eb_ready, n_ready, incl_ready = sem("nbm_ready"), sem("eb_ready"), sem("n_ready"), sem("incl_ready")
        w2_ready, sdec_ready, o_stored = sem("w2_ready"), sem("sdec_ready"), sem("o_stored")
        block = start_block()

        def per_head(t, c, g):
            return t[:, c, g * GH:(g + 1) * GH].unsqueeze(2).broadcast_to([P, GH, P])

        def per_group(m):
            return m.unsqueeze(1).broadcast_to([P, GH, P])

        def schedule(eng, prep, invert, update):
            def step(n, u, first, last):
                invert(n, u, lambda part: None if first else update(n - 1, 1 - u, part),
                       lambda part: None if last else prep(n + 1, 1 - u, part))

            for part in range(3):
                prep(0, 0, part)
            step(0, 0, True, False)
            step(1, 1, False, False)
            with eng.Fori(1, NT // 2 - 1) as j:
                step(2 * j, 0, False, False)
                step(2 * j + 1, 1, False, False)
            step(NT - 2, 0, False, False)
            step(NT - 1, 1, False, True)
            for part in range(3):
                update(NT - 1, 1, part)

        def static(n):
            return isinstance(n, int)

        @block.sync
        def _(sp):
            sp.dma_start(masks[:], a["mask_levels"]).then_inc(const_loaded, 16)
            sp.dma_start(mask_incl[:], a["mask_incl"]).then_inc(const_loaded, 16)
            sp.dma_start(mask_strict[:], a["mask_strict"]).then_inc(const_loaded, 16)
            sp.dma_start(mask_one[:], a["mask_one"]).then_inc(const_loaded, 16)

            def load(n, u, reuse):
                row = sp.snap(n * P) if reuse and not static(n) else n * P
                if reuse:
                    sp.wait_ge(r_ready, 2 * n - 2)
                    sp.wait_ge(kw_done, 2 * n - 2)
                sp.dma_start(qkv[u][:], qkv_dram[ds(row, P), :].rearrange("p (c h d) -> p c h d", c=3, h=H)).then_inc(loaded[u], 16)
                sp.dma_start(gb[u][:], grow_dram[ds(n * H, H), :].partition_broadcast(P)).then_inc(loaded[u], 16)
                sp.dma_start(sc[u][:], scal_dram[ds(n, 1), :, :].rearrange("n p (c h) -> (n p) c h", c=NSC)).then_inc(loaded[u], 16)

            def store(n):
                row = n * P if static(n) else sp.snap(n * P)
                for g in range(NG):
                    sp.wait_ge(o_copied, 2 * n + g + 1)
                    sp.dma_start(o_dram[ds(row, P), g * GH * HD:(g + 1) * GH * HD].rearrange("p (h d) -> p h d", h=GH),
                                 o_sb[g][:]).then_inc(o_stored, 16)

            load(0, 0, False)
            load(1, 1, False)
            store(0)
            load(2, 0, True)
            with sp.Fori(1, NT // 2 - 1) as j:
                store(2 * j - 1)
                load(2 * j + 1, 1, True)
                store(2 * j)
                load(2 * j + 2, 0, True)
            store(NT - 3)
            load(NT - 1, 1, True)
            store(NT - 2)
            store(NT - 1)
            sp.wait_ge(o_stored, 32 * NT)

        @block.tensor
        def _(pe):
            def four(out, lhs, rhs_, **flags):
                for h in range(GH):
                    last = nc.tensor.matmul(out[:, h, :], lhs(h), rhs_(h), start=flags.get("start", True),
                                            stop=flags.get("stop", True), skip_group_check=True)
                return last

            def four_transposed(out, src):
                for h in range(GH):
                    last = nc.tensor.transpose(out[:, h, :], src[:, h, :], ident[:])
                return last

            def prep(n, u, part):
                if part == 0:
                    pe.wait_ge(loaded[u], 48 * (n // 2 + 1) if static(n) else 24 * n + (48 if u == 0 else 24))
                    for g in range(NG):
                        k_bank, q_bank = bank[2 * g], bank[2 * g + 1]
                        if not (static(n) and n < 2):
                            if g == 0:
                                pe.wait_ge(o_copied, 2 * n - 2)
                            else:
                                pe.wait_ge(s_ready, 2 * n - 2)
                        elif n == 1:
                            pe.wait_ge(attn_ready, g + 1)
                        four_transposed(k_bank, qkv[u][:, 1, g * GH:(g + 1) * GH, :]).then_inc(kt_done, 1)
                        four_transposed(q_bank, qkv[u][:, 0, g * GH:(g + 1) * GH, :]).then_inc(qt_done, 1)
                elif part == 1:
                    for g in range(NG):
                        kk, kq = bank[2 * g], bank[2 * g + 1]
                        pe.wait_ge(kt_copied, 2 * n + g + 1)
                        four(kk, lambda h: k_t[u][g][:, h, :], lambda h: k_t[u][g][:, h, :]).then_inc(kk_done, 1)
                        pe.wait_ge(qt_copied, 2 * n + g + 1)
                        four(kq, lambda h: k_t[u][g][:, h, :], lambda h: q_t[u][g][:, h, :]).then_inc(kq_done, 1)
                else:
                    for g in range(NG):
                        pe.wait_ge(tinv2t_ready, 2 * n + g + 1)
                        four_transposed(bank[2 * g], tinv_t[u][g]).then_inc(tinv2_done, 1)

            def invert(n, u, update_, prep_):
                for lev in range(LEVELS):
                    for g in range(NG):
                        if lev == 0:
                            pe.wait_ge(tinv2_copied, 2 * n + g + 1)
                            pe.wait_ge(n_ready, 2 * n + g + 1)
                            if not (static(n) and n == 0):
                                pe.wait_ge(tt_copied, 12 * n - 1 + g)
                        else:
                            pe.wait_ge(t_copied, 10 * n + 2 * (lev - 1) + g + 1)
                            pe.wait_ge(tt_copied, 12 * n + 2 * (lev - 1) + g + 1)
                        four(xb[g], lambda h: n_mat_t[u][g][:, h, :], lambda h: tinv[u][g][:, h, :]).then_inc(x_done, 1)
                    if lev < 3:
                        update_(lev)
                    else:
                        prep_(lev - 3)
                    for g in range(NG):
                        pe.wait_ge(ymat_ready, 12 * n + 2 * lev + g + 1)
                        if lev < LEVELS - 1:
                            four(tb[g], lambda h: tinv_t[u][g][:, h, :], lambda h: ymat[g][:, h, :]).then_inc(t_done, 1)
                        four(xb[g], lambda h: ymat[g][:, h, :], lambda h: tinv_t[u][g][:, h, :]).then_inc(tt_done, 1)

            def update(n, u, part):
                for g in range(NG):
                    if part == 0:
                        if not (static(n) and n == NT - 1):
                            if g == 0:
                                pe.wait_ge(tinv2_copied, 2 * n + 3)
                            else:
                                pe.wait_ge(attn_ready, 2 * n + 3)
                        if static(n) and n == 0:
                            pe.wait_ge(state_zero, 2)
                        else:
                            pe.wait_ge(s_ready, 2 * n - 1 + g)
                        pe.wait_ge(kg_ready, 2 * n + g + 1)
                        four(bank[g], lambda h: kg_t[u][g][:, h, :], lambda h: state[g][:, h, :]).then_inc(ks_done, 1)
                    elif part == 1:
                        pe.wait_ge(r_ready, 2 * n + g + 1)
                        pe.wait_ge(tt_copied, 12 * n + 11 + g)
                        if not (static(n) and n == NT - 1):
                            if g == 0:
                                pe.wait_ge(tinv2_copied, 2 * n + 4)
                            else:
                                pe.wait_ge(attn_ready, 2 * n + 4)
                        four(bank[2 + g], lambda h: tinv_t[u][g][:, h, :], lambda h: rhs[g][:, h, :]).then_inc(y_done, 1)
                    else:
                        pe.wait_ge(w_ready, 2 * n + g + 1)
                        pe.wait_ge(incl_ready, 2 * n + g + 1)
                        pe.wait_ge(qg_ready, 2 * n + g + 1)
                        for h in range(GH):
                            nc.tensor.matmul(bank[g][:, h, :], qg_t[u][g][:, h, :], state[g][:, h, :],
                                             start=True, stop=False, skip_group_check=True)
                            last = nc.tensor.matmul(bank[g][:, h, :], attn_t[u][g][:, h, :], w[g][:, h, :],
                                                    start=False, stop=True, skip_group_check=True)
                        last.then_inc(o_done, 1)
                if part == 2:
                    for g in range(NG):
                        pe.wait_ge(w2_ready, 2 * n + g + 1)
                        four(bank[2 + g], lambda h: qkv[u][:, 1, g * GH + h, :],
                             lambda h: w2[g][:, h, :]).then_inc(kw_done, 1)

            pe.wait_ge(const_loaded, 64)
            schedule(pe, prep, invert, update)

        @block.scalar
        def _(act):
            def prep(n, u, part):
                if part == 0:
                    act.wait_ge(loaded[u], 48 * (n // 2 + 1) if static(n) else 24 * n + (48 if u == 0 else 24))
                    for g in range(NG):
                        heads = slice(g * GH, (g + 1) * GH)
                        if not (static(n) and n == 0):
                            act.wait_ge(qg_ready, 2 * n - 1 + g)
                        nc.scalar.activation(eg[g][:], gb[u][:, heads, :], ACT.Exp).then_inc(eg_ready, 1)
                    for g in range(NG):
                        act.wait_ge(kt_done, 2 * n + g + 1)
                        nc.scalar.activation(k_t[u][g][:], bank[2 * g][:], ACT.Copy).then_inc(kt_copied, 1)
                        act.wait_ge(qt_done, 2 * n + g + 1)
                        nc.scalar.activation(q_t[u][g][:], bank[2 * g + 1][:], ACT.Copy).then_inc(qt_copied, 1)
                        act.wait_ge(diff_ready, 8 * n + 4 * g + 4)
                        nc.scalar.activation(edec[g][:], edec[g][:], ACT.Exp).then_inc(edec_ready, 1)
                elif part == 2:
                    for g in range(NG):
                        act.wait_ge(tinv2_done, 2 * n + g + 1)
                        nc.scalar.activation(tinv[u][g][:], bank[2 * g][:], ACT.Copy).then_inc(tinv2_copied, 1)

            def invert(n, u, update_, prep_):
                for lev in range(LEVELS):
                    if lev < 3:
                        update_(lev)
                    else:
                        prep_(lev - 3)
                    for g in range(NG):
                        if lev < LEVELS - 1:
                            act.wait_ge(t_done, 10 * n + 2 * lev + g + 1)
                            nc.scalar.activation(tinv[u][g][:], tb[g][:], ACT.Copy).then_inc(t_copied, 1)
                        act.wait_ge(tt_done, 12 * n + 2 * lev + g + 1)
                        nc.scalar.activation(tinv_t[u][g][:], xb[g][:], ACT.Copy).then_inc(tt_copied, 1)

            def update(n, u, part):
                if part != 2:
                    return
                for g in range(NG):
                    if not (static(n) and n == 0):
                        act.wait_ge(o_stored, 32 * n)
                    act.wait_ge(o_done, 2 * n + g + 1)
                    nc.scalar.activation(o_sb[g][:], bank[g][:], ACT.Copy).then_inc(o_copied, 1)

            schedule(act, prep, invert, update)

        @block.vector
        def _(dve):
            for g in range(NG):
                nc.vector.memset(state[g][:], 0.0).then_inc(state_zero, 1)

            def prep(n, u, part):
                if part == 0:
                    dve.wait_ge(loaded[u], 48 * (n // 2 + 1) if static(n) else 24 * n + (48 if u == 0 else 24))
                    for g in range(NG):
                        if not (static(n) and n == 0):
                            dve.wait_ge(eb_ready, 2 * n - 1 + g)
                            dve.wait_ge(attn_ready, 2 * n - 1 + g)
                        for h in range(GH):
                            hh = g * GH + h
                            nc.vector.tensor_scalar(edec[g][:, h, :], gb[u][:, hh, :], sc[u][:, GSUM, hh:hh + 1], 0.0,
                                                    ALU.subtract, ALU.min).then_inc(diff_ready, 1)
                    for g in range(NG):
                        dve.wait_ge(eg_ready, 2 * n + g + 1)
                        dve.wait_ge(kt_copied, 2 * n + g + 1)
                        nc.vector.tensor_tensor(kg_t[u][g][:], k_t[u][g][:], eg[g][:], ALU.mult).then_inc(kg_ready, 1)
                        dve.wait_ge(qt_copied, 2 * n + g + 1)
                        nc.vector.tensor_tensor(qg_t[u][g][:], q_t[u][g][:], eg[g][:], ALU.mult).then_inc(qg_ready, 1)
                elif part == 1:
                    for g in range(NG):
                        dve.wait_ge(kk_done, 2 * n + g + 1)
                        dve.wait_ge(eb_ready, 2 * n + g + 1)
                        nc.vector.tensor_tensor(n_mat_t[u][g][:], bank[2 * g][:], eb[g][:], ALU.mult).then_inc(a_ready, 1)
                        dve.wait_ge(kq_done, 2 * n + g + 1)
                        nc.vector.tensor_tensor(attn_t[u][g][:], bank[2 * g + 1][:], edec[g][:], ALU.mult).then_inc(attn_ready, 1)
                    for g in range(NG):
                        dve.wait_ge(n_ready, 2 * n + g + 1)
                        nc.vector.tensor_tensor(tinv_t[u][g][:], n_mat_t[u][g][:], per_group(mask_one[:]),
                                                ALU.mult).then_inc(tinv2t_ready, 1)

            def invert(n, u, update_, prep_):
                for lev in range(LEVELS):
                    for g in range(NG):
                        dve.wait_ge(x_done, 12 * n + 2 * lev + g + 1)
                        nc.vector.tensor_tensor(ymat[g][:], xb[g][:], per_group(masks[:, lev, :]),
                                                ALU.mult).then_inc(ymat_ready, 1)
                    if lev < 3:
                        update_(lev)
                    else:
                        prep_(lev - 3)

            def update(n, u, part):
                for g in range(NG):
                    if part == 0:
                        dve.wait_ge(ks_done, 2 * n + g + 1)
                        nc.vector.tensor_tensor(rhs[g][:], qkv[u][:, 2, g * GH:(g + 1) * GH, :], bank[g][:],
                                                ALU.subtract).then_inc(r_ready, 1)
                    elif part == 1:
                        dve.wait_ge(y_done, 2 * n + g + 1)
                        nc.vector.tensor_tensor(w[g][:], bank[2 + g][:], per_head(sc[u], BETA, g), ALU.mult).then_inc(w_ready, 1)
                    else:
                        dve.wait_ge(kw_done, 2 * n + g + 1)
                        dve.wait_ge(sdec_ready, 2 * n + g + 1)
                        nc.vector.tensor_tensor(state[g][:], sdec[g][:], bank[2 + g][:], ALU.add).then_inc(s_ready, 1)

            dve.wait_ge(const_loaded, 64)
            schedule(dve, prep, invert, update)

        @block.gpsimd
        def _(pool):
            pool.wait_ge(const_loaded, 64)

            def prep(n, u, part):
                if part == 0:
                    for g in range(NG):
                        pool.wait_ge(loaded[u], 48 * (n // 2 + 1) if static(n) else 24 * n + (48 if u == 0 else 24))
                        if not (static(n) and n == 0):
                            pool.wait_ge(a_ready, 2 * n - 1 + g)
                        nc.gpsimd.tensor_tensor(eb[g][:], per_group(mask_strict[:]), per_head(sc[u], NBETA, g),
                                                ALU.mult).then_inc(nbm_ready, 1)
                elif part == 1:
                    for g in range(NG):
                        pool.wait_ge(edec_ready, 2 * n + g + 1)
                        pool.wait_ge(nbm_ready, 2 * n + g + 1)
                        nc.gpsimd.tensor_tensor(eb[g][:], eb[g][:], edec[g][:], ALU.mult).then_inc(eb_ready, 1)
                    for g in range(NG):
                        pool.wait_ge(a_ready, 2 * n + g + 1)
                        nc.gpsimd.tensor_tensor(n_mat_t[u][g][:], n_mat_t[u][g][:], per_group(ident[:]),
                                                ALU.add).then_inc(n_ready, 1)
                else:
                    for g in range(NG):
                        pool.wait_ge(attn_ready, 2 * n + g + 1)
                        nc.gpsimd.tensor_tensor(attn_t[u][g][:], attn_t[u][g][:], per_group(mask_incl[:]),
                                                ALU.mult).then_inc(incl_ready, 1)

            def invert(n, u, update_, prep_):
                for part in range(3):
                    update_(part)
                for part in range(3):
                    prep_(part)

            def update(n, u, part):
                for g in range(NG):
                    if part == 0:
                        if static(n) and n == 0:
                            pool.wait_ge(state_zero, 2)
                        else:
                            pool.wait_ge(s_ready, 2 * n - 1 + g)
                        nc.gpsimd.tensor_tensor(sdec[g][:], state[g][:], per_head(sc[u], GEND, g), ALU.mult).then_inc(sdec_ready, 1)
                    elif part == 1:
                        pool.wait_ge(w_ready, 2 * n + g + 1)
                        nc.gpsimd.tensor_tensor(w2[g][:], w[g][:], per_head(sc[u], WDECAY, g), ALU.mult).then_inc(w2_ready, 1)

            schedule(pool, prep, invert, update)


def ffn_stage(nc, a, ident, o_dram, x1_all):
    with ExitStack() as ctx:
        sb, ps, sem, start_block = tensors(nc, ctx, "ff_")
        x_all = sb("x_all", [P, NT, D])
        xb_all = sb("xb_all", [P, NT, D])
        wo = sb("wo", [P, H, D])
        w1 = sb("w1", [P, KD, F])
        w2 = sb("w2", [P, FT, D])
        b1 = sb("b1", [P, FT])
        b2 = sb("b2", [P, D])
        ln_w, ln_b = sb("ln_w", [P, KD]), sb("ln_b", [P, KD])
        half = sb("half", [P, 1])
        o_in = [sb(f"o_in{u}", [P, H, HD]) for u in range(2)]
        o_t = sb("o_t", [P, H, P])
        x1 = sb("x1", [P, D])
        z = sb("z", [P, D])
        h_t = sb("h_t", [P, KD, P])
        g_t = sb("g_t", [P, FT, P])
        base = [sb(f"base{u}", [P, D]) for u in range(2)]
        total = sb("total", [P, D])
        stats = [sb(f"stats{c}", [P, 6]) for c in range(2)]
        mv = [sb(f"mv{c}", [P, 2]) for c in range(2)]
        var = [sb(f"var{c}", [P, 1]) for c in range(2)]
        rstd = [sb(f"rstd{c}", [P, 1]) for c in range(2)]
        shift = [sb(f"shift{c}", [P, 1]) for c in range(2)]
        ps_ot = [ps(f"ot{i}", [P, 4, P]) for i in range(2)]
        ps_at = ps("at", [P, D])
        ps_z = ps("z_ps", [P, KD, P])
        ps_f1 = [ps(f"f1{i}", [P, 4, P]) for i in range(2)]
        ps_f2 = ps("f2", [P, D])

        w_loaded, half_ready, xb_ready = sem("w_loaded"), sem("half_ready"), sem("xb_ready")
        o_loaded = [sem(f"o_loaded{u}") for u in range(2)]
        ot_done, ot_copied, attn_done, x1_ready = sem("ot_done"), sem("ot_copied"), sem("attn_done"), sem("x1_ready")
        z_ready, zt_done, ht_ready = sem("z_ready"), sem("zt_done"), sem("ht_ready")
        f1_done, gelu_ready, f2_done, total_ready = sem("f1_done"), sem("gelu_ready"), sem("f2_done"), sem("total_ready")
        base_ready, out_ready = sem("base_ready"), sem("out_ready")
        stats_ready = [sem(f"stats_ready{c}") for c in range(2)]
        mv_ready = [sem(f"mv_ready{c}") for c in range(2)]
        var_ready = [sem(f"var_ready{c}") for c in range(2)]
        rstd_ready = [sem(f"rstd_ready{c}") for c in range(2)]
        shift_ready = [sem(f"shift_ready{c}") for c in range(2)]
        block = start_block()
        LOADS = 8

        def schedule(eng, prologue, step):
            prologue()
            step(0, 0)
            step(1, 1)
            with eng.Fori(1, NT // 2 - 1) as j:
                step(2 * j, 0)
                step(2 * j + 1, 1)
            step(NT - 2, 0)
            step(NT - 1, 1)

        def has(n, k):
            return not isinstance(n, int) or n + k < NT

        @block.sync
        def _(sp):
            sp.dma_start(wo[:], a["Wo"].rearrange("(h p) m -> p h m", p=P)).then_inc(w_loaded, 16)
            sp.dma_start(x_all[:], a["x"].rearrange("(n p) d -> p n d", p=P)).then_inc(w_loaded, 16)
            sp.dma_start(b2[:], a["b2"].rearrange("(o d) -> o d", o=1).broadcast_to([P, D])).then_inc(w_loaded, 16)
            sp.dma_start(ln_w[:], a["ln2_w"].rearrange("(k p) -> p k", p=P),
                         allow_slow_non_contiguous=True).then_inc(w_loaded, 16)
            sp.dma_start(ln_b[:], a["ln2_b"].rearrange("(k p) -> p k", p=P),
                         allow_slow_non_contiguous=True).then_inc(w_loaded, 16)
            sp.dma_start(b1[:], a["b1"].rearrange("(f p) -> p f", p=P),
                         allow_slow_non_contiguous=True).then_inc(w_loaded, 16)

            def load(n, u):
                row = n * P if isinstance(n, int) else sp.snap(n * P)
                if not (isinstance(n, int) and n < 2):
                    sp.wait_ge(ot_done, 2 * n - 2)
                sp.dma_start(o_in[u][:], o_dram[ds(row, P), :].rearrange("p (h d) -> p h d", h=H)).then_inc(o_loaded[u], 16)

            load(0, 0)
            load(1, 1)
            sp.dma_start(w1[:], a["W1"].rearrange("(k p) m -> p k m", p=P)).then_inc(w_loaded, 16)
            sp.dma_start(w2[:], a["W2"].rearrange("(f p) m -> p f m", p=P)).then_inc(w_loaded, 16)
            with sp.Fori(1, NT // 2) as j:
                load(2 * j, 0)
                load(2 * j + 1, 1)

        @block.tensor
        def _(pe):
            def o_transposes(n, u):
                pe.wait_ge(o_loaded[u], 16 * (n // 2 + 1) if isinstance(n, int) else 8 * n + (16 if u == 0 else 8))
                if not (isinstance(n, int) and n == 0):
                    pe.wait_ge(ot_copied, 2 * n)
                for h in range(H):
                    last = nc.tensor.transpose(ps_ot[h // 4][:, h % 4, :], o_in[u][:, h, :], ident[:])
                    if h % 4 == 3:
                        last.then_inc(ot_done, 1)

            def attn(n):
                pe.wait_ge(ot_copied, 2 * n + 2)
                if not (isinstance(n, int) and n == 0):
                    pe.wait_ge(x1_ready, n)
                for h in range(H):
                    last = nc.tensor.matmul(ps_at[:], o_t[:, h, :], wo[:, h, :], start=(h == 0), stop=(h == H - 1))
                last.then_inc(attn_done, 1)

            def z_transposes(n):
                pe.wait_ge(z_ready, n + 1)
                if not (isinstance(n, int) and n == 0):
                    pe.wait_ge(ht_ready, 2 * n)
                for k in range(KD):
                    last = nc.tensor.transpose(ps_z[:, k, :], z[:, k * P:(k + 1) * P], ident[:])
                last.then_inc(zt_done, 1)

            def ffn1(n):
                pe.wait_ge(ht_ready, 2 * n + 2)
                for f in range(FT):
                    if f % 4 == 0 and not (isinstance(n, int) and n == 0):
                        pe.wait_ge(gelu_ready, 8 * n - 4 + f)
                    for k in range(KD):
                        last = nc.tensor.matmul(ps_f1[f // 4][:, f % 4, :], w1[:, k, f * P:(f + 1) * P], h_t[:, k, :],
                                                start=(k == 0), stop=(k == KD - 1), skip_group_check=True)
                    if f % 4 == 3:
                        last.then_inc(f1_done, 1)

            def ffn2(n):
                pe.wait_ge(gelu_ready, 8 * n + 8)
                if not (isinstance(n, int) and n == 0):
                    pe.wait_ge(total_ready, n)
                for f in range(FT):
                    last = nc.tensor.matmul(ps_f2[:], g_t[:, f, :], w2[:, f, :], start=(f == 0), stop=(f == FT - 1))
                last.then_inc(f2_done, 1)

            def prologue():
                pe.wait_ge(w_loaded, 16 * LOADS)
                o_transposes(0, 0)
                attn(0)
                o_transposes(1, 1)
                z_transposes(0)

            def step(n, u):
                ffn1(n)
                if has(n, 1):
                    attn(n + 1)
                ffn2(n)
                if has(n, 1):
                    z_transposes(n + 1)
                if has(n, 2):
                    o_transposes(n + 2, u)

            schedule(pe, prologue, step)

        @block.scalar
        def _(act):
            def o_copies(n):
                for i in range(2):
                    act.wait_ge(ot_done, 2 * n + i + 1)
                    nc.scalar.activation(o_t[:, 4 * i:4 * i + 4, :], ps_ot[i][:], ACT.Copy).then_inc(ot_copied, 1)

            def h_copies(n):
                act.wait_ge(zt_done, n + 1)
                for k in range(KD):
                    nc.scalar.activation(h_t[:, k, :], ps_z[:, k, :], ACT.Identity,
                                         bias=ln_b[:, k:k + 1], scale=ln_w[:, k:k + 1]).then_inc(ht_ready, 1)

            def gelus(n):
                for f in range(FT):
                    if f % 4 == 0:
                        act.wait_ge(f1_done, 2 * n + f // 4 + 1)
                    nc.scalar.activation(g_t[:, f, :], ps_f1[f // 4][:, f % 4, :], ACT.Gelu,
                                         bias=b1[:, f:f + 1]).then_inc(gelu_ready, 1)

            def prologue():
                act.wait_ge(w_loaded, 16 * LOADS)
                o_copies(0)
                o_copies(1)
                h_copies(0)

            def step(n, u):
                gelus(n)
                if has(n, 1):
                    h_copies(n + 1)
                if has(n, 2):
                    o_copies(n + 2)

            schedule(act, prologue, step)

        @block.vector
        def _(dve):
            def moments(c, n, t):
                nc.vector.bn_stats(stats[c][:], t).then_inc(stats_ready[c], 1)
                wait_apart(dve, stats_ready[c], n + 1, (w_loaded, 16 * LOADS))
                nc.vector.bn_aggr(mv[c][:], stats[c][:]).then_inc(mv_ready[c], 1)
                dve.wait_ge(mv_ready[c], n + 1)
                nc.vector.tensor_scalar(var[c][:], mv[c][:, 1:2], EPS, None, ALU.add).then_inc(var_ready[c], 1)
                dve.wait_ge(rstd_ready[c], n + 1)
                nc.vector.scalar_tensor_tensor(shift[c][:], mv[c][:, 0:1], -1.0, rstd[c][:], ALU.mult,
                                               ALU.mult).then_inc(shift_ready[c], 1)
                dve.wait_ge(shift_ready[c], n + 1)

            def tile_of(t, n):
                return t[:, ds(n, 1), :].rearrange("p a d -> p (a d)")

            def after_attn(n, u):
                if not (isinstance(n, int) and n == 0):
                    dve.wait_ge(base_ready, n)
                dve.wait_ge(attn_done, n + 1)
                nc.vector.tensor_tensor(x1[:], ps_at[:], tile_of(x_all, n), ALU.add).then_inc(x1_ready, 1)
                dve.wait_ge(x1_ready, n + 1)
                moments(0, n, x1[:])
                nc.vector.tensor_scalar(z[:], x1[:], rstd[0][:], shift[0][:], ALU.mult, ALU.add).then_inc(z_ready, 1)
                nc.vector.tensor_tensor(base[u][:], x1[:], tile_of(xb_all, n), ALU.add).then_inc(base_ready, 1)

            def after_ffn(n, u):
                dve.wait_ge(base_ready, n + 1)
                if not (isinstance(n, int) and n == 0):
                    dve.wait_ge(out_ready, n)
                dve.wait_ge(f2_done, n + 1)
                nc.vector.tensor_tensor(total[:], ps_f2[:], base[u][:], ALU.add).then_inc(total_ready, 1)
                dve.wait_ge(total_ready, n + 1)
                moments(1, n, total[:])
                nc.vector.tensor_scalar(tile_of(x1_all, n), total[:], rstd[1][:], shift[1][:], ALU.mult,
                                        ALU.add).then_inc(out_ready, 1)

            def prologue():
                dve.wait_ge(w_loaded, 16 * LOADS)
                nc.vector.tensor_tensor(xb_all[:], x_all[:], b2[:].unsqueeze(1).broadcast_to([P, NT, D]),
                                        ALU.add).then_inc(xb_ready, 1)
                dve.wait_ge(xb_ready, 1)
                after_attn(0, 0)

            def step(n, u):
                if has(n, 1):
                    after_attn(n + 1, 1 - u)
                after_ffn(n, u)

            schedule(dve, prologue, step)

        @block.gpsimd
        def _(pool):
            nc.gpsimd.memset(half[:], -0.5).then_inc(half_ready, 1)
            pool.wait_ge(half_ready, 1)

            def power(c, n):
                pool.wait_ge(var_ready[c], n + 1)
                nc.gpsimd.tensor_tensor(rstd[c][:], var[c][:], half[:], ALU.pow).then_inc(rstd_ready[c], 1)

            def prologue():
                power(0, 0)

            def step(n, u):
                if has(n, 1):
                    power(0, n + 1)
                power(1, n)

            schedule(pool, prologue, step)


NF = 4
TOPK = 12
FAR = -3.0e38


def xattn_stage(nc, a, ident, x1_all, x2_all):
    with ExitStack() as ctx:
        sb, ps, sem, start_block = tensors(nc, ctx, "xa_")
        fwd = sb("fwd", [P, 768])
        inv = sb("inv", [P, NF, 256])
        wts = {c: sb(f"w{c}", [P, KD, D]) for c in "qkvo"}
        dc_bias = sb("dc_bias", [1, 3, D])
        bo = sb("bo", [P, D])
        half = sb("half", [P, 4])
        ctx_in = sb("ctx_in", [P, CB, D])
        comb = {c: sb(f"comb_{c}", [P, 4, D]) for c in "xc"}
        fold = sb("fold", [P, 2, D])
        spec = {c: sb(f"spec_{c}", [P, KD, T]) for c in "xc"}
        proj = {c: sb(f"proj_{c}", [P, 2, 2, D]) for c in "qkv"}
        wspec = sb("wspec", [P, 2, 2, D])
        prod = sb("prod", [P, 2, 2, D])
        m = [sb(f"m{i}", [P, 2, D]) for i in range(4)]
        half_sums = [sb(f"half_sums{c}", [P, T]) for c in range(KD)]
        corr = [sb(f"corr{c}", [P, T]) for c in range(KD)]
        corr8 = [sb(f"corr8_{c}", [P, T]) for c in range(KD)]
        top = [sb(f"top{c}", [P, 16]) for c in range(KD)]
        nmax = [sb(f"nmax{c}", [P, 1]) for c in range(KD)]
        texp = [sb(f"texp{c}", [P, TOPK]) for c in range(KD)]
        tsum = [sb(f"tsum{c}", [P, 1]) for c in range(KD)]
        rsum = [sb(f"rsum{c}", [P, 1]) for c in range(KD)]
        dfold = [sb(f"dfold{c}", [P, 2, P]) for c in range(KD)]
        dcomb = [sb(f"dcomb{c}", [P, 4, P]) for c in range(KD)]
        dcomb_t = sb("dcomb_t", [P, 4, D])
        agg_t = [sb(f"agg_t{c}", [P, T]) for c in range(KD)]
        xbo = sb("xbo", [P, CB, D])
        stats, mv = sb("stats", [P, CB, 6]), sb("mv", [P, CB, 2])
        var, rstd, shift = sb("var", [P, CB]), sb("rstd", [P, CB]), sb("shift", [P, CB])
        tbank = [ps(f"t{i}", [P, T]) for i in range(2)]
        pbank = [ps(f"p{i}", [P, 2, D]) for i in range(4)]
        cbank = [ps(f"c{i}", [P, T]) for i in range(2)]

        loaded, ctx_loaded, half_ready, bias_ready = sem("loaded"), sem("ctx_loaded"), sem("half_ready"), sem("bias_ready")
        fold_ready = {c: sem(f"fold_{c}") for c in "xc"}
        comb_ready = {c: sem(f"comb_{c}") for c in "xc"}
        dft_done = {c: sem(f"dft_{c}") for c in "xc"}
        spec_ready = {c: sem(f"spec_{c}") for c in "xc"}
        proj_done = {c: sem(f"projd_{c}") for c in "qkv"}
        proj_ready = {c: sem(f"projr_{c}") for c in "qkv"}
        dc_ready = {c: sem(f"dc_{c}") for c in "qkv"}
        mul_ready = {c: sem(f"mul_{c}") for c in "qv"}
        add_ready = {c: sem(f"add_{c}") for c in "qv"}
        prod_ready = {c: sem(f"prod_{c}") for c in "qv"}
        corr_done, sums_ready, corr_ready = sem("corr_done"), sem("sums_ready"), sem("corr_ready")
        top8_ready, corr8_ready, top16_ready = sem("top8_ready"), sem("corr8_ready"), sem("top16_ready")
        taken_ready, nmax_ready, exp_ready, texp_ready = sem("taken_ready"), sem("nmax_ready"), sem("exp_ready"), sem("texp_ready")
        rsum_ready, weight_ready, scaled_ready = sem("rsum_ready"), sem("weight_ready"), sem("scaled_ready")
        dfold_ready, dcomb_ready = sem("dfold_ready"), sem("dcomb_ready")
        dt_done, dt_copied, wspec_done, wspec_ready = sem("dt_done"), sem("dt_copied"), sem("wspec_done"), sem("wspec_ready")
        agg_done, agg_sums, agg_ready = sem("agg_done"), sem("agg_sums"), sem("agg_ready")
        out_done, xbo_ready, res_ready = sem("out_done"), sem("xbo_ready"), sem("res_ready")
        stats_ready, mv_ready, var_ready, rstd_ready, shift_ready, x2_ready = (
            sem(q) for q in ("stats_ready", "mv_ready", "var_ready", "rstd_ready", "shift_ready", "x2_ready"))
        block = start_block()

        def schedule(eng, front, body):
            for part in range(3):
                front(0, part)
            body(0, lambda part: front(1, part))
            with eng.Fori(1, B - 1) as b:
                body(b, lambda part: front(b + 1, part))
            body(B - 1, lambda part: None)

        def ahead(b):
            return 0 if isinstance(b, int) and b == B - 1 else 1

        def wait_past(eng, sem_, value):
            if not (isinstance(value, int) and value == 0):
                eng.wait_ge(sem_, value)

        def first(b):
            return isinstance(b, int) and b == 0

        RE0, IM0, RE2, IM2 = (slice(64 * i, 64 * i + 64) for i in range(4))
        A_COLS, B_COLS = slice(256, 512), slice(512, 768)

        @block.sync
        def _(sp):
            sp.dma_start(fwd[:], a["dft_fwd"]).then_inc(loaded, 16)
            for c in "qkvo":
                sp.dma_start(wts[c][:], a[f"xattn_W{c}"].rearrange("(k p) m -> p k m", p=P)).then_inc(loaded, 16)
            sp.dma_start(inv[:], a["dft_inv"]).then_inc(loaded, 16)
            for i, c in enumerate("qkv"):
                sp.dma_start(dc_bias[:, i, :], a[f"xattn_b{c}"].rearrange("(o d) -> o d", o=1)).then_inc(loaded, 16)
            sp.dma_start(bo[:], a["xattn_bo"].rearrange("(o d) -> o d", o=1).broadcast_to([P, D])).then_inc(loaded, 16)

            def load(b):
                row = 0 if first(b) else sp.snap(b * T)
                if not first(b):
                    sp.wait_ge(fold_ready["c"], 2 * b)
                sp.dma_start(ctx_in[:], a["ctx_1024"][ds(row, T), :].rearrange("(j p) d -> p j d", p=P)).then_inc(ctx_loaded, 16)

            load(0)
            with sp.Fori(1, B) as b:
                load(b)

        @block.tensor
        def _(pe):
            def dft(c, b):
                pe.wait_ge(comb_ready[c], 2 * b + 2)
                for k in range(KD):
                    bank = tbank[k]
                    if c == "c":
                        pe.wait_ge(spec_ready["x"], 2 * b + k + 1)
                    elif not first(b):
                        pe.wait_ge(spec_ready["c"], 2 * b)
                        wait_past(pe, dt_copied, 2 * b - 2)

                    def mm(lo, hi, q, cols, start=True, stop=True):
                        return nc.tensor.matmul(bank[:, lo:hi], comb[c][:, q, k * P:(k + 1) * P], fwd[:, cols],
                                                start=start, stop=stop, skip_group_check=True)
                    mm(0, 64, 0, RE0)
                    mm(128, 192, 0, IM0)
                    mm(64, 128, 1, RE2)
                    mm(192, 256, 1, IM2)
                    mm(256, 512, 2, A_COLS, stop=False)
                    mm(256, 512, 3, B_COLS, start=False).then_inc(dft_done[c], 1)

            def project(c, b):
                src = "x" if c == "q" else "c"
                banks = pbank[0:2] if c == "q" else pbank[2:4]
                pe.wait_ge(spec_ready[src], 2 * b + 2)
                for half_ in range(2):
                    for reim in range(2):
                        ft = 2 * half_ + reim
                        for k in range(KD):
                            last = nc.tensor.matmul(banks[half_][:, reim, :], spec[src][:, k, ft * P:(ft + 1) * P],
                                                    wts[c][:, k, :], start=(k == 0), stop=(k == KD - 1),
                                                    skip_group_check=True)
                    last.then_inc(proj_done[c], 1)

            def inverse(done):
                for k in range(KD):
                    for ft in range(NF):
                        half_, reim = divmod(ft, 2)
                        last = nc.tensor.matmul(cbank[k][:, 256 * half_:256 * half_ + 256],
                                                prod[:, half_, reim, k * P:(k + 1) * P], inv[:, ft, :],
                                                start=(reim == 0), stop=(reim == 1), skip_group_check=True)
                    last.then_inc(done, 1)

            def front(b, part):
                if part == 0:
                    dft("x", b)
                    dft("c", b)
                    if not first(b):
                        pe.wait_ge(proj_ready["q"], 2 * b)
                        wait_past(pe, res_ready, 2 * b - 2)
                    project("q", b)
                    if not first(b):
                        pe.wait_ge(proj_ready["v"], 2 * b)
                    project("k", b)
                elif part == 1:
                    pe.wait_ge(prod_ready["q"], b + 1)
                    if not first(b):
                        pe.wait_ge(sums_ready, 2 * b)
                        wait_past(pe, agg_sums, 2 * b - 2)
                    inverse(corr_done)
                else:
                    pe.wait_ge(proj_ready["k"], 2 * b + 2)
                    project("v", b)

            def body(b, front_):
                front_(0)
                for k in range(KD):
                    pe.wait_ge(dcomb_ready, 4 * b + 2 * k + 2)
                    pe.wait_ge(spec_ready["c"], 2 * (b + ahead(b)) + 2)
                    for q in range(4):
                        last = nc.tensor.transpose(tbank[k][:, q * P:(q + 1) * P], dcomb[k][:, q, :], ident[:])
                    last.then_inc(dt_done, 1)
                pe.wait_ge(dt_copied, 2 * b + 2)
                pe.wait_ge(proj_ready["q"], 2 * (b + ahead(b)) + 2)

                def mm(out, cols, q, start=True, stop=True):
                    return nc.tensor.matmul(out, fwd[:, cols], dcomb_t[:, q, :], start=start, stop=stop,
                                            skip_group_check=True)
                mm(pbank[0][0:64, 0, :], RE0, 0)
                mm(pbank[0][64:128, 0, :], RE2, 1)
                mm(pbank[0][0:64, 1, :], IM0, 0)
                mm(pbank[0][64:128, 1, :], IM2, 1).then_inc(wspec_done, 1)
                for reim in range(2):
                    mm(pbank[1][:, reim, :], slice(256 + P * reim, 256 + P * (reim + 1)), 2, stop=False)
                    last = mm(pbank[1][:, reim, :], slice(512 + P * reim, 512 + P * (reim + 1)), 3, start=False)
                last.then_inc(wspec_done, 1)
                front_(1)
                pe.wait_ge(prod_ready["v"], b + 1)
                pe.wait_ge(sums_ready, 2 * (b + ahead(b)) + 2)
                inverse(agg_done)
                front_(2)
                pe.wait_ge(agg_ready, 4 * b + 4)
                pe.wait_ge(wspec_ready, 2 * b + 2)
                for tt in range(CB):
                    for k in range(KD):
                        last = nc.tensor.matmul(pbank[tt // 2][:, tt % 2, :], agg_t[k][:, tt * P:(tt + 1) * P],
                                                wts["o"][:, k, :], start=(k == 0), stop=(k == KD - 1),
                                                skip_group_check=True)
                    if tt % 2:
                        last.then_inc(out_done, 1)

            pe.wait_ge(loaded, 16 * 10)
            schedule(pe, front, body)

        @block.scalar
        def _(act):
            def copy(out, in_, done):
                nc.scalar.activation(out, in_, ACT.Copy).then_inc(done, 1)

            def front(b, part):
                if part == 0:
                    for c in "xc":
                        for k in range(KD):
                            act.wait_ge(dft_done[c], 2 * b + k + 1)
                            copy(spec[c][:, k, :], tbank[k][:], spec_ready[c])
                    if not first(b):
                        act.wait_ge(mul_ready["q"], 4 * b)
                    for c in "qk":
                        for i in range(2):
                            act.wait_ge(proj_done[c], 2 * b + i + 1)
                            copy(proj[c][:, i, :, :], pbank[i + (0 if c == "q" else 2)][:], proj_ready[c])
                elif part == 1:
                    for k in range(KD):
                        act.wait_ge(corr_done, 2 * b + k + 1)
                        if not first(b):
                            act.wait_ge(corr_ready, 4 * b)
                            wait_past(act, agg_ready, 4 * b - 4)
                        copy(half_sums[k][:], cbank[k][:], sums_ready)
                else:
                    for i in range(2):
                        act.wait_ge(proj_done["v"], 2 * b + i + 1)
                        if not first(b):
                            act.wait_ge(prod_ready["v"], b)
                        copy(proj["v"][:, i, :, :], pbank[2 + i][:], proj_ready["v"])

            def body(b, front_):
                front_(0)
                for k in range(KD):
                    act.wait_ge(nmax_ready, 2 * b + k + 1)
                    nc.scalar.activation(texp[k][:], top[k][:, 0:TOPK], ACT.Exp, bias=nmax[k][:],
                                         accum_out=tsum[k][:]).then_inc(texp_ready, 1)
                    act.wait_ge(corr8_ready, 2 * b + k + 1)
                    nc.scalar.activation(corr[k][:], corr[k][:], ACT.Exp, bias=nmax[k][:]).then_inc(exp_ready, 1)
                    act.wait_ge(taken_ready, 2 * b + k + 1)
                    nc.scalar.activation(corr8[k][:], corr8[k][:], ACT.Exp, bias=nmax[k][:]).then_inc(exp_ready, 1)
                for k in range(KD):
                    act.wait_ge(dt_done, 2 * b + k + 1)
                    copy(dcomb_t[:, :, k * P:(k + 1) * P], tbank[k][:].rearrange("p (q t) -> p q t", q=4), dt_copied)
                wait_past(act, mul_ready["v"], 4 * b)
                for i in range(2):
                    act.wait_ge(wspec_done, 2 * b + i + 1)
                    copy(wspec[:, i, :, :], pbank[i][:], wspec_ready)
                front_(1)
                for k in range(KD):
                    act.wait_ge(agg_done, 2 * b + k + 1)
                    act.wait_ge(corr_ready, 4 * (b + ahead(b)) + 4)
                    copy(half_sums[k][:], cbank[k][:], agg_sums)
                front_(2)

            act.wait_ge(loaded, 16 * 10)
            nc.scalar.activation(dc_bias[:], dc_bias[:], ACT.Copy, scale=float(T)).then_inc(bias_ready, 1)
            schedule(act, front, body)

        @block.vector
        def _(dve):
            V = nc.vector
            held = (loaded, 16 * 10)

            def four_quarters(c, b, src):
                V.tensor_tensor(fold[:], src[:, 0:2, :], src[:, 2:4, :], ALU.add).then_inc(fold_ready[c], 1)
                V.tensor_tensor(comb[c][:, 2:4, :], src[:, 0:2, :], src[:, 2:4, :], ALU.subtract).then_inc(fold_ready[c], 1)
                dve.wait_ge(fold_ready[c], 2 * b + 2)
                V.tensor_tensor(comb[c][:, 0, :], fold[:, 0, :], fold[:, 1, :], ALU.add).then_inc(comb_ready[c], 1)
                V.tensor_tensor(comb[c][:, 1, :], fold[:, 0, :], fold[:, 1, :], ALU.subtract).then_inc(comb_ready[c], 1)

            def bias_at_dc(c, b):
                i = "qkv".index(c)
                dve.wait_ge(proj_ready[c], 2 * b + 2)
                V.tensor_tensor(proj[c][0:1, 0, 0, :], proj[c][0:1, 0, 0, :], dc_bias[0:1, i, :], ALU.add).then_inc(dc_ready[c], 1)
                dve.wait_ge(dc_ready[c], b + 1)

            def multiply(key, b, p, q):
                re, im = (lambda t: t[:, :, 0, :]), (lambda t: t[:, :, 1, :])
                for i, (x, y) in enumerate(((re(p), re(q)), (im(p), im(q)), (im(p), re(q)), (re(p), im(q)))):
                    V.tensor_tensor(m[i][:], x, y, ALU.mult).then_inc(mul_ready[key], 1)
                dve.wait_ge(mul_ready[key], 4 * b + 4)
                V.tensor_tensor(prod[:, :, 0, :], m[0][:], m[1][:], ALU.add).then_inc(add_ready[key], 1)
                V.tensor_tensor(prod[:, :, 1, :], m[2][:], m[3][:], ALU.subtract).then_inc(add_ready[key], 1)
                dve.wait_ge(add_ready[key], 2 * b + 2)
                V.tensor_copy(prod[0:1, 0, 0, :], m[0][0:1, 0, :])
                V.tensor_copy(prod[0:1, 0, 1, :], m[1][0:1, 0, :]).then_inc(prod_ready[key], 1)

            def unfold(out, sums, done, k):
                V.tensor_tensor(out[:, 0:256], sums[:, 0:256], sums[:, 256:512], ALU.add).then_inc(done, 1)
                V.tensor_tensor(out[:, 256:512], sums[:, 0:256], sums[:, 256:512], ALU.subtract).then_inc(done, 1)

            def front(b, part):
                if part == 0:
                    if not first(b):
                        dve.wait_ge(comb_ready["c"], 2 * b)
                        dve.wait_ge(dft_done["c"], 2 * b)
                    four_quarters("x", b, x1_all[:, ds(b * CB, CB), :])
                    dve.wait_ge(ctx_loaded, 16 * b + 16)
                    dve.wait_ge(comb_ready["x"], 2 * b + 2)
                    four_quarters("c", b, ctx_in)
                elif part == 1:
                    bias_at_dc("q", b)
                    bias_at_dc("k", b)
                    multiply("q", b, proj["q"], proj["k"])
                else:
                    for k in range(KD):
                        dve.wait_ge(sums_ready, 2 * b + k + 1)
                        unfold(corr[k], half_sums[k], corr_ready, k)

            def body(b, front_):
                front_(0)
                for k in range(KD):
                    wait_apart(dve, corr_ready, 4 * b + 2 * k + 2, held)
                    V.max(top[k][:, 0:8], corr[k][:]).then_inc(top8_ready, 1)
                    wait_apart(dve, top8_ready, 2 * b + k + 1, held)
                    V.match_replace(corr8[k][:], top[k][:, 0:8], corr[k][:], FAR).then_inc(corr8_ready, 1)
                    wait_apart(dve, corr8_ready, 2 * b + k + 1, held)
                    V.max(top[k][:, 8:16], corr8[k][:]).then_inc(top16_ready, 1)
                    dve.wait_ge(top16_ready, 2 * b + k + 1)
                    V.tensor_scalar(nmax[k][:], top[k][:, 0:1], -1.0, None, ALU.mult).then_inc(nmax_ready, 1)
                    V.memset(top[k][:, TOPK:16], FAR).then_inc(rsum_ready, 1)
                    wait_apart(dve, rsum_ready, 4 * b + 2 * k + 1, held)
                    V.match_replace(corr8[k][:], top[k][:, 8:16], corr8[k][:], FAR).then_inc(taken_ready, 1)
                    dve.wait_ge(texp_ready, 2 * b + k + 1)
                    V.reciprocal(rsum[k][:], tsum[k][:]).then_inc(rsum_ready, 1)
                for k in range(KD):
                    dve.wait_ge(exp_ready, 4 * b + 2 * k + 2)
                    dve.wait_ge(rsum_ready, 4 * b + 2 * k + 2)
                    V.tensor_tensor(corr[k][:], corr[k][:], corr8[k][:], ALU.subtract).then_inc(weight_ready, 1)
                    dve.wait_ge(weight_ready, 2 * b + k + 1)
                    V.tensor_scalar(corr[k][:], corr[k][:], rsum[k][:], None, ALU.mult).then_inc(scaled_ready, 1)
                    dve.wait_ge(scaled_ready, 2 * b + k + 1)
                    quarters = corr[k][:].rearrange("p (j t) -> p j t", j=4)
                    V.tensor_tensor(dfold[k][:], quarters[:, 0:2, :], quarters[:, 2:4, :], ALU.add).then_inc(dfold_ready, 1)
                    V.tensor_tensor(dcomb[k][:, 2:4, :], quarters[:, 0:2, :], quarters[:, 2:4, :], ALU.subtract).then_inc(dfold_ready, 1)
                    dve.wait_ge(dfold_ready, 4 * b + 2 * k + 2)
                    V.tensor_tensor(dcomb[k][:, 0, :], dfold[k][:, 0, :], dfold[k][:, 1, :], ALU.add).then_inc(dcomb_ready, 1)
                    V.tensor_tensor(dcomb[k][:, 1, :], dfold[k][:, 0, :], dfold[k][:, 1, :], ALU.subtract).then_inc(dcomb_ready, 1)
                front_(1)
                front_(2)
                bias_at_dc("v", b)
                dve.wait_ge(wspec_ready, 2 * b + 2)
                dve.wait_ge(corr_done, 2 * (b + ahead(b)) + 2)
                multiply("v", b, proj["v"], wspec)
                V.tensor_tensor(xbo[:], x1_all[:, ds(b * CB, CB), :], bo[:].unsqueeze(1).broadcast_to([P, CB, D]),
                                ALU.add).then_inc(xbo_ready, 1)
                for k in range(KD):
                    dve.wait_ge(agg_sums, 2 * b + k + 1)
                    unfold(agg_t[k], half_sums[k], agg_ready, k)
                dve.wait_ge(xbo_ready, b + 1)
                for i in range(2):
                    dve.wait_ge(out_done, 2 * b + i + 1)
                    V.tensor_tensor(xbo[:, 2 * i:2 * i + 2, :], pbank[i][:], xbo[:, 2 * i:2 * i + 2, :], ALU.add).then_inc(res_ready, 1)
                for j in range(CB):
                    dve.wait_ge(res_ready, 2 * b + j // 2 + 1)
                    V.bn_stats(stats[:, j, :], xbo[:, j, :]).then_inc(stats_ready, 1)
                for j in range(CB):
                    wait_apart(dve, stats_ready, 4 * b + j + 1, held)
                    V.bn_aggr(mv[:, j, :], stats[:, j, :]).then_inc(mv_ready, 1)
                dve.wait_ge(mv_ready, 4 * b + 4)
                V.tensor_scalar(var[:], mv[:, :, 1], EPS, None, ALU.add).then_inc(var_ready, 1)
                dve.wait_ge(rstd_ready, b + 1)
                V.scalar_tensor_tensor(shift[:], mv[:, :, 0], -1.0, rstd[:], ALU.mult, ALU.mult).then_inc(shift_ready, 1)
                dve.wait_ge(shift_ready, b + 1)
                for j in range(CB):
                    V.tensor_scalar(x2_all[:, ds(b * CB + j, 1), :].rearrange("p a d -> p (a d)"), xbo[:, j, :],
                                    rstd[:, j:j + 1], shift[:, j:j + 1], ALU.mult, ALU.add).then_inc(x2_ready, 1)

            dve.wait_ge(loaded, 16 * 10)
            dve.wait_ge(bias_ready, 1)
            schedule(dve, front, body)

        @block.gpsimd
        def _(pool):
            nc.gpsimd.memset(half[:], -0.5).then_inc(half_ready, 1)
            pool.wait_ge(half_ready, 1)
            with pool.Fori(0, B) as b:
                pool.wait_ge(var_ready, b + 1)
                nc.gpsimd.tensor_tensor(rstd[:], var[:], half[:], ALU.pow).then_inc(rstd_ready, 1)


NE = 8
TILES = NT + NE - 1


def experts_stage(nc, a, ident, x2_all, gathered_all, out, xs_dram, ys_dram):
    with ExitStack() as ctx:
        sb, ps, sem, start_block = tensors(nc, ctx, "ex_")
        w1 = sb("w1", [P, NE, KD, F])
        w2 = sb("w2", [P, NE, FT, D])
        b1 = sb("b1", [P, NE, FT])
        b2 = sb("b2", [P, NE, D])
        wr = sb("wr", [P, KD, NE])
        br = sb("br", [P, NE])
        order = sb("order", [P, NE])
        edges = sb("edges", [P, NT])
        index = sb("index", [P, TILES])
        mask_strict = sb("mask_strict", [P, P])
        ones = sb("ones", [P, P])
        zero = sb("zero", [P, D])
        half = sb("half", [P, NT])
        xr = [sb(f"xr{i}", [P, 2, KD, P]) for i in range(2)]
        logit, ex, onehot = sb("logit", [P, NT, NE]), sb("exps", [P, NT, NE]), sb("onehot", [P, NT, NE])
        rank, tot, incl = sb("rank", [P, NT, NE]), sb("tot", [P, NT, NE]), sb("incl", [P, NT, NE])
        top, gate = sb("top", [P, NT]), sb("gate", [P, NT])
        over = sb("over", [P, NE, NT])
        tiles, tend, tstart = sb("tiles", [P, NE]), sb("tend", [P, NE]), sb("tstart", [P, NE])
        starts = sb("starts", [P, TILES, NE])
        expert_f, expert = sb("expert_f", [P, TILES]), sb("expert", [P, TILES], I32)
        pos_f, pos = sb("pos_f", [P, NT]), sb("pos", [P, NT], I32)
        x_in = sb("x_in", [P, D])
        x_t = sb("x_t", [P, KD, P])
        h = sb("h", [P, F])
        h_t = sb("h_t", [P, FT, P])
        b1_now = sb("b1_now", [P, FT])
        y = sb("y", [P, D])
        stats, mv = sb("stats", [P, NT, 6]), sb("mv", [P, NT, 2])
        var, rstd, shift = sb("var", [P, NT]), sb("rstd", [P, NT]), sb("shift", [P, NT])
        ps_r = [ps(f"r{i}", [P, 2, KD, P]) for i in range(2)]
        ps_l = ps("l", [P, NT, NE])
        ps_h = [ps(f"h_ps{i}", [P, 512]) for i in range(2)]
        ps_ht = [ps(f"ht{i}", [P, 4, P]) for i in range(2)]
        ps_y = ps("y_ps", [P, D])
        ps_x = ps_r[0]

        r_loaded, w_loaded, ones_ready, half_ready, zero_ready, zeroed = (
            sem(q) for q in ("r_loaded", "w_loaded", "ones_ready", "half_ready", "zero_ready", "zeroed"))
        rt_done, rt_copied, logits_done = sem("rt_done"), sem("rt_copied"), sem("logits_done")
        route, diff_ready, ex_ready, onehot_ready = sem("route"), sem("diff_ready"), sem("ex_ready"), sem("onehot_ready")
        counts_done, pos_ready, expert_ready = sem("counts_done"), sem("pos_ready"), sem("expert_ready")
        scattered, x_loaded, xt_done, xt_copied = sem("scattered"), sem("x_loaded"), sem("xt_done"), sem("xt_copied")
        h_done, h_copied, ht_done, relu_ready = sem("h_done"), sem("h_copied"), sem("ht_done"), sem("relu_ready")
        b1_ready, y_done, y_ready, y_stored, gathered = (
            sem(q) for q in ("b1_ready", "y_done", "y_ready", "y_stored", "gathered"))
        sum_ready, stats_ready, var_ready, rstd_ready, out_ready, out_stored = (
            sem(q) for q in ("sum_ready", "stats_ready", "var_ready", "rstd_ready", "out_ready", "out_stored"))
        block = start_block()
        R_LOADS, W_LOADS = 6, 2 * NE + 2

        @block.sync
        def _(sp):
            sp.dma_start(wr[:], a["ffn_Wr"].rearrange("(k p) e -> p k e", p=P)).then_inc(r_loaded, 16)
            sp.dma_start(br[:], a["ffn_br"].rearrange("(o e) -> o e", o=1).broadcast_to([P, NE])).then_inc(r_loaded, 16)
            sp.dma_start(order[:], a["expert_order"]).then_inc(r_loaded, 16)
            sp.dma_start(edges[:], a["tile_edges"]).then_inc(r_loaded, 16)
            sp.dma_start(index[:], a["tile_index"]).then_inc(r_loaded, 16)
            sp.dma_start(mask_strict[:], a["mask_strict"]).then_inc(r_loaded, 16)
            sp.wait_ge(zero_ready, 1)
            sp.dma_start(xs_dram.rearrange("(n p) d -> p n d", p=P),
                         zero[:].unsqueeze(1).broadcast_to([P, TILES, D])).then_inc(zeroed, 16)
            sp.dma_start(b1[:], a["ffn_b1_cols"]).then_inc(w_loaded, 16)
            sp.dma_start(b2[:], a["ffn_b2"].rearrange("(o e) d -> o e d", o=1).broadcast_to([P, NE, D])).then_inc(w_loaded, 16)
            for e in range(NE):
                sp.dma_start(w1[:, e, :, :], a["ffn_W1"][e, :, :].rearrange("(k p) f -> p k f", p=P)).then_inc(w_loaded, 16)
                sp.dma_start(w2[:, e, :, :], a["ffn_W2"][e, :, :].rearrange("(f p) d -> p f d", p=P)).then_inc(w_loaded, 16)

            def load(j):
                row = j * P if isinstance(j, int) else sp.snap(j * P)
                if not (isinstance(j, int) and j == 0):
                    sp.wait_ge(xt_done, j)
                sp.dma_start(x_in[:], xs_dram[ds(row, P), :]).then_inc(x_loaded, 16)

            def store(j):
                row = j * P if isinstance(j, int) else sp.snap(j * P)
                sp.wait_ge(y_ready, j + 1)
                sp.dma_start(ys_dram[ds(row, P), :], y[:]).then_inc(y_stored, 16)

            sp.wait_ge(scattered, 16 * NT)
            load(0)
            load(1)
            load(2)
            with sp.Fori(0, TILES - 3) as j:
                store(j)
                load(j + 3)
            for j in range(TILES - 3, TILES):
                store(j)
            for q in range(4):
                sp.wait_ge(out_ready, 4 * q + 4)
                sp.dma_start(out.rearrange("(n p) d -> p n d", p=P)[:, 4 * q:4 * q + 4, :],
                             gathered_all[:, 4 * q:4 * q + 4, :]).then_inc(out_stored, 16)
            sp.wait_ge(out_stored, 64)
            sp.wait_ge(y_stored, 16 * TILES)

        @block.tensor
        def _(pe):
            pe.wait_ge(r_loaded, 16 * R_LOADS)

            def logits(g):
                pe.wait_ge(rt_copied, g + 1)
                for n in (2 * g, 2 * g + 1):
                    for k in range(KD):
                        last = nc.tensor.matmul(ps_l[:, n, :], xr[g % 2][:, n % 2, k, :], wr[:, k, :],
                                                start=(k == 0), stop=(k == KD - 1), skip_group_check=True)
                return last

            for g in range(NT // 2):
                if g >= 2:
                    pe.wait_ge(rt_copied, g - 1)
                for n in (2 * g, 2 * g + 1):
                    for k in range(KD):
                        last = nc.tensor.transpose(ps_r[g % 2][:, n % 2, k, :], x2_all[:, n, k * P:(k + 1) * P], ident[:])
                last.then_inc(rt_done, 1)
                if g:
                    logits(g - 1)
            logits(NT // 2 - 1).then_inc(logits_done, 1)
            pe.wait_ge(onehot_ready, 1)
            pe.wait_ge(ones_ready, 1)
            flat = onehot[:].rearrange("p n e -> p (n e)")
            nc.tensor.matmul(ps_h[0][:, 0:NT * NE], mask_strict[:], flat, start=True, stop=True)
            nc.tensor.matmul(ps_h[1][:, 0:NT * NE], ones[:], flat, start=True, stop=True).then_inc(counts_done, 1)

            def x_transposes(j):
                pe.wait_ge(x_loaded, 16 * j + 16)
                if not (isinstance(j, int) and j == 0):
                    pe.wait_ge(xt_copied, j)
                for k in range(KD):
                    last = nc.tensor.transpose(ps_x[:, 0, k, :], x_in[:, k * P:(k + 1) * P], ident[:])
                last.then_inc(xt_done, 1)

            def up(j, e):
                pe.wait_ge(xt_copied, j + 1)
                for i in range(2):
                    if not (isinstance(j, int) and j == 0):
                        pe.wait_ge(h_copied, 2 * j + i - 1)
                    for k in range(KD):
                        last = nc.tensor.matmul(ps_h[i][:], x_t[:, k, :],
                                                w1[:, ds(e, 1), k, i * 512:(i + 1) * 512].rearrange("p o f -> p (o f)"),
                                                start=(k == 0), stop=(k == KD - 1))
                    last.then_inc(h_done, 1)

            def h_transposes(j):
                for i in range(2):
                    pe.wait_ge(h_copied, 2 * j + i + 1)
                    if not (isinstance(j, int) and j == 0):
                        pe.wait_ge(relu_ready, 8 * j + 4 * i - 4)
                    for f in range(4):
                        last = nc.tensor.transpose(ps_ht[i][:, f, :], h[:, (4 * i + f) * P:(4 * i + f + 1) * P], ident[:])
                    last.then_inc(ht_done, 1)

            def down(j, e):
                pe.wait_ge(relu_ready, 8 * j + 8)
                if not (isinstance(j, int) and j == 0):
                    pe.wait_ge(y_ready, j)
                for f in range(FT):
                    last = nc.tensor.matmul(ps_y[:], h_t[:, f, :], w2[:, ds(e, 1), f, :].rearrange("p o d -> p (o d)"),
                                            start=(f == 0), stop=(f == FT - 1))
                last.then_inc(y_done, 1)

            def expert_of(j):
                return pe.value_load(expert[0:1, ds(j, 1)], min_val=0, max_val=NE - 1)

            pe.wait_ge(expert_ready, 1)
            e0 = expert_of(0)
            pe.wait_ge(w_loaded, 16 * W_LOADS)
            x_transposes(0)
            up(0, e0)
            h_transposes(0)
            x_transposes(1)
            with pe.Fori(0, TILES - 2) as j:
                e_up, e_down = expert_of(j + 1), expert_of(j)
                up(j + 1, e_up)
                down(j, e_down)
                h_transposes(j + 1)
                x_transposes(j + 2)
            j = TILES - 2
            e_up, e_down = expert_of(j + 1), expert_of(j)
            up(j + 1, e_up)
            down(j, e_down)
            h_transposes(j + 1)
            down(j + 1, e_up)

        @block.scalar
        def _(act):
            for g in range(NT // 2):
                if g >= 2:
                    act.wait_ge(rt_done, g)
                act.wait_ge(rt_done, g + 1)
                nc.scalar.activation(xr[g % 2][:], ps_r[g % 2][:], ACT.Copy).then_inc(rt_copied, 1)
            act.wait_ge(diff_ready, 1)
            nc.scalar.activation(ex[:], ex[:], ACT.Exp).then_inc(ex_ready, 1)

            def x_copy(j):
                act.wait_ge(xt_done, j + 1)
                nc.scalar.activation(x_t[:], ps_x[:, 0, :, :], ACT.Copy).then_inc(xt_copied, 1)

            def h_copies(j):
                for i in range(2):
                    act.wait_ge(h_done, 2 * j + i + 1)
                    nc.scalar.activation(h[:, i * 512:(i + 1) * 512], ps_h[i][:], ACT.Copy).then_inc(h_copied, 1)

            x_copy(0)
            h_copies(0)
            x_copy(1)
            with act.Fori(0, TILES - 2) as j:
                h_copies(j + 1)
                x_copy(j + 2)
            h_copies(TILES - 1)

        @block.vector
        def _(dve):
            V = nc.vector
            made = [0]

            def then(ins):
                made[0] += 1
                ins.then_inc(route, 1)
                dve.wait_ge(route, made[0])

            def over_experts(t):
                return t.unsqueeze(2).broadcast_to([P, NT, NE])

            def over_tiles(t):
                return t.unsqueeze(1).broadcast_to([P, NT, NE])

            V.memset(zero[:], 0.0).then_inc(zero_ready, 1)
            V.memset(ones[:], 1.0).then_inc(ones_ready, 1)
            dve.wait_ge(ones_ready, 1)
            dve.wait_ge(r_loaded, 16 * R_LOADS)
            dve.wait_ge(logits_done, 1)
            then(V.tensor_tensor(logit[:], ps_l[:], over_tiles(br[:]), ALU.add))
            then(V.tensor_reduce(top[:], logit[:], AX, ALU.max))
            V.tensor_tensor(ex[:], logit[:], over_experts(top[:]), ALU.subtract).then_inc(diff_ready, 1)
            then(V.tensor_tensor(onehot[:], logit[:], over_experts(top[:]), ALU.is_equal))
            then(V.tensor_tensor(onehot[:], onehot[:], over_tiles(order[:]), ALU.mult))
            then(V.tensor_reduce(top[:], onehot[:], AX, ALU.max))
            V.tensor_tensor(onehot[:], onehot[:], over_experts(top[:]), ALU.is_equal).then_inc(onehot_ready, 1)
            dve.wait_ge(ex_ready, 1)
            then(V.tensor_reduce(gate[:], ex[:], AX, ALU.add))
            then(V.reciprocal(gate[:], gate[:]))
            dve.wait_ge(counts_done, 1)
            then(V.tensor_copy(rank[:].rearrange("p n e -> p (n e)"), ps_h[0][:, 0:NT * NE]))
            then(V.tensor_copy(tot[:].rearrange("p n e -> p (n e)"), ps_h[1][:, 0:NT * NE]))
            for e in range(NE):
                then(V.tensor_tensor_scan(incl[:, :, e], ones[:, 0:NT], tot[:, :, e], 0.0, ALU.mult, ALU.add))
            then(V.tensor_tensor(over[:], incl[:, NT - 1, :].unsqueeze(2).broadcast_to([P, NE, NT]),
                                 edges[:].unsqueeze(1).broadcast_to([P, NE, NT]), ALU.is_gt))
            then(V.tensor_reduce(tiles[:], over[:], AX, ALU.add))
            then(V.tensor_tensor_scan(tend[:], ones[:, 0:NE], tiles[:], 0.0, ALU.mult, ALU.add))
            then(V.tensor_tensor(tstart[:], tend[:], tiles[:], ALU.subtract))
            then(V.tensor_tensor(starts[:], index[:].unsqueeze(2).broadcast_to([P, TILES, NE]),
                                 tstart[:].unsqueeze(1).broadcast_to([P, TILES, NE]), ALU.is_ge))
            then(V.tensor_reduce(expert_f[:], starts[:], AX, ALU.add))
            V.tensor_scalar(expert[:], expert_f[:], -1.0, None, ALU.add).then_inc(expert_ready, 1)
            then(V.tensor_tensor(rank[:], rank[:], incl[:], ALU.add))
            then(V.tensor_tensor(rank[:], rank[:], tot[:], ALU.subtract))
            then(V.tensor_scalar(tstart[:], tstart[:], float(P), None, ALU.mult))
            then(V.tensor_tensor(rank[:], rank[:], over_tiles(tstart[:]), ALU.add))
            then(V.tensor_tensor(rank[:], rank[:], onehot[:], ALU.mult))
            then(V.tensor_reduce(pos_f[:], rank[:], AX, ALU.add))
            V.tensor_copy(pos[:], pos_f[:]).then_inc(pos_ready, 1)
            dve.wait_ge(expert_ready, 1)
            dve.wait_ge(w_loaded, 16 * W_LOADS)

            def expert_of(j):
                return dve.value_load(expert[0:1, ds(j, 1)], min_val=0, max_val=NE - 1)

            def relus(j, e):
                if not (isinstance(j, int) and j == 0):
                    dve.wait_ge(relu_ready, 8 * j)
                V.tensor_scalar(b1_now[:], b1[:, ds(e, 1), :].rearrange("p o f -> p (o f)"), 1.0, None,
                                ALU.mult).then_inc(b1_ready, 1)
                dve.wait_ge(b1_ready, j + 1)
                for i in range(2):
                    dve.wait_ge(ht_done, 2 * j + i + 1)
                    for f in range(4):
                        V.tensor_scalar(h_t[:, 4 * i + f, :], ps_ht[i][:, f, :], b1_now[:, 4 * i + f:4 * i + f + 1], 0.0,
                                        ALU.add, ALU.max).then_inc(relu_ready, 1)

            def y_out(j, e):
                if not (isinstance(j, int) and j == 0):
                    dve.wait_ge(y_stored, 16 * j)
                dve.wait_ge(y_done, j + 1)
                V.tensor_tensor(y[:], ps_y[:], b2[:, ds(e, 1), :].rearrange("p o d -> p (o d)"), ALU.add).then_inc(y_ready, 1)

            relus(0, expert_of(0))
            e_first = expert_of(0)
            y_out(0, e_first)
            e_next = expert_of(1)
            relus(1, e_next)
            with dve.Fori(1, TILES - 1) as j:
                e_down, e_up = expert_of(j), expert_of(j + 1)
                y_out(j, e_down)
                relus(j + 1, e_up)
            y_out(TILES - 1, expert_of(TILES - 1))

            dve.wait_ge(gathered, 16 * NT)
            with dve.Fori(0, NT) as n:
                row = gathered_all[:, ds(n, 1), :].rearrange("p a d -> p (a d)")
                V.scalar_tensor_tensor(row, row, gate[:, ds(n, 1)], x2_all[:, ds(n, 1), :].rearrange("p a d -> p (a d)"),
                                       ALU.mult, ALU.add).then_inc(sum_ready, 1)
                dve.wait_ge(sum_ready, n + 1)
                V.bn_stats(stats[:, ds(n, 1), :].rearrange("p a d -> p (a d)"), row).then_inc(stats_ready, 1)
            dve.wait_ge(stats_ready, NT)
            for n in range(NT):
                V.bn_aggr(mv[:, n, :], stats[:, n, :]).then_inc(stats_ready, 1)
            dve.wait_ge(stats_ready, 2 * NT)
            V.tensor_scalar(var[:], mv[:, :, 1], EPS, None, ALU.add).then_inc(var_ready, 1)
            dve.wait_ge(rstd_ready, 1)
            then(V.scalar_tensor_tensor(shift[:], mv[:, :, 0], -1.0, rstd[:], ALU.mult, ALU.mult))
            with dve.Fori(0, NT) as n:
                row = gathered_all[:, ds(n, 1), :].rearrange("p a d -> p (a d)")
                V.tensor_scalar(row, row, rstd[:, ds(n, 1)], shift[:, ds(n, 1)], ALU.mult, ALU.add).then_inc(out_ready, 1)

        @block.gpsimd
        def _(pool):
            nc.gpsimd.memset(half[:], -0.5).then_inc(half_ready, 1)
            pool.wait_ge(half_ready, 1)
            pool.wait_ge(zeroed, 16)
            pool.wait_ge(pos_ready, 1)
            for n in range(NT):
                nc.gpsimd.indirect_dma_start(out=xs_dram, out_offset=bass.IndirectOffsetOnAxis(ap=pos[:, n:n + 1], axis=0),
                                             in_=x2_all[:, n, :], in_offset=None).then_inc(scattered, 16)
            pool.wait_ge(y_stored, 16 * TILES)
            for n in range(NT):
                nc.gpsimd.indirect_dma_start(out=gathered_all[:, n, :], out_offset=None, in_=ys_dram,
                                             in_offset=bass.IndirectOffsetOnAxis(ap=pos[:, n:n + 1], axis=0)).then_inc(gathered, 16)
            pool.wait_ge(var_ready, 1)
            nc.gpsimd.tensor_tensor(rstd[:], var[:], half[:], ALU.pow).then_inc(rstd_ready, 1)


def constants():
    import numpy as np
    i = np.arange(P)
    row, colm = i[:, None], i[None, :]
    c = {"ident": np.eye(P), "mask_incl": row <= colm, "mask_strict": row < colm}
    keep = np.ones((P, NT, H))
    keep[:, CB - 1::CB, :] = 0
    c["keep"] = keep.reshape(P, NT * H)

    def joins(b):
        return (row // (2 * b) == colm // (2 * b)) & (row // b % 2 == 1) & (colm // b % 2 == 0)

    c["mask_one"] = joins(1).T | (row == colm)
    c["mask_levels"] = np.stack([joins(2 << lev) | (row == colm) for lev in range(LEVELS)], axis=1)

    c["expert_order"] = np.tile(np.arange(NE, 0, -1), (P, 1))
    c["tile_edges"] = np.tile(P * np.arange(NT), (P, 1))
    c["tile_index"] = np.tile(np.arange(TILES), (P, 1))
    p, m64, m128 = np.arange(P)[:, None], np.arange(64)[None, :], np.arange(P)[None, :]

    def angle(f, t):
        return 2 * np.pi * ((f * t) % T) / T

    re0, im0 = np.cos(angle(4 * m64, p)), -np.sin(angle(4 * m64, p))
    im0[:, 0] = np.cos(angle(T // 2, p))[:, 0]
    re2, im2 = np.cos(angle(4 * m64 + 2, p)), -np.sin(angle(4 * m64 + 2, p))
    c1, s1 = np.cos(angle(4 * m128 + 1, p)), np.sin(angle(4 * m128 + 1, p))
    c["dft_fwd"] = np.concatenate([re0, im0, re2, im2, c1, -s1, -s1, -c1], axis=1)
    weight = np.where(m64.T == 0, 1.0, 2.0) / T
    z0re, z0im = weight * re0.T, weight * im0.T
    z2re, z2im = 2 / T * re2.T, 2 / T * im2.T
    even_re = np.concatenate([np.hstack([z0re, z0re]), np.hstack([z2re, -z2re])])
    even_im = np.concatenate([np.hstack([z0im, z0im]), np.hstack([z2im, -z2im])])
    odd_re = 2 / T * np.hstack([c1.T, -s1.T])
    odd_im = 2 / T * np.hstack([-s1.T, -c1.T])
    c["dft_inv"] = np.stack([even_re, even_im, odd_re, odd_im], axis=1)
    return {k: np.ascontiguousarray(v, np.float32) for k, v in c.items()}


UPTO = 5


def program(nc, a, out):
    qkv_dram = nc.dram_tensor("qkv_dram", (B * T, 3 * HW), F32, kind="Internal").ap()
    scal_dram = nc.dram_tensor("scal_dram", (NT, P, NSC * H), F32, kind="Internal").ap()
    grow_dram = nc.dram_tensor("grow_dram", (NT * H, P), F32, kind="Internal").ap()
    o_dram = nc.dram_tensor("o_dram", (B * T, HW), F32, kind="Internal").ap()
    xs_dram = nc.dram_tensor("xs_dram", (TILES * P, D), F32, kind="Internal").ap()
    ys_dram = nc.dram_tensor("ys_dram", (TILES * P, D), F32, kind="Internal").ap()
    with ExitStack() as ctx:
        ident = ctx.enter_context(nc.sbuf_tensor("ident", [P, P], F32))
        ident_loaded = ctx.enter_context(nc.semaphore("ident_loaded"))
        with nc.Block() as block:
            @block.sync
            def _(sp):
                sp.dma_start(ident[:], a["ident"]).then_inc(ident_loaded, 16)
                sp.wait_ge(ident_loaded, 16)
        project_stage(nc, a, ident, qkv_dram, scal_dram, grow_dram)
        if UPTO >= 2:
            delta_stage(nc, a, ident, qkv_dram, scal_dram, grow_dram, o_dram)
        x1_all = ctx.enter_context(nc.sbuf_tensor("x1_all", [P, NT, D], F32))
        x2_all = ctx.enter_context(nc.sbuf_tensor("x2_all", [P, NT, D], F32))
        if UPTO >= 3:
            ffn_stage(nc, a, ident, o_dram, x1_all)
        if UPTO >= 4:
            xattn_stage(nc, a, ident, x1_all, x2_all)
        if UPTO >= 5:
            experts_stage(nc, a, ident, x2_all, x1_all, out, xs_dram, ys_dram)


def kernel(**inputs):
    import numpy as np
    import concourse.bacc as bacc
    from concourse.bass_utils import run_bass_kernel_spmd

    nc = bacc.Bacc("TRN2", target_bir_lowering=False, num_devices=1)
    arrays = {}
    for name, v in inputs.items():
        v = np.ascontiguousarray(v)
        if name in ("x", "ctx_1024"):
            v = v.reshape(B * T, D)
        name = name.replace("L0_attn_", "").replace("L0_", "")
        if name == "ffn_b1":
            name, v = "ffn_b1_cols", np.ascontiguousarray(v.reshape(NE, FT, P).transpose(2, 0, 1))
        arrays[name] = v
    arrays.update(constants())
    a, feed = {}, {}
    for name, v in arrays.items():
        feed[f"in_{name}"] = v
        a[name] = nc.dram_tensor(f"in_{name}", v.shape, mybir.dt.from_np(v.dtype), kind="ExternalInput").ap()
    out = nc.dram_tensor("out", (B * T, D), F32, kind="ExternalOutput").ap()
    program(nc, a, out)
    r = run_bass_kernel_spmd(nc, [feed], core_ids=[0])
    return r.results[0]["out"].reshape(B, T, D)
```

```python
from contextlib import ExitStack

import concourse.bass as bass
from concourse import mybir

P = 128
B, T, D = 4, 512, 256
NT = B * T // P
CB = T // P
H, HD = 8, 128
HW = H * HD
GH = 4
NG = H // GH
F = 1024
KD = D // P
FT = F // P
LEVELS = 6
NE = 8
TILES = NT + NE - 1
XW = D + 2
GATE, NUMBER = D, D + 1
NSC = 5
EPS = 1e-5

F32 = mybir.dt.float32
I32 = mybir.dt.int32
ALU = mybir.AluOpType
ACT = mybir.ActivationFunctionType
AX = mybir.AxisListType.X
ds = bass.ds


def tensors(nc, ctx, prefix):
    def sb(name, shape, dt=F32):
        return ctx.enter_context(nc.sbuf_tensor(prefix + name, shape, dt))

    def ps(name, shape):
        return ctx.enter_context(nc.psum_tensor(prefix + name, shape, F32))

    numbers = []

    def sem(name):
        s = ctx.enter_context(nc.semaphore(prefix + name))
        numbers.append(s.num)
        return s

    def clear():
        runs = []
        for n in sorted(numbers):
            if runs and runs[-1][1] == n:
                runs[-1][1] = n + 1
            else:
                runs.append([n, n + 1])
        with nc.Block() as block:
            @block.sync
            def _(sp):
                for lo, hi in runs:
                    sp.sem_clear(range(lo, hi))

    def start_block():
        ctx.callback(clear)
        return ctx.enter_context(nc.Block())

    return sb, ps, sem, start_block


def wait_apart(eng, sem, value, held):
    if not isinstance(value, int):
        value = eng.to_reg(value)
    eng.wait_ge(*held)
    eng.wait_ge(sem, value)


def project_stage(nc, a, ident, qkv_dram, scal_dram, grow_dram):
    with ExitStack() as ctx:
        sb, ps, sem, start_block = tensors(nc, ctx, "pj_")
        x_all = sb("x_all", [P, NT, D])
        w_qkv = sb("w_qkv", [P, KD, 3 * HW])
        w_gate = sb("w_gate", [P, KD, 2 * H])
        ln_w = sb("ln_w", [P, KD])
        ln_b = sb("ln_b", [P, KD])
        stats = sb("stats", [P, NT, 6])
        meanvar = sb("meanvar", [P, NT, 2])
        rstd = sb("rstd", [P, NT])
        shift = sb("shift", [P, NT])
        z = sb("z", [P, 2, D])
        n_t = sb("n_t", [P, 2, KD, P])
        sig = sb("sig", [P, 6, 512])
        act = sb("act", [P, 2, 3 * HW])
        sq = sb("sq", [P, 2 * HW])
        ss = sb("ss", [P, 2 * H])
        rn = sb("rn", [P, 2, 2 * H])
        half = sb("half", [P, 2 * H])
        gates = sb("gates", [P, NT, 2 * H])
        cumul = sb("cumul", [P, P])
        ones = sb("ones", [P, P])
        keep = sb("keep", [P, NT * H])
        beta = sb("beta", [P, NT * H])
        la = sb("la", [P, NT * H])
        tmp = sb("tmp", [P, NT * H])
        gsum = sb("gsum", [P, NT * H])
        gtot = sb("gtot", [P, NT * H])
        grow = sb("grow", [P, P])
        scal = sb("scal", [P, NT, NSC, H])
        ps_t = [ps(f"t{u}", [P, 512]) for u in range(2)]
        ps_p = [ps(f"p{j}", [P, 512]) for j in range(6)]

        x_loaded, w_loaded, g_loaded = sem("x_loaded"), sem("w_loaded"), sem("g_loaded")
        stats_done, ln_done = sem("stats_done"), sem("ln_done")
        z_ready, zt_done, nt_ready = sem("z_ready"), sem("zt_done"), sem("nt_ready")
        chunk_done, gate_done, gate_read = sem("chunk_done"), sem("gate_done"), sem("gate_read")
        sig_ready, act_ready = sem("sig_ready"), sem("act_ready")
        sq_ready, ss_ready, rn_ready, unit_ready = sem("sq_ready"), sem("ss_ready"), sem("rn_ready"), sem("unit_ready")
        stored = [sem(f"stored{u}") for u in range(2)]
        pow_ready, half_ready = sem("pow_ready"), sem("half_ready")
        const_ready, chain, la_ready = sem("const_ready"), sem("chain"), sem("la_ready")
        beta_ready, ex_ready, ln1p_ready = sem("beta_ready"), sem("ex_ready"), sem("ln1p_ready")
        sums_done, gsum_ready, grow_done, grow_ready = sem("sums_done"), sem("gsum_ready"), sem("grow_done"), sem("grow_ready")
        ediff_ready, eg_ready, scal_ready, out_stored = sem("ediff_ready"), sem("eg_ready"), sem("scal_ready"), sem("out_stored")
        block = start_block()

        @block.sync
        def _(sp):
            sp.dma_start(x_all[:], a["x"].rearrange("(n p) d -> p n d", p=P)).then_inc(x_loaded, 16)
            sp.dma_start(ln_w[:], a["ln1_w"].rearrange("(k p) -> p k", p=P),
                         allow_slow_non_contiguous=True).then_inc(w_loaded, 16)
            sp.dma_start(ln_b[:], a["ln1_b"].rearrange("(k p) -> p k", p=P),
                         allow_slow_non_contiguous=True).then_inc(w_loaded, 16)
            for j, w in enumerate(("Wq", "Wk", "Wv")):
                sp.dma_start(w_qkv[:, :, j * HW:(j + 1) * HW],
                             a[w].rearrange("(k p) m -> p k m", p=P)).then_inc(w_loaded, 16)
            sp.dma_start(w_gate[:, :, 0:H], a["Wb"].rearrange("(k p) m -> p k m", p=P)).then_inc(w_loaded, 16)
            sp.dma_start(w_gate[:, :, H:2 * H], a["Wa"].rearrange("(k p) m -> p k m", p=P)).then_inc(w_loaded, 16)
            sp.dma_start(cumul[:], a["mask_incl"]).then_inc(g_loaded, 16)
            sp.dma_start(keep[:], a["keep"]).then_inc(g_loaded, 16)
            with sp.Fori(0, NT // 2) as it:
                for u in range(2):
                    row = sp.snap(it * 2 * P + u * P)
                    sp.wait_ge(unit_ready, 2 * it + u + 1)
                    sp.dma_start(qkv_dram[ds(row, P), :], act[:, u, :]).then_inc(stored[u], 16)
            sp.wait_ge(grow_ready, 1)
            sp.dma_start(grow_dram, grow[:]).then_inc(out_stored, 16)
            sp.wait_ge(scal_ready, 1)
            sp.dma_start(scal_dram.rearrange("n p c -> p n c"), scal[:].rearrange("p n c h -> p n (c h)")).then_inc(out_stored, 16)
            for u in range(2):
                sp.wait_ge(stored[u], 16 * (NT // 2))
            sp.wait_ge(out_stored, 32)

        @block.vector
        def _(dve):
            dve.wait_ge(x_loaded, 16)
            for n in range(NT):
                nc.vector.bn_stats(stats[:, n, :], x_all[:, n, :]).then_inc(stats_done, 1)
            for n in range(NT):
                dve.wait_ge(stats_done, n + 1)
                nc.vector.bn_aggr(meanvar[:, n, :], stats[:, n, :]).then_inc(stats_done, 1)
            dve.wait_ge(stats_done, 2 * NT)
            dve.wait_ge(ln_done, 1)
            nc.vector.scalar_tensor_tensor(shift[:], meanvar[:, :, 0], -1.0, rstd[:], ALU.mult, ALU.mult).then_inc(ln_done, 1)
            nc.vector.memset(ones[:], 1.0).then_inc(const_ready, 1)
            dve.wait_ge(ln_done, 2)
            for u in range(2):
                nc.vector.tensor_scalar(z[:, u, :], x_all[:, u, :], rstd[:, u:u + 1], shift[:, u:u + 1],
                                        ALU.mult, ALU.add).then_inc(z_ready, 1)

            def tile(it, u, more):
                n = 2 * it + u
                if more:
                    dve.wait_ge(zt_done, n + 1)
                    nc.vector.tensor_scalar(z[:, u, :], x_all[:, ds(n + 2, 1), :].rearrange("p a d -> p (a d)"),
                                            rstd[:, ds(n + 2, 1)], shift[:, ds(n + 2, 1)],
                                            ALU.mult, ALU.add).then_inc(z_ready, 1)
                for j in range(6):
                    dve.wait_ge(sig_ready, 6 * n + j + 1)
                    if j == 0 and not (isinstance(it, int) and it == 0):
                        dve.wait_ge(stored[u], 16 * it)
                    nc.vector.tensor_tensor(act[:, u, j * 512:(j + 1) * 512], ps_p[j][:], sig[:, j, :],
                                            ALU.mult).then_inc(act_ready, 1)
                dve.wait_ge(gate_done, n + 1)
                nc.vector.tensor_scalar(gates[:, ds(n, 1), :].rearrange("p a c -> p (a c)"), ps_t[u][:, 256:256 + 2 * H],
                                        1.0, None, ALU.mult).then_inc(gate_read, 1)
                dve.wait_ge(sq_ready, n + 1)
                nc.vector.tensor_reduce(ss[:], sq[:].rearrange("p (h d) -> p h d", d=HD), AX, ALU.add).then_inc(ss_ready, 1)
                dve.wait_ge(ss_ready, n + 1)
                nc.vector.tensor_scalar(rn[:, u, :], ss[:], 1e-6, None, ALU.add).then_inc(rn_ready, 1)

            for u in range(2):
                tile(0, u, True)
            with dve.Fori(1, NT // 2 - 1) as it:
                for u in range(2):
                    tile(it, u, True)
            for u in range(2):
                tile(NT // 2 - 1, u, False)

            dve.wait_ge(gate_read, NT)
            nc.vector.scalar_tensor_tensor(tmp[:].rearrange("p (n h) -> p n h", h=H), gates[:, :, H:2 * H], -1.0,
                                           gates[:, :, H:2 * H], ALU.mult, ALU.max).then_inc(chain, 1)
            nc.vector.tensor_scalar(la[:].rearrange("p (n h) -> p n h", h=H), gates[:, :, H:2 * H], 0.0, None,
                                    ALU.min).then_inc(la_ready, 1)
            dve.wait_ge(ln1p_ready, 1)
            dve.wait_ge(la_ready, 1)
            nc.vector.tensor_tensor(la[:], la[:], tmp[:], ALU.subtract).then_inc(la_ready, 1)
            dve.wait_ge(sums_done, 1)
            nc.vector.tensor_copy(gsum[:], ps_p[0][:, 0:P]).then_inc(gsum_ready, 1)
            nc.vector.tensor_copy(gtot[:], ps_p[1][:, 0:P]).then_inc(gsum_ready, 1)
            dve.wait_ge(gsum_ready, 2)
            nc.vector.tensor_tensor(tmp[:], gtot[:], gsum[:], ALU.subtract).then_inc(ediff_ready, 1)
            dve.wait_ge(grow_done, 1)
            nc.vector.tensor_copy(grow[:], ps_p[2][:, 0:P]).then_inc(grow_ready, 1)

            def col(c):
                return scal[:, :, c, :]

            def nh(t):
                return t[:].rearrange("p (n h) -> p n h", h=H)

            dve.wait_ge(beta_ready, 1)
            dve.wait_ge(g_loaded, 32)
            nc.vector.tensor_scalar(col(0), nh(beta), 1.0, None, ALU.mult).then_inc(chain, 1)
            nc.vector.tensor_scalar(col(1), nh(beta), -1.0, None, ALU.mult).then_inc(chain, 1)
            nc.vector.tensor_scalar(col(2), nh(gsum), 1.0, None, ALU.mult).then_inc(chain, 1)
            dve.wait_ge(eg_ready, 2)
            nc.vector.tensor_tensor(col(3), nh(gtot), nh(keep), ALU.mult).then_inc(chain, 1)
            nc.vector.tensor_tensor(col(4), nh(tmp), nh(keep), ALU.mult).then_inc(chain, 1)
            dve.wait_ge(chain, 6)
            nc.vector.nop().then_inc(scal_ready, 1)

        @block.gpsimd
        def _(pool):
            nc.gpsimd.memset(half[:], -0.5).then_inc(half_ready, 1)
            pool.wait_ge(half_ready, 1)
            pool.wait_ge(stats_done, 2 * NT)
            nc.gpsimd.tensor_scalar(rstd[:], meanvar[:, :, 1], EPS, None, ALU.add).then_inc(half_ready, 1)
            pool.wait_ge(half_ready, 2)
            nc.gpsimd.tensor_tensor(rstd[:], rstd[:], half[:, 0:NT], ALU.pow).then_inc(ln_done, 1)
            with pool.Fori(0, NT // 2) as it:
                for u in range(2):
                    n = 2 * it + u
                    qk = act[:, u, 0:2 * HW]
                    pool.wait_ge(rn_ready, n + 1)
                    nc.gpsimd.tensor_tensor(rn[:, u, :], rn[:, u, :], half[:], ALU.pow).then_inc(pow_ready, 1)
                    pool.wait_ge(pow_ready, n + 1)
                    nc.gpsimd.tensor_tensor(qk.rearrange("p (h d) -> p h d", d=HD),
                                            qk.rearrange("p (h d) -> p h d", d=HD),
                                            rn[:, u, :].unsqueeze(2).broadcast_to([P, 2 * H, HD]),
                                            ALU.mult).then_inc(unit_ready, 1)

        @block.scalar
        def _(act_e):
            act_e.wait_ge(w_loaded, 16 * 7)

            def normed(n, u):
                act_e.wait_ge(zt_done, n + 1)
                for k in range(KD):
                    nc.scalar.activation(n_t[:, u, k, :], ps_t[u][:, k * P:(k + 1) * P], ACT.Identity,
                                         bias=ln_b[:, k:k + 1], scale=ln_w[:, k:k + 1]).then_inc(nt_ready, 1)

            def sigmoids(n, u, first=False, last=False):
                for j in range(6):
                    if j == 3 and not last:
                        normed(n + 1, 1 - u)
                    act_e.wait_ge(chunk_done, 6 * n + j + 1)
                    nc.scalar.activation(sig[:, j, :], ps_p[j][:], ACT.Sigmoid).then_inc(sig_ready, 1)
                act_e.wait_ge(act_ready, 6 * n + 4)
                if not first:
                    act_e.wait_ge(ss_ready, n)
                nc.scalar.activation(sq[:], act[:, u, 0:2 * HW], ACT.Square).then_inc(sq_ready, 1)

            normed(0, 0)
            sigmoids(0, 0, first=True)
            sigmoids(1, 1)
            with act_e.Fori(1, NT // 2 - 1) as it:
                sigmoids(2 * it, 0)
                sigmoids(2 * it + 1, 1)
            sigmoids(NT - 2, 0)
            sigmoids(NT - 1, 1, last=True)
            act_e.wait_ge(gate_read, NT)
            nc.scalar.activation(beta[:].rearrange("p (n h) -> p n h", h=H), gates[:, :, 0:H],
                                 ACT.Sigmoid).then_inc(beta_ready, 1)
            act_e.wait_ge(chain, 1)
            nc.scalar.activation(tmp[:], tmp[:], ACT.Exp, scale=-1.0).then_inc(ex_ready, 1)
            act_e.wait_ge(ex_ready, 1)
            nc.scalar.activation(tmp[:], tmp[:], ACT.Ln, bias=1.0).then_inc(ln1p_ready, 1)
            act_e.wait_ge(ediff_ready, 1)
            nc.scalar.activation(gtot[:], gtot[:], ACT.Exp).then_inc(eg_ready, 1)
            nc.scalar.activation(tmp[:], tmp[:], ACT.Exp).then_inc(eg_ready, 1)

        @block.tensor
        def _(pe):
            pe.wait_ge(w_loaded, 16 * 7)

            def transposes(n, u):
                pe.wait_ge(z_ready, n + 1)
                for k in range(KD):
                    last = nc.tensor.transpose(ps_t[u][:, k * P:(k + 1) * P], z[:, u, k * P:(k + 1) * P], ident[:])
                last.then_inc(zt_done, 1)

            def products(it, u, first, between):
                n = 2 * it + u
                for j in range(6):
                    if j == 3:
                        between()
                    if j == 0:
                        pe.wait_ge(nt_ready, 2 * n + 2)
                    if not first:
                        pe.wait_ge(act_ready, 6 * n - 6 + j + 1)
                    for k in range(KD):
                        last = nc.tensor.matmul(ps_p[j][:], n_t[:, u, k, :], w_qkv[:, k, j * 512:(j + 1) * 512],
                                                start=(k == 0), stop=(k == KD - 1))
                    last.then_inc(chunk_done, 1)
                for k in range(KD):
                    last = nc.tensor.matmul(ps_t[u][:, 256:256 + 2 * H], n_t[:, u, k, :], w_gate[:, k, :],
                                            start=(k == 0), stop=(k == KD - 1))
                last.then_inc(gate_done, 1)

            def tile(it, u, first=False, last=False):
                n = 2 * it + u

                def next_transposes():
                    if not last:
                        if not first:
                            pe.wait_ge(gate_read, n)
                        transposes(n + 1, 1 - u)

                products(it, u, first, next_transposes)

            transposes(0, 0)
            tile(0, 0, first=True)
            tile(0, 1)
            with pe.Fori(1, NT // 2 - 1) as it:
                for u in range(2):
                    tile(it, u)
            tile(NT // 2 - 1, 0)
            tile(NT // 2 - 1, 1, last=True)
            pe.wait_ge(la_ready, 2)
            pe.wait_ge(g_loaded, 32)
            pe.wait_ge(const_ready, 1)
            nc.tensor.matmul(ps_p[0][:, 0:P], cumul[:], la[:], start=True, stop=True)
            nc.tensor.matmul(ps_p[1][:, 0:P], ones[:], la[:], start=True, stop=True).then_inc(sums_done, 1)
            pe.wait_ge(gsum_ready, 2)
            nc.tensor.transpose(ps_p[2][:, 0:P], gsum[:], ident[:]).then_inc(grow_done, 1)


def delta_stage(nc, a, ident, qkv_dram, scal_dram, grow_dram, o_dram):
    with ExitStack() as ctx:
        sb, ps, sem, start_block = tensors(nc, ctx, "dl_")
        qkv = [sb(f"qkv{u}", [P, 3, H, HD]) for u in range(2)]
        gb = [sb(f"gb{u}", [P, H, P]) for u in range(2)]
        sc = [sb(f"sc{u}", [P, NSC, H]) for u in range(2)]
        BETA, NBETA, GSUM, GEND, WDECAY = range(NSC)
        masks = sb("masks", [P, LEVELS, P])
        mask_incl = sb("mask_incl", [P, P])
        mask_strict = sb("mask_strict", [P, P])
        mask_one = sb("mask_one", [P, P])
        zero = sb("zero", [P, 2])

        def pair(name, slots=2):
            return [[sb(f"{name}{u}{g}", [P, GH, P]) for g in range(NG)] for u in range(slots)]

        k_t, q_t, kg_t, qg_t = pair("k_t"), pair("q_t", 1) * 2, pair("kg_t"), pair("qg_t")
        n_mat_t, attn_t, tinv, tinv_t = pair("n_mat_t"), pair("attn_t"), pair("tinv"), pair("tinv_t")
        k_t = pair("k_tt", 1) * 2
        eg, edec, eb = pair("eg", 1)[0], pair("edec", 1)[0], pair("eb", 1)[0]
        ymat, rhs, w, w2, sdec, state = (pair(s, 1)[0] for s in ("ymat", "rhs", "w", "w2", "sdec", "state"))
        o_sb = pair("o_sb", 1)[0]
        bank = [ps(f"m{i}", [P, GH, P]) for i in range(4)]
        xb = [ps(f"x{g}", [P, GH, P]) for g in range(NG)]
        tb = [ps(f"t{g}", [P, GH, P]) for g in range(NG)]

        loaded = [sem(f"loaded{u}") for u in range(2)]
        const_loaded, state_zero = sem("const_loaded"), sem("state_zero")
        kt_done, qt_done, kk_done, kq_done, tinv2_done = (sem(s) for s in ("kt_done", "qt_done", "kk_done", "kq_done", "tinv2_done"))
        x_done, t_done, tt_done = sem("x_done"), sem("t_done"), sem("tt_done")
        ks_done, y_done, o_done, kw_done = sem("ks_done"), sem("y_done"), sem("o_done"), sem("kw_done")
        eg_ready, edec_ready, kt_copied, qt_copied, tinv2_copied = (
            sem(s) for s in ("eg_ready", "edec_ready", "kt_copied", "qt_copied", "tinv2_copied"))
        t_copied, tt_copied, o_copied = sem("t_copied"), sem("tt_copied"), sem("o_copied")
        kg_ready, qg_ready, diff_ready, a_ready, attn_ready, tinv2t_ready = (
            sem(s) for s in ("kg_ready", "qg_ready", "diff_ready", "a_ready", "attn_ready", "tinv2t_ready"))
        ymat_ready, r_ready, w_ready, s_ready = sem("ymat_ready"), sem("r_ready"), sem("w_ready"), sem("s_ready")
        nbm_ready, eb_ready, n_ready, incl_ready = sem("nbm_ready"), sem("eb_ready"), sem("n_ready"), sem("incl_ready")
        w2_ready, sdec_ready, o_stored = sem("w2_ready"), sem("sdec_ready"), sem("o_stored")
        block = start_block()

        def per_head(t, c, g):
            return t[:, c, g * GH:(g + 1) * GH].unsqueeze(2).broadcast_to([P, GH, P])

        def per_group(m):
            return m.unsqueeze(1).broadcast_to([P, GH, P])

        def schedule(eng, prep, invert, update):
            def step(n, u, first, last):
                invert(n, u, lambda part: None if first else update(n - 1, 1 - u, part),
                       lambda part: None if last else prep(n + 1, 1 - u, part))

            for part in range(3):
                prep(0, 0, part)
            step(0, 0, True, False)
            step(1, 1, False, False)
            with eng.Fori(1, NT // 2 - 1) as j:
                step(2 * j, 0, False, False)
                step(2 * j + 1, 1, False, False)
            step(NT - 2, 0, False, False)
            step(NT - 1, 1, False, True)
            for part in range(3):
                update(NT - 1, 1, part)

        def static(n):
            return isinstance(n, int)

        @block.sync
        def _(sp):
            sp.dma_start(masks[:], a["mask_levels"]).then_inc(const_loaded, 16)
            sp.dma_start(mask_incl[:], a["mask_incl"]).then_inc(const_loaded, 16)
            sp.dma_start(mask_strict[:], a["mask_strict"]).then_inc(const_loaded, 16)
            sp.dma_start(mask_one[:], a["mask_one"]).then_inc(const_loaded, 16)

            def load(n, u, reuse):
                row = sp.snap(n * P) if reuse and not static(n) else n * P
                if reuse:
                    sp.wait_ge(r_ready, 2 * n - 2)
                    sp.wait_ge(kw_done, 2 * n - 2)
                sp.dma_start(qkv[u][:], qkv_dram[ds(row, P), :].rearrange("p (c h d) -> p c h d", c=3, h=H)).then_inc(loaded[u], 16)
                sp.dma_start(gb[u][:], grow_dram[ds(n * H, H), :].partition_broadcast(P)).then_inc(loaded[u], 16)
                sp.dma_start(sc[u][:], scal_dram[ds(n, 1), :, :].rearrange("n p (c h) -> (n p) c h", c=NSC)).then_inc(loaded[u], 16)

            def store(n):
                row = n * P if static(n) else sp.snap(n * P)
                for g in range(NG):
                    sp.wait_ge(o_copied, 2 * n + g + 1)
                    sp.dma_start(o_dram[ds(row, P), g * GH * HD:(g + 1) * GH * HD].rearrange("p (h d) -> p h d", h=GH),
                                 o_sb[g][:]).then_inc(o_stored, 16)

            load(0, 0, False)
            load(1, 1, False)
            store(0)
            load(2, 0, True)
            with sp.Fori(1, NT // 2 - 1) as j:
                store(2 * j - 1)
                load(2 * j + 1, 1, True)
                store(2 * j)
                load(2 * j + 2, 0, True)
            store(NT - 3)
            load(NT - 1, 1, True)
            store(NT - 2)
            store(NT - 1)
            sp.wait_ge(o_stored, 32 * NT)

        @block.tensor
        def _(pe):
            def four(out, lhs, rhs_, **flags):
                for h in range(GH):
                    last = nc.tensor.matmul(out[:, h, :], lhs(h), rhs_(h), start=flags.get("start", True),
                                            stop=flags.get("stop", True), skip_group_check=True)
                return last

            def four_transposed(out, src):
                for h in range(GH):
                    last = nc.tensor.transpose(out[:, h, :], src[:, h, :], ident[:])
                return last

            def prep(n, u, part):
                if part == 0:
                    pe.wait_ge(loaded[u], 48 * (n // 2 + 1) if static(n) else 24 * n + (48 if u == 0 else 24))
                    for g in range(NG):
                        k_bank, q_bank = bank[2 * g], bank[2 * g + 1]
                        if not (static(n) and n < 2):
                            if g == 0:
                                pe.wait_ge(o_copied, 2 * n - 2)
                            else:
                                pe.wait_ge(s_ready, 2 * n - 2)
                        elif n == 1:
                            pe.wait_ge(attn_ready, g + 1)
                        four_transposed(k_bank, qkv[u][:, 1, g * GH:(g + 1) * GH, :]).then_inc(kt_done, 1)
                        four_transposed(q_bank, qkv[u][:, 0, g * GH:(g + 1) * GH, :]).then_inc(qt_done, 1)
                elif part == 1:
                    for g in range(NG):
                        kk, kq = bank[2 * g], bank[2 * g + 1]
                        pe.wait_ge(kt_copied, 2 * n + g + 1)
                        four(kk, lambda h: k_t[u][g][:, h, :], lambda h: k_t[u][g][:, h, :]).then_inc(kk_done, 1)
                        pe.wait_ge(qt_copied, 2 * n + g + 1)
                        four(kq, lambda h: k_t[u][g][:, h, :], lambda h: q_t[u][g][:, h, :]).then_inc(kq_done, 1)
                else:
                    for g in range(NG):
                        pe.wait_ge(tinv2t_ready, 2 * n + g + 1)
                        four_transposed(bank[2 * g], tinv_t[u][g]).then_inc(tinv2_done, 1)

            def invert(n, u, update_, prep_):
                for lev in range(LEVELS):
                    for g in range(NG):
                        if lev == 0:
                            pe.wait_ge(tinv2_copied, 2 * n + g + 1)
                            pe.wait_ge(n_ready, 2 * n + g + 1)
                        else:
                            pe.wait_ge(t_copied, 10 * n + 2 * (lev - 1) + g + 1)
                            four_transposed(tb[g], tinv[u][g]).then_inc(tt_done, 1)
                        four(xb[g], lambda h: n_mat_t[u][g][:, h, :], lambda h: tinv[u][g][:, h, :]).then_inc(x_done, 1)
                    if lev < 3:
                        update_(lev)
                    else:
                        prep_(lev - 3)
                    for g in range(NG):
                        pe.wait_ge(ymat_ready, 12 * n + 2 * lev + g + 1)
                        if not (static(n) and n == 0 and lev == 0):
                            pe.wait_ge(tt_copied, 12 * n + 2 * (lev - 1) + g + 1)
                        if lev < LEVELS - 1:
                            four(tb[g], lambda h: tinv_t[u][g][:, h, :], lambda h: ymat[g][:, h, :]).then_inc(t_done, 1)
                        else:
                            four(tb[g], lambda h: ymat[g][:, h, :], lambda h: tinv_t[u][g][:, h, :]).then_inc(tt_done, 1)

            def update(n, u, part):
                for g in range(NG):
                    if part == 0:
                        if not (static(n) and n == NT - 1):
                            if g == 0:
                                pe.wait_ge(tinv2_copied, 2 * n + 3)
                            else:
                                pe.wait_ge(attn_ready, 2 * n + 3)
                        if static(n) and n == 0:
                            pe.wait_ge(state_zero, 2)
                        else:
                            pe.wait_ge(s_ready, 2 * n - 1 + g)
                        pe.wait_ge(kg_ready, 2 * n + g + 1)
                        four(bank[g], lambda h: kg_t[u][g][:, h, :], lambda h: state[g][:, h, :]).then_inc(ks_done, 1)
                    elif part == 1:
                        pe.wait_ge(r_ready, 2 * n + g + 1)
                        pe.wait_ge(tt_copied, 12 * n + 11 + g)
                        if not (static(n) and n == NT - 1):
                            if g == 0:
                                pe.wait_ge(tinv2_copied, 2 * n + 4)
                            else:
                                pe.wait_ge(attn_ready, 2 * n + 4)
                        four(bank[2 + g], lambda h: tinv_t[u][g][:, h, :], lambda h: rhs[g][:, h, :]).then_inc(y_done, 1)
                    else:
                        pe.wait_ge(w_ready, 2 * n + g + 1)
                        pe.wait_ge(incl_ready, 2 * n + g + 1)
                        pe.wait_ge(qg_ready, 2 * n + g + 1)
                        for h in range(GH):
                            nc.tensor.matmul(bank[g][:, h, :], qg_t[u][g][:, h, :], state[g][:, h, :],
                                             start=True, stop=False, skip_group_check=True)
                            last = nc.tensor.matmul(bank[g][:, h, :], attn_t[u][g][:, h, :], w[g][:, h, :],
                                                    start=False, stop=True, skip_group_check=True)
                        last.then_inc(o_done, 1)
                if part == 2:
                    for g in range(NG):
                        pe.wait_ge(w2_ready, 2 * n + g + 1)
                        four(bank[2 + g], lambda h: qkv[u][:, 1, g * GH + h, :],
                             lambda h: w2[g][:, h, :]).then_inc(kw_done, 1)

            pe.wait_ge(const_loaded, 64)
            schedule(pe, prep, invert, update)

        @block.scalar
        def _(act):
            def prep(n, u, part):
                if part == 0:
                    act.wait_ge(loaded[u], 48 * (n // 2 + 1) if static(n) else 24 * n + (48 if u == 0 else 24))
                    for g in range(NG):
                        heads = slice(g * GH, (g + 1) * GH)
                        if not (static(n) and n == 0):
                            act.wait_ge(qg_ready, 2 * n - 1 + g)
                        nc.scalar.activation(eg[g][:], gb[u][:, heads, :], ACT.Exp).then_inc(eg_ready, 1)
                    for g in range(NG):
                        act.wait_ge(kt_done, 2 * n + g + 1)
                        nc.scalar.activation(k_t[u][g][:], bank[2 * g][:], ACT.Copy).then_inc(kt_copied, 1)
                        act.wait_ge(qt_done, 2 * n + g + 1)
                        nc.scalar.activation(q_t[u][g][:], bank[2 * g + 1][:], ACT.Copy).then_inc(qt_copied, 1)
                        act.wait_ge(diff_ready, 8 * n + 4 * g + 4)
                        nc.scalar.activation(edec[g][:], edec[g][:], ACT.Exp).then_inc(edec_ready, 1)
                elif part == 2:
                    for g in range(NG):
                        act.wait_ge(tinv2_done, 2 * n + g + 1)
                        nc.scalar.activation(tinv[u][g][:], bank[2 * g][:], ACT.Copy).then_inc(tinv2_copied, 1)

            def invert(n, u, update_, prep_):
                for lev in range(LEVELS):
                    if lev < 3:
                        update_(lev)
                    else:
                        prep_(lev - 3)
                    if lev < LEVELS - 1:
                        for g in range(NG):
                            act.wait_ge(t_done, 10 * n + 2 * lev + g + 1)
                            nc.scalar.activation(tinv[u][g][:], tb[g][:], ACT.Copy).then_inc(t_copied, 1)
                    for g in range(NG):
                        act.wait_ge(tt_done, 12 * n + 2 * lev + g + 1)
                        nc.scalar.activation(tinv_t[u][g][:], tb[g][:], ACT.Copy).then_inc(tt_copied, 1)

            def update(n, u, part):
                if part != 2:
                    return
                for g in range(NG):
                    if not (static(n) and n == 0):
                        act.wait_ge(o_stored, 32 * n)
                    act.wait_ge(o_done, 2 * n + g + 1)
                    nc.scalar.activation(o_sb[g][:], bank[g][:], ACT.Copy).then_inc(o_copied, 1)

            schedule(act, prep, invert, update)

        @block.vector
        def _(dve):
            for g in range(NG):
                nc.vector.memset(state[g][:], 0.0).then_inc(state_zero, 1)

            def prep(n, u, part):
                if part == 0:
                    dve.wait_ge(loaded[u], 48 * (n // 2 + 1) if static(n) else 24 * n + (48 if u == 0 else 24))
                    for g in range(NG):
                        if not (static(n) and n == 0):
                            dve.wait_ge(eb_ready, 2 * n - 1 + g)
                            dve.wait_ge(attn_ready, 2 * n - 1 + g)
                        for h in range(GH):
                            hh = g * GH + h
                            nc.vector.tensor_scalar(edec[g][:, h, :], gb[u][:, hh, :], sc[u][:, GSUM, hh:hh + 1], 0.0,
                                                    ALU.subtract, ALU.min).then_inc(diff_ready, 1)
                    for g in range(NG):
                        dve.wait_ge(eg_ready, 2 * n + g + 1)
                        dve.wait_ge(kt_copied, 2 * n + g + 1)
                        nc.vector.tensor_tensor(kg_t[u][g][:], k_t[u][g][:], eg[g][:], ALU.mult).then_inc(kg_ready, 1)
                        dve.wait_ge(qt_copied, 2 * n + g + 1)
                        nc.vector.tensor_tensor(qg_t[u][g][:], q_t[u][g][:], eg[g][:], ALU.mult).then_inc(qg_ready, 1)
                elif part == 1:
                    for g in range(NG):
                        dve.wait_ge(kk_done, 2 * n + g + 1)
                        dve.wait_ge(eb_ready, 2 * n + g + 1)
                        nc.vector.tensor_tensor(n_mat_t[u][g][:], bank[2 * g][:], eb[g][:], ALU.mult).then_inc(a_ready, 1)
                        dve.wait_ge(kq_done, 2 * n + g + 1)
                        nc.vector.tensor_tensor(attn_t[u][g][:], bank[2 * g + 1][:], edec[g][:], ALU.mult).then_inc(attn_ready, 1)
                    for g in range(NG):
                        dve.wait_ge(n_ready, 2 * n + g + 1)
                        nc.vector.tensor_tensor(tinv_t[u][g][:], n_mat_t[u][g][:], per_group(mask_one[:]),
                                                ALU.mult).then_inc(tinv2t_ready, 1)

            def invert(n, u, update_, prep_):
                for lev in range(LEVELS):
                    for g in range(NG):
                        dve.wait_ge(x_done, 12 * n + 2 * lev + g + 1)
                        nc.vector.tensor_tensor(ymat[g][:], xb[g][:], per_group(masks[:, lev, :]),
                                                ALU.mult).then_inc(ymat_ready, 1)
                    if lev < 3:
                        update_(lev)
                    else:
                        prep_(lev - 3)

            def update(n, u, part):
                for g in range(NG):
                    if part == 0:
                        dve.wait_ge(ks_done, 2 * n + g + 1)
                        nc.vector.tensor_tensor(rhs[g][:], qkv[u][:, 2, g * GH:(g + 1) * GH, :], bank[g][:],
                                                ALU.subtract).then_inc(r_ready, 1)
                    elif part == 1:
                        dve.wait_ge(y_done, 2 * n + g + 1)
                        nc.vector.tensor_tensor(w[g][:], bank[2 + g][:], per_head(sc[u], BETA, g), ALU.mult).then_inc(w_ready, 1)
                    else:
                        dve.wait_ge(kw_done, 2 * n + g + 1)
                        dve.wait_ge(sdec_ready, 2 * n + g + 1)
                        nc.vector.tensor_tensor(state[g][:], sdec[g][:], bank[2 + g][:], ALU.add).then_inc(s_ready, 1)

            dve.wait_ge(const_loaded, 64)
            schedule(dve, prep, invert, update)

        @block.gpsimd
        def _(pool):
            pool.wait_ge(const_loaded, 64)

            def prep(n, u, part):
                if part == 0:
                    for g in range(NG):
                        pool.wait_ge(loaded[u], 48 * (n // 2 + 1) if static(n) else 24 * n + (48 if u == 0 else 24))
                        if not (static(n) and n == 0):
                            pool.wait_ge(a_ready, 2 * n - 1 + g)
                        nc.gpsimd.tensor_tensor(eb[g][:], per_group(mask_strict[:]), per_head(sc[u], NBETA, g),
                                                ALU.mult).then_inc(nbm_ready, 1)
                elif part == 1:
                    for g in range(NG):
                        pool.wait_ge(edec_ready, 2 * n + g + 1)
                        pool.wait_ge(nbm_ready, 2 * n + g + 1)
                        nc.gpsimd.tensor_tensor(eb[g][:], eb[g][:], edec[g][:], ALU.mult).then_inc(eb_ready, 1)
                    for g in range(NG):
                        pool.wait_ge(a_ready, 2 * n + g + 1)
                        nc.gpsimd.tensor_tensor(n_mat_t[u][g][:], n_mat_t[u][g][:], per_group(ident[:]),
                                                ALU.add).then_inc(n_ready, 1)
                else:
                    for g in range(NG):
                        pool.wait_ge(attn_ready, 2 * n + g + 1)
                        nc.gpsimd.tensor_tensor(attn_t[u][g][:], attn_t[u][g][:], per_group(mask_incl[:]),
                                                ALU.mult).then_inc(incl_ready, 1)

            def invert(n, u, update_, prep_):
                for part in range(3):
                    update_(part)
                for part in range(3):
                    prep_(part)

            def update(n, u, part):
                for g in range(NG):
                    if part == 0:
                        if static(n) and n == 0:
                            pool.wait_ge(state_zero, 2)
                        else:
                            pool.wait_ge(s_ready, 2 * n - 1 + g)
                        nc.gpsimd.tensor_tensor(sdec[g][:], state[g][:], per_head(sc[u], GEND, g), ALU.mult).then_inc(sdec_ready, 1)
                    elif part == 1:
                        pool.wait_ge(w_ready, 2 * n + g + 1)
                        nc.gpsimd.tensor_tensor(w2[g][:], w[g][:], per_head(sc[u], WDECAY, g), ALU.mult).then_inc(w2_ready, 1)

            schedule(pool, prep, invert, update)


def ffn_stage(nc, a, ident, o_dram, x_rows):
    x1_all = x_rows[:, :, 0:D]
    with ExitStack() as ctx:
        sb, ps, sem, start_block = tensors(nc, ctx, "ff_")
        x_all = sb("x_all", [P, NT, D])
        xb_all = sb("xb_all", [P, NT, D])
        wo = sb("wo", [P, H, D])
        w1 = sb("w1", [P, KD, F])
        w2 = sb("w2", [P, FT, D])
        b1 = sb("b1", [P, FT])
        b2 = sb("b2", [P, D])
        ln_w, ln_b = sb("ln_w", [P, KD]), sb("ln_b", [P, KD])
        half = sb("half", [P, 1])
        o_in = [sb(f"o_in{u}", [P, H, HD]) for u in range(2)]
        o_t = sb("o_t", [P, H, P])
        x1 = sb("x1", [P, D])
        z = sb("z", [P, D])
        h_t = sb("h_t", [P, KD, P])
        g_t = sb("g_t", [P, FT, P])
        base = [sb(f"base{u}", [P, D]) for u in range(2)]
        total = sb("total", [P, D])
        stats = [sb(f"stats{c}", [P, 6]) for c in range(2)]
        mv = [sb(f"mv{c}", [P, 2]) for c in range(2)]
        var = [sb(f"var{c}", [P, 1]) for c in range(2)]
        rstd = [sb(f"rstd{c}", [P, 1]) for c in range(2)]
        shift = [sb(f"shift{c}", [P, 1]) for c in range(2)]
        ps_ot = [ps(f"ot{i}", [P, 4, P]) for i in range(2)]
        ps_at = ps("at", [P, D])
        ps_z = ps("z_ps", [P, KD, P])
        ps_f1 = [ps(f"f1{i}", [P, 4, P]) for i in range(2)]
        ps_f2 = ps("f2", [P, D])

        w_loaded, half_ready, xb_ready = sem("w_loaded"), sem("half_ready"), sem("xb_ready")
        o_loaded = [sem(f"o_loaded{u}") for u in range(2)]
        ot_done, ot_copied, attn_done, x1_ready = sem("ot_done"), sem("ot_copied"), sem("attn_done"), sem("x1_ready")
        z_ready, zt_done, ht_ready = sem("z_ready"), sem("zt_done"), sem("ht_ready")
        f1_done, gelu_ready, f2_done, total_ready = sem("f1_done"), sem("gelu_ready"), sem("f2_done"), sem("total_ready")
        base_ready, out_ready = sem("base_ready"), sem("out_ready")
        stats_ready = [sem(f"stats_ready{c}") for c in range(2)]
        mv_ready = [sem(f"mv_ready{c}") for c in range(2)]
        var_ready = [sem(f"var_ready{c}") for c in range(2)]
        rstd_ready = [sem(f"rstd_ready{c}") for c in range(2)]
        shift_ready = [sem(f"shift_ready{c}") for c in range(2)]
        block = start_block()
        LOADS = 8

        def schedule(eng, prologue, step):
            prologue()
            step(0, 0)
            step(1, 1)
            with eng.Fori(1, NT // 2 - 1) as j:
                step(2 * j, 0)
                step(2 * j + 1, 1)
            step(NT - 2, 0)
            step(NT - 1, 1)

        def has(n, k):
            return not isinstance(n, int) or n + k < NT

        @block.sync
        def _(sp):
            sp.dma_start(wo[:], a["Wo"].rearrange("(h p) m -> p h m", p=P)).then_inc(w_loaded, 16)
            sp.dma_start(x_all[:], a["x"].rearrange("(n p) d -> p n d", p=P)).then_inc(w_loaded, 16)
            sp.dma_start(b2[:], a["b2"].rearrange("(o d) -> o d", o=1).broadcast_to([P, D])).then_inc(w_loaded, 16)
            sp.dma_start(ln_w[:], a["ln2_w"].rearrange("(k p) -> p k", p=P),
                         allow_slow_non_contiguous=True).then_inc(w_loaded, 16)
            sp.dma_start(ln_b[:], a["ln2_b"].rearrange("(k p) -> p k", p=P),
                         allow_slow_non_contiguous=True).then_inc(w_loaded, 16)
            sp.dma_start(b1[:], a["b1"].rearrange("(f p) -> p f", p=P),
                         allow_slow_non_contiguous=True).then_inc(w_loaded, 16)

            def load(n, u):
                row = n * P if isinstance(n, int) else sp.snap(n * P)
                if not (isinstance(n, int) and n < 2):
                    sp.wait_ge(ot_done, 2 * n - 2)
                sp.dma_start(o_in[u][:], o_dram[ds(row, P), :].rearrange("p (h d) -> p h d", h=H)).then_inc(o_loaded[u], 16)

            load(0, 0)
            load(1, 1)
            sp.dma_start(w1[:], a["W1"].rearrange("(k p) m -> p k m", p=P)).then_inc(w_loaded, 16)
            sp.dma_start(w2[:], a["W2"].rearrange("(f p) m -> p f m", p=P)).then_inc(w_loaded, 16)
            with sp.Fori(1, NT // 2) as j:
                load(2 * j, 0)
                load(2 * j + 1, 1)

        @block.tensor
        def _(pe):
            def o_transposes(n, u):
                pe.wait_ge(o_loaded[u], 16 * (n // 2 + 1) if isinstance(n, int) else 8 * n + (16 if u == 0 else 8))
                if not (isinstance(n, int) and n == 0):
                    pe.wait_ge(ot_copied, 2 * n)
                for h in range(H):
                    last = nc.tensor.transpose(ps_ot[h // 4][:, h % 4, :], o_in[u][:, h, :], ident[:])
                    if h % 4 == 3:
                        last.then_inc(ot_done, 1)

            def attn(n):
                pe.wait_ge(ot_copied, 2 * n + 2)
                if not (isinstance(n, int) and n == 0):
                    pe.wait_ge(x1_ready, n)
                for h in range(H):
                    last = nc.tensor.matmul(ps_at[:], o_t[:, h, :], wo[:, h, :], start=(h == 0), stop=(h == H - 1))
                last.then_inc(attn_done, 1)

            def z_transposes(n):
                pe.wait_ge(z_ready, n + 1)
                if not (isinstance(n, int) and n == 0):
                    pe.wait_ge(ht_ready, 2 * n)
                for k in range(KD):
                    last = nc.tensor.transpose(ps_z[:, k, :], z[:, k * P:(k + 1) * P], ident[:])
                last.then_inc(zt_done, 1)

            def ffn1(n):
                pe.wait_ge(ht_ready, 2 * n + 2)
                for f in range(FT):
                    if f % 4 == 0 and not (isinstance(n, int) and n == 0):
                        pe.wait_ge(gelu_ready, 8 * n - 4 + f)
                    for k in range(KD):
                        last = nc.tensor.matmul(ps_f1[f // 4][:, f % 4, :], w1[:, k, f * P:(f + 1) * P], h_t[:, k, :],
                                                start=(k == 0), stop=(k == KD - 1), skip_group_check=True)
                    if f % 4 == 3:
                        last.then_inc(f1_done, 1)

            def ffn2(n):
                pe.wait_ge(gelu_ready, 8 * n + 8)
                if not (isinstance(n, int) and n == 0):
                    pe.wait_ge(total_ready, n)
                for f in range(FT):
                    last = nc.tensor.matmul(ps_f2[:], g_t[:, f, :], w2[:, f, :], start=(f == 0), stop=(f == FT - 1))
                last.then_inc(f2_done, 1)

            def prologue():
                pe.wait_ge(w_loaded, 16 * LOADS)
                o_transposes(0, 0)
                attn(0)
                o_transposes(1, 1)
                z_transposes(0)

            def step(n, u):
                ffn1(n)
                if has(n, 1):
                    attn(n + 1)
                ffn2(n)
                if has(n, 1):
                    z_transposes(n + 1)
                if has(n, 2):
                    o_transposes(n + 2, u)

            schedule(pe, prologue, step)

        @block.scalar
        def _(act):
            def o_copies(n):
                for i in range(2):
                    act.wait_ge(ot_done, 2 * n + i + 1)
                    nc.scalar.activation(o_t[:, 4 * i:4 * i + 4, :], ps_ot[i][:], ACT.Copy).then_inc(ot_copied, 1)

            def h_copies(n):
                act.wait_ge(zt_done, n + 1)
                for k in range(KD):
                    nc.scalar.activation(h_t[:, k, :], ps_z[:, k, :], ACT.Identity,
                                         bias=ln_b[:, k:k + 1], scale=ln_w[:, k:k + 1]).then_inc(ht_ready, 1)

            def gelus(n):
                for f in range(FT):
                    if f % 4 == 0:
                        act.wait_ge(f1_done, 2 * n + f // 4 + 1)
                    nc.scalar.activation(g_t[:, f, :], ps_f1[f // 4][:, f % 4, :], ACT.Gelu,
                                         bias=b1[:, f:f + 1]).then_inc(gelu_ready, 1)

            def prologue():
                act.wait_ge(w_loaded, 16 * LOADS)
                o_copies(0)
                o_copies(1)
                h_copies(0)

            def step(n, u):
                gelus(n)
                if has(n, 1):
                    h_copies(n + 1)
                if has(n, 2):
                    o_copies(n + 2)

            schedule(act, prologue, step)

        @block.vector
        def _(dve):
            def moments(c, n, t):
                nc.vector.bn_stats(stats[c][:], t).then_inc(stats_ready[c], 1)
                wait_apart(dve, stats_ready[c], n + 1, (w_loaded, 16 * LOADS))
                nc.vector.bn_aggr(mv[c][:], stats[c][:]).then_inc(mv_ready[c], 1)
                dve.wait_ge(mv_ready[c], n + 1)
                nc.vector.tensor_scalar(var[c][:], mv[c][:, 1:2], EPS, None, ALU.add).then_inc(var_ready[c], 1)
                dve.wait_ge(rstd_ready[c], n + 1)
                nc.vector.scalar_tensor_tensor(shift[c][:], mv[c][:, 0:1], -1.0, rstd[c][:], ALU.mult,
                                               ALU.mult).then_inc(shift_ready[c], 1)
                dve.wait_ge(shift_ready[c], n + 1)

            def tile_of(t, n):
                return t[:, ds(n, 1), :].rearrange("p a d -> p (a d)")

            def after_attn(n, u):
                if not (isinstance(n, int) and n == 0):
                    dve.wait_ge(base_ready, n)
                dve.wait_ge(attn_done, n + 1)
                nc.vector.tensor_tensor(x1[:], ps_at[:], tile_of(x_all, n), ALU.add).then_inc(x1_ready, 1)
                dve.wait_ge(x1_ready, n + 1)
                moments(0, n, x1[:])
                nc.vector.tensor_scalar(z[:], x1[:], rstd[0][:], shift[0][:], ALU.mult, ALU.add).then_inc(z_ready, 1)
                nc.vector.tensor_tensor(base[u][:], x1[:], tile_of(xb_all, n), ALU.add).then_inc(base_ready, 1)

            def after_ffn(n, u):
                dve.wait_ge(base_ready, n + 1)
                if not (isinstance(n, int) and n == 0):
                    dve.wait_ge(out_ready, n)
                dve.wait_ge(f2_done, n + 1)
                nc.vector.tensor_tensor(total[:], ps_f2[:], base[u][:], ALU.add).then_inc(total_ready, 1)
                dve.wait_ge(total_ready, n + 1)
                moments(1, n, total[:])
                nc.vector.tensor_scalar(tile_of(x1_all, n), total[:], rstd[1][:], shift[1][:], ALU.mult,
                                        ALU.add).then_inc(out_ready, 1)

            def prologue():
                dve.wait_ge(w_loaded, 16 * LOADS)
                nc.vector.tensor_tensor(xb_all[:], x_all[:], b2[:].unsqueeze(1).broadcast_to([P, NT, D]),
                                        ALU.add).then_inc(xb_ready, 1)
                dve.wait_ge(xb_ready, 1)
                after_attn(0, 0)

            def step(n, u):
                if has(n, 1):
                    after_attn(n + 1, 1 - u)
                after_ffn(n, u)

            schedule(dve, prologue, step)

        @block.gpsimd
        def _(pool):
            nc.gpsimd.memset(half[:], -0.5).then_inc(half_ready, 1)
            pool.wait_ge(half_ready, 1)

            def power(c, n):
                pool.wait_ge(var_ready[c], n + 1)
                nc.gpsimd.tensor_tensor(rstd[c][:], var[c][:], half[:], ALU.pow).then_inc(rstd_ready[c], 1)

            def prologue():
                power(0, 0)

            def step(n, u):
                if has(n, 1):
                    power(0, n + 1)
                power(1, n)

            schedule(pool, prologue, step)


NF = 4
TOPK = 12
FAR = -3.0e38


def xattn_stage(nc, a, ident, x_rows, expert_w1):
    x1_all = x2_all = x_rows[:, :, 0:D]
    with ExitStack() as ctx:
        sb, ps, sem, start_block = tensors(nc, ctx, "xa_")
        fwd = sb("fwd", [P, 768])
        inv = sb("inv", [P, NF, 256])
        wts = {c: sb(f"w{c}", [P, KD, D]) for c in "qkvo"}
        dc_bias = sb("dc_bias", [1, 3, D])
        bo = sb("bo", [P, D])
        half = sb("half", [P, 4])
        ctx_in = sb("ctx_in", [P, CB, D])
        comb = {c: sb(f"comb_{c}", [P, 4, D]) for c in "xc"}
        fold = {c: sb(f"fold_{c}", [P, 2, D]) for c in "xc"}
        spec = {c: sb(f"spec_{c}", [P, KD, T]) for c in "xc"}
        proj = {c: sb(f"proj_{c}", [P, 2, 2, D]) for c in "qkv"}
        wspec = sb("wspec", [P, 2, 2, D])
        prod = {c: sb(f"prod_{c}", [P, 2, 2, D]) for c in "qv"}
        m = [sb(f"m{i}", [P, 2, D]) for i in range(4)]
        half_sums = [sb(f"half_sums{c}", [P, T]) for c in range(KD)]
        corr = [sb(f"corr{c}", [P, T]) for c in range(KD)]
        corr8 = [sb(f"corr8_{c}", [P, T]) for c in range(KD)]
        top = [sb(f"top{c}", [P, 16]) for c in range(KD)]
        nmax = [sb(f"nmax{c}", [P, 1]) for c in range(KD)]
        texp = [sb(f"texp{c}", [P, TOPK]) for c in range(KD)]
        tsum = [sb(f"tsum{c}", [P, 1]) for c in range(KD)]
        rsum = [sb(f"rsum{c}", [P, 1]) for c in range(KD)]
        dfold = [sb(f"dfold{c}", [P, 2, P]) for c in range(KD)]
        dcomb = [sb(f"dcomb{c}", [P, 4, P]) for c in range(KD)]
        dcomb_t = sb("dcomb_t", [P, 4, D])
        agg_t = [sb(f"agg_t{c}", [P, T]) for c in range(KD)]
        xbo = sb("xbo", [P, CB, D])
        stats, mv = sb("stats", [P, CB, 6]), sb("mv", [P, CB, 2])
        var, rstd, shift = sb("var", [P, CB]), sb("rstd", [P, CB]), sb("shift", [P, CB])
        tbank = [ps(f"t{i}", [P, T]) for i in range(2)]
        pbank = [ps(f"p{i}", [P, 2, D]) for i in range(4)]
        cbank = [ps(f"c{i}", [P, T]) for i in range(2)]

        w1_loaded = sem("w1_loaded")
        loaded, ctx_loaded, half_ready, bias_ready = sem("loaded"), sem("ctx_loaded"), sem("half_ready"), sem("bias_ready")
        fold_ready = {c: sem(f"fold_{c}") for c in "xc"}
        comb_ready = {c: sem(f"comb_{c}") for c in "xc"}
        dft_done = {c: sem(f"dft_{c}") for c in "xc"}
        spec_ready = {c: sem(f"spec_{c}") for c in "xc"}
        proj_done = {c: sem(f"projd_{c}") for c in "qkv"}
        proj_ready = {c: sem(f"projr_{c}") for c in "qkv"}
        dc_ready = {c: sem(f"dc_{c}") for c in "qkv"}
        mul_ready = {c: sem(f"mul_{c}") for c in "qv"}
        add_ready = {c: sem(f"add_{c}") for c in "qv"}
        prod_ready = {c: sem(f"prod_{c}") for c in "qv"}
        corr_done, sums_ready, corr_ready = sem("corr_done"), sem("sums_ready"), sem("corr_ready")
        top8_ready, corr8_ready, top16_ready = sem("top8_ready"), sem("corr8_ready"), sem("top16_ready")
        taken_ready, nmax_ready, exp_ready, texp_ready = sem("taken_ready"), sem("nmax_ready"), sem("exp_ready"), sem("texp_ready")
        far_ready = sem("far_ready")
        rsum_ready, weight_ready, scaled_ready = sem("rsum_ready"), sem("weight_ready"), sem("scaled_ready")
        dfold_ready, dcomb_ready = sem("dfold_ready"), sem("dcomb_ready")
        dt_done, dt_copied, wspec_done, wspec_ready = sem("dt_done"), sem("dt_copied"), sem("wspec_done"), sem("wspec_ready")
        agg_done, agg_sums, agg_ready = sem("agg_done"), sem("agg_sums"), sem("agg_ready")
        out_done, xbo_ready, res_ready = sem("out_done"), sem("xbo_ready"), sem("res_ready")
        stats_ready, mv_ready, var_ready, rstd_ready, shift_ready, x2_ready = (
            sem(q) for q in ("stats_ready", "mv_ready", "var_ready", "rstd_ready", "shift_ready", "x2_ready"))
        block = start_block()

        def schedule(eng, front, body, parts=(0, 1, 2)):
            for part in parts:
                front(0, part)
            body(0, lambda part: front(1, part))
            with eng.Fori(1, B - 1) as b:
                body(b, lambda part: front(b + 1, part))
            body(B - 1, lambda part: None)

        def ahead(b):
            return 0 if isinstance(b, int) and b == B - 1 else 1

        def wait_past(eng, sem_, value):
            if not (isinstance(value, int) and value == 0):
                eng.wait_ge(sem_, value)

        def first(b):
            return isinstance(b, int) and b == 0

        RE0, IM0, RE2, IM2 = (slice(64 * i, 64 * i + 64) for i in range(4))
        A_COLS, B_COLS = slice(256, 512), slice(512, 768)

        @block.sync
        def _(sp):
            sp.dma_start(fwd[:], a["dft_fwd"]).then_inc(loaded, 16)
            for c in "qkvo":
                sp.dma_start(wts[c][:], a[f"xattn_W{c}"].rearrange("(k p) m -> p k m", p=P)).then_inc(loaded, 16)
            sp.dma_start(inv[:], a["dft_inv"]).then_inc(loaded, 16)
            for i, c in enumerate("qkv"):
                sp.dma_start(dc_bias[:, i, :], a[f"xattn_b{c}"].rearrange("(o d) -> o d", o=1)).then_inc(loaded, 16)
            sp.dma_start(bo[:], a["xattn_bo"].rearrange("(o d) -> o d", o=1).broadcast_to([P, D])).then_inc(loaded, 16)

            def load(b):
                row = 0 if first(b) else sp.snap(b * T)
                if not first(b):
                    sp.wait_ge(fold_ready["c"], 2 * b)
                sp.dma_start(ctx_in[:], a["ctx_1024"][ds(row, T), :].rearrange("(j p) d -> p j d", p=P)).then_inc(ctx_loaded, 16)

            load(0)
            for e in range(NE):
                sp.dma_start(expert_w1[:, e, :, :], a["ffn_W1"][e, :, :].rearrange("(k p) f -> p k f", p=P)).then_inc(w1_loaded, 16)
            with sp.Fori(1, B) as b:
                load(b)
            sp.wait_ge(w1_loaded, 16 * NE)

        @block.tensor
        def _(pe):
            def dft(c, b):
                pe.wait_ge(comb_ready[c], 2 * b + 2)
                for k in range(KD):
                    bank = tbank[k]
                    if c == "c":
                        pe.wait_ge(spec_ready["x"], 2 * b + k + 1)
                    elif not first(b):
                        pe.wait_ge(spec_ready["c"], 2 * b)
                        wait_past(pe, dt_copied, 2 * b - 2)

                    def mm(lo, hi, q, cols, start=True, stop=True):
                        return nc.tensor.matmul(bank[:, lo:hi], comb[c][:, q, k * P:(k + 1) * P], fwd[:, cols],
                                                start=start, stop=stop, skip_group_check=True)
                    mm(0, 64, 0, RE0)
                    mm(128, 192, 0, IM0)
                    mm(64, 128, 1, RE2)
                    mm(192, 256, 1, IM2)
                    mm(256, 512, 2, A_COLS, stop=False)
                    mm(256, 512, 3, B_COLS, start=False).then_inc(dft_done[c], 1)

            def project(c, b):
                src = "x" if c == "q" else "c"
                banks = pbank[0:2] if c == "q" else pbank[2:4]
                pe.wait_ge(spec_ready[src], 2 * b + 2)
                for half_ in range(2):
                    for reim in range(2):
                        ft = 2 * half_ + reim
                        for k in range(KD):
                            last = nc.tensor.matmul(banks[half_][:, reim, :], spec[src][:, k, ft * P:(ft + 1) * P],
                                                    wts[c][:, k, :], start=(k == 0), stop=(k == KD - 1),
                                                    skip_group_check=True)
                    last.then_inc(proj_done[c], 1)

            def inverse(key, done):
                for k in range(KD):
                    for ft in range(NF):
                        half_, reim = divmod(ft, 2)
                        last = nc.tensor.matmul(cbank[k][:, 256 * half_:256 * half_ + 256],
                                                prod[key][:, half_, reim, k * P:(k + 1) * P], inv[:, ft, :],
                                                start=(reim == 0), stop=(reim == 1), skip_group_check=True)
                    last.then_inc(done, 1)

            def front(b, part):
                if part == 0:
                    dft("x", b)
                    dft("c", b)
                    if not first(b):
                        pe.wait_ge(proj_ready["q"], 2 * b)
                        wait_past(pe, res_ready, 2 * b - 2)
                    project("q", b)
                    if not first(b):
                        pe.wait_ge(proj_ready["v"], 2 * b)
                    project("k", b)
                elif part == 1:
                    pe.wait_ge(prod_ready["q"], b + 1)
                    if not first(b):
                        pe.wait_ge(sums_ready, 2 * b)
                        wait_past(pe, agg_sums, 2 * b - 2)
                    inverse("q", corr_done)
                else:
                    pe.wait_ge(proj_ready["k"], 2 * b + 2)
                    project("v", b)

            def body(b, front_):
                front_(0)
                for k in range(KD):
                    pe.wait_ge(dcomb_ready, 4 * b + 2 * k + 2)
                    pe.wait_ge(spec_ready["c"], 2 * (b + ahead(b)) + 2)
                    for q in range(4):
                        last = nc.tensor.transpose(tbank[k][:, q * P:(q + 1) * P], dcomb[k][:, q, :], ident[:])
                    last.then_inc(dt_done, 1)
                pe.wait_ge(dt_copied, 2 * b + 2)
                pe.wait_ge(proj_ready["q"], 2 * (b + ahead(b)) + 2)

                def mm(out, cols, q, start=True, stop=True):
                    return nc.tensor.matmul(out, fwd[:, cols], dcomb_t[:, q, :], start=start, stop=stop,
                                            skip_group_check=True)
                mm(pbank[0][0:64, 0, :], RE0, 0)
                mm(pbank[0][64:128, 0, :], RE2, 1)
                mm(pbank[0][0:64, 1, :], IM0, 0)
                mm(pbank[0][64:128, 1, :], IM2, 1).then_inc(wspec_done, 1)
                for reim in range(2):
                    mm(pbank[1][:, reim, :], slice(256 + P * reim, 256 + P * (reim + 1)), 2, stop=False)
                    last = mm(pbank[1][:, reim, :], slice(512 + P * reim, 512 + P * (reim + 1)), 3, start=False)
                last.then_inc(wspec_done, 1)
                front_(2)
                front_(1)
                pe.wait_ge(prod_ready["v"], b + 1)
                pe.wait_ge(sums_ready, 2 * (b + ahead(b)) + 2)
                inverse("v", agg_done)
                pe.wait_ge(agg_ready, 4 * b + 4)
                pe.wait_ge(wspec_ready, 2 * b + 2)
                for tt in range(CB):
                    for k in range(KD):
                        last = nc.tensor.matmul(pbank[tt // 2][:, tt % 2, :], agg_t[k][:, tt * P:(tt + 1) * P],
                                                wts["o"][:, k, :], start=(k == 0), stop=(k == KD - 1),
                                                skip_group_check=True)
                    if tt % 2:
                        last.then_inc(out_done, 1)

            pe.wait_ge(loaded, 16 * 10)
            schedule(pe, front, body)

        @block.scalar
        def _(act):
            def copy(out, in_, done):
                nc.scalar.activation(out, in_, ACT.Copy).then_inc(done, 1)

            def front(b, part):
                if part == 0:
                    for c in "xc":
                        for k in range(KD):
                            act.wait_ge(dft_done[c], 2 * b + k + 1)
                            copy(spec[c][:, k, :], tbank[k][:], spec_ready[c])
                elif part == 3:
                    if not first(b):
                        act.wait_ge(mul_ready["q"], 4 * b)
                    for c in "qk":
                        for i in range(2):
                            act.wait_ge(proj_done[c], 2 * b + i + 1)
                            copy(proj[c][:, i, :, :], pbank[i + (0 if c == "q" else 2)][:], proj_ready[c])
                elif part == 1:
                    for k in range(KD):
                        act.wait_ge(corr_done, 2 * b + k + 1)
                        if not first(b):
                            act.wait_ge(corr_ready, 4 * b)
                            wait_past(act, agg_ready, 4 * b - 4)
                        copy(half_sums[k][:], cbank[k][:], sums_ready)
                else:
                    for i in range(2):
                        act.wait_ge(proj_done["v"], 2 * b + i + 1)
                        if not first(b):
                            act.wait_ge(prod_ready["v"], b)
                        copy(proj["v"][:, i, :, :], pbank[2 + i][:], proj_ready["v"])

            def body(b, front_):
                front_(0)
                for k in range(KD):
                    act.wait_ge(nmax_ready, 2 * b + k + 1)
                    nc.scalar.activation(texp[k][:], top[k][:, 0:TOPK], ACT.Exp, bias=nmax[k][:],
                                         accum_out=tsum[k][:]).then_inc(texp_ready, 1)
                    act.wait_ge(corr8_ready, 2 * b + k + 1)
                    nc.scalar.activation(corr[k][:], corr[k][:], ACT.Exp, bias=nmax[k][:]).then_inc(exp_ready, 1)
                    act.wait_ge(taken_ready, 2 * b + k + 1)
                    nc.scalar.activation(corr8[k][:], corr8[k][:], ACT.Exp, bias=nmax[k][:]).then_inc(exp_ready, 1)
                front_(3)
                for k in range(KD):
                    act.wait_ge(dt_done, 2 * b + k + 1)
                    copy(dcomb_t[:, :, k * P:(k + 1) * P], tbank[k][:].rearrange("p (q t) -> p q t", q=4), dt_copied)
                wait_past(act, mul_ready["v"], 4 * b)
                for i in range(2):
                    act.wait_ge(wspec_done, 2 * b + i + 1)
                    copy(wspec[:, i, :, :], pbank[i][:], wspec_ready)
                front_(1)
                front_(2)
                for k in range(KD):
                    act.wait_ge(agg_done, 2 * b + k + 1)
                    act.wait_ge(corr_ready, 4 * (b + ahead(b)) + 4)
                    copy(half_sums[k][:], cbank[k][:], agg_sums)

            act.wait_ge(loaded, 16 * 10)
            nc.scalar.activation(dc_bias[:], dc_bias[:], ACT.Copy, scale=float(T)).then_inc(bias_ready, 1)
            schedule(act, front, body, (0, 3, 1, 2))

        @block.vector
        def _(dve):
            V = nc.vector
            held = (loaded, 16 * 10)

            def bias_at_dc(c, b):
                i = "qkv".index(c)
                dve.wait_ge(proj_ready[c], 2 * b + 2)
                V.tensor_tensor(proj[c][0:1, 0, 0, :], proj[c][0:1, 0, 0, :], dc_bias[0:1, i, :], ALU.add).then_inc(dc_ready[c], 1)
                dve.wait_ge(dc_ready[c], b + 1)

            def multiply(key, b, p, q):
                re, im = (lambda t: t[:, :, 0, :]), (lambda t: t[:, :, 1, :])
                for i, (x, y) in enumerate(((re(p), re(q)), (im(p), im(q)), (im(p), re(q)), (re(p), im(q)))):
                    V.tensor_tensor(m[i][:], x, y, ALU.mult).then_inc(mul_ready[key], 1)
                dve.wait_ge(mul_ready[key], 4 * b + 4)
                V.tensor_tensor(prod[key][:, :, 0, :], m[0][:], m[1][:], ALU.add).then_inc(add_ready[key], 1)
                V.tensor_tensor(prod[key][:, :, 1, :], m[2][:], m[3][:], ALU.subtract).then_inc(add_ready[key], 1)
                dve.wait_ge(add_ready[key], 2 * b + 2)
                V.tensor_copy(prod[key][0:1, 0, 0, :], m[0][0:1, 0, :])
                V.tensor_copy(prod[key][0:1, 0, 1, :], m[1][0:1, 0, :]).then_inc(prod_ready[key], 1)

            def unfold(out, sums, done, k):
                V.tensor_tensor(out[:, 0:256], sums[:, 0:256], sums[:, 256:512], ALU.add).then_inc(done, 1)
                V.tensor_tensor(out[:, 256:512], sums[:, 0:256], sums[:, 256:512], ALU.subtract).then_inc(done, 1)

            def front(b, part):
                if part == 1:
                    bias_at_dc("q", b)
                    bias_at_dc("k", b)
                    multiply("q", b, proj["q"], proj["k"])
                elif part == 2:
                    for k in range(KD):
                        dve.wait_ge(sums_ready, 2 * b + k + 1)
                        unfold(corr[k], half_sums[k], corr_ready, k)

            def largest(b, k):
                wait_apart(dve, corr_ready, 4 * b + 2 * k + 2, held)
                V.max(top[k][:, 0:8], corr[k][:]).then_inc(top8_ready, 1)
                wait_apart(dve, top8_ready, 2 * b + k + 1, held)
                V.match_replace(corr8[k][:], top[k][:, 0:8], corr[k][:], FAR).then_inc(corr8_ready, 1)
                wait_apart(dve, corr8_ready, 2 * b + k + 1, held)
                V.max(top[k][:, 8:16], corr8[k][:]).then_inc(top16_ready, 1)
                dve.wait_ge(top16_ready, 2 * b + k + 1)
                V.tensor_scalar(nmax[k][:], top[k][:, 0:1], -1.0, None, ALU.mult).then_inc(nmax_ready, 1)
                V.memset(top[k][:, TOPK:16], FAR).then_inc(far_ready, 1)
                wait_apart(dve, far_ready, 2 * b + k + 1, held)
                V.match_replace(corr8[k][:], top[k][:, 8:16], corr8[k][:], FAR).then_inc(taken_ready, 1)

            def weights(b):
                for k in range(KD):
                    dve.wait_ge(texp_ready, 2 * b + k + 1)
                    V.reciprocal(rsum[k][:], tsum[k][:]).then_inc(rsum_ready, 1)
                for k in range(KD):
                    dve.wait_ge(exp_ready, 4 * b + 2 * k + 2)
                    V.tensor_tensor(corr[k][:], corr[k][:], corr8[k][:], ALU.subtract).then_inc(weight_ready, 1)
                dve.wait_ge(rsum_ready, 2 * b + 2)
                for k in range(KD):
                    dve.wait_ge(weight_ready, 2 * b + k + 1)
                    V.tensor_scalar(corr[k][:], corr[k][:], rsum[k][:], None, ALU.mult).then_inc(scaled_ready, 1)
                for k in range(KD):
                    dve.wait_ge(scaled_ready, 2 * b + k + 1)
                    quarters = corr[k][:].rearrange("p (j t) -> p j t", j=4)
                    V.tensor_tensor(dfold[k][:], quarters[:, 0:2, :], quarters[:, 2:4, :], ALU.add).then_inc(dfold_ready, 1)
                    V.tensor_tensor(dcomb[k][:, 2:4, :], quarters[:, 0:2, :], quarters[:, 2:4, :], ALU.subtract).then_inc(dfold_ready, 1)
                for k in range(KD):
                    dve.wait_ge(dfold_ready, 4 * b + 2 * k + 2)
                    V.tensor_tensor(dcomb[k][:, 0, :], dfold[k][:, 0, :], dfold[k][:, 1, :], ALU.add).then_inc(dcomb_ready, 1)
                    V.tensor_tensor(dcomb[k][:, 1, :], dfold[k][:, 0, :], dfold[k][:, 1, :], ALU.subtract).then_inc(dcomb_ready, 1)

            def residual(b):
                dve.wait_ge(xbo_ready, b + 1)
                for i in range(2):
                    dve.wait_ge(out_done, 2 * b + i + 1)
                    V.tensor_tensor(xbo[:, 2 * i:2 * i + 2, :], pbank[i][:], xbo[:, 2 * i:2 * i + 2, :], ALU.add).then_inc(res_ready, 1)

            def layernorm(b):
                for j in range(CB):
                    dve.wait_ge(res_ready, 2 * b + j // 2 + 1)
                    V.bn_stats(stats[:, j, :], xbo[:, j, :]).then_inc(stats_ready, 1)
                for j in range(CB):
                    wait_apart(dve, stats_ready, 4 * b + j + 1, held)
                    V.bn_aggr(mv[:, j, :], stats[:, j, :]).then_inc(mv_ready, 1)
                dve.wait_ge(mv_ready, 4 * b + 4)
                V.tensor_scalar(var[:], mv[:, :, 1], EPS, None, ALU.add).then_inc(var_ready, 1)

            def normed(b):
                dve.wait_ge(rstd_ready, b + 1)
                V.scalar_tensor_tensor(shift[:], mv[:, :, 0], -1.0, rstd[:], ALU.mult, ALU.mult).then_inc(shift_ready, 1)
                dve.wait_ge(shift_ready, b + 1)
                for j in range(CB):
                    V.tensor_scalar(x2_all[:, ds(b * CB + j, 1), :].rearrange("p a d -> p (a d)"), xbo[:, j, :],
                                    rstd[:, j:j + 1], shift[:, j:j + 1], ALU.mult, ALU.add).then_inc(x2_ready, 1)

            def body(b, front_):
                largest(b, 0)
                if not first(b):
                    residual(b - 1)
                largest(b, 1)
                if not first(b):
                    layernorm(b - 1)
                weights(b)
                if not first(b):
                    normed(b - 1)
                front_(1)
                bias_at_dc("v", b)
                dve.wait_ge(wspec_ready, 2 * b + 2)
                dve.wait_ge(prod_ready["q"], b + ahead(b) + 1)
                multiply("v", b, proj["v"], wspec)
                front_(2)
                for k in range(KD):
                    dve.wait_ge(agg_sums, 2 * b + k + 1)
                    unfold(agg_t[k], half_sums[k], agg_ready, k)

            dve.wait_ge(loaded, 16 * 10)
            dve.wait_ge(bias_ready, 1)
            schedule(dve, front, body)
            residual(B - 1)
            layernorm(B - 1)
            normed(B - 1)

        @block.gpsimd
        def _(pool):
            G = nc.gpsimd
            G.memset(half[:], -0.5).then_inc(half_ready, 1)
            pool.wait_ge(half_ready, 1)

            def four_quarters(c, b, src):
                G.tensor_tensor(fold[c][:], src[:, 0:2, :], src[:, 2:4, :], ALU.add).then_inc(fold_ready[c], 1)
                G.tensor_tensor(comb[c][:, 2:4, :], src[:, 0:2, :], src[:, 2:4, :], ALU.subtract).then_inc(fold_ready[c], 1)
                pool.wait_ge(fold_ready[c], 2 * b + 2)
                G.tensor_tensor(comb[c][:, 0, :], fold[c][:, 0, :], fold[c][:, 1, :], ALU.add).then_inc(comb_ready[c], 1)
                G.tensor_tensor(comb[c][:, 1, :], fold[c][:, 0, :], fold[c][:, 1, :], ALU.subtract).then_inc(comb_ready[c], 1)

            def combine(b):
                for c in "xc":
                    if not first(b):
                        pool.wait_ge(dft_done[c], 2 * b)
                    if c == "c":
                        pool.wait_ge(ctx_loaded, 16 * b + 16)
                    four_quarters(c, b, x1_all[:, ds(b * CB, CB), :] if c == "x" else ctx_in)

            def residual(b):
                if not first(b):
                    pool.wait_ge(x2_ready, CB * b)
                G.tensor_tensor(xbo[:], x1_all[:, ds(b * CB, CB), :], bo[:].unsqueeze(1).broadcast_to([P, CB, D]),
                                ALU.add).then_inc(xbo_ready, 1)

            def inverse_deviation(b):
                pool.wait_ge(var_ready, b + 1)
                G.tensor_tensor(rstd[:], var[:], half[:], ALU.pow).then_inc(rstd_ready, 1)

            combine(0)
            combine(1)
            pool.wait_ge(loaded, 16 * 10)
            residual(0)
            with pool.Fori(0, B - 2) as b:
                combine(b + 2)
                inverse_deviation(b)
                residual(b + 1)
            inverse_deviation(B - 2)
            residual(B - 1)
            inverse_deviation(B - 1)




def experts_stage(nc, a, ident, x_rows, w1, out, xs_dram):
    x2_all = x_rows[:, :, 0:D]
    with ExitStack() as ctx:
        sb, ps, sem, start_block = tensors(nc, ctx, "ex_")
        w2 = sb("w2", [P, NE, FT, D])
        b1 = sb("b1", [P, NE, FT])
        b2 = sb("b2", [P, NE, D])
        wr = sb("wr", [P, KD, NE])
        br = sb("br", [P, NE])
        order = sb("order", [P, NE])
        edges = sb("edges", [P, NT])
        index = sb("index", [P, TILES])
        mask_strict = sb("mask_strict", [P, P])
        ones = sb("ones", [P, P])
        token = sb("token", [P, NT])
        empty = sb("empty", [P, XW])
        half = sb("half", [P, 1])
        xr = [sb(f"xr{i}", [P, 2, KD, P]) for i in range(2)]
        logit, ex, onehot = sb("logit", [P, NT, NE]), sb("exps", [P, NT, NE]), sb("onehot", [P, NT, NE])
        rank, tot, incl = sb("rank", [P, NT, NE]), sb("tot", [P, NT, NE]), sb("incl", [P, NT, NE])
        top, gate = sb("top", [P, NT]), sb("gate", [P, NT])
        over = sb("over", [P, NE, NT])
        tiles, tend, tstart = sb("tiles", [P, NE]), sb("tend", [P, NE]), sb("tstart", [P, NE])
        starts = sb("starts", [P, TILES, NE])
        expert_f, expert = sb("expert_f", [P, TILES]), sb("expert", [P, TILES], I32)
        pos_f, pos = sb("pos_f", [P, NT]), sb("pos", [P, NT], I32)
        x_in = [sb(f"x_in{u}", [P, XW]) for u in range(2)]
        row = [sb(f"row{u}", [P, XW]) for u in range(2)]
        x_t = sb("x_t", [P, KD, P])
        h = sb("h", [P, F])
        h_t = sb("h_t", [P, FT, P])
        b1_now = sb("b1_now", [P, FT])
        y = sb("y", [P, D])
        number = [sb(f"number{u}", [P, 1], I32) for u in range(2)]
        result = [sb(f"result{u}", [P, D]) for u in range(2)]
        stats, mv = sb("stats", [P, 6]), sb("mv", [P, 2])
        var, rstd, shift = sb("var", [P, 1]), sb("rstd", [P, 1]), sb("shift", [P, 1])
        ps_r = [ps(f"r{i}", [P, 2, KD, P]) for i in range(2)]
        ps_l = ps("l", [P, NT, NE])
        ps_h = [ps(f"h_ps{i}", [P, 512]) for i in range(2)]
        ps_ht = [ps(f"ht{i}", [P, 4, P]) for i in range(2)]
        ps_y = ps("y_ps", [P, D])
        ps_x = ps_r[0]

        r_loaded, w_loaded, ones_ready, half_ready, emptied, row_ready = (
            sem(q) for q in ("r_loaded", "w_loaded", "ones_ready", "half_ready", "emptied", "row_ready"))
        rt_done, rt_copied, logits_done = sem("rt_done"), sem("rt_copied"), sem("logits_done")
        route, diff_ready, ex_ready, onehot_ready = sem("route"), sem("diff_ready"), sem("ex_ready"), sem("onehot_ready")
        counts_done, pos_ready, expert_ready = sem("counts_done"), sem("pos_ready"), sem("expert_ready")
        scattered, xt_done, xt_copied = sem("scattered"), sem("xt_done"), sem("xt_copied")
        x_loaded = [sem(f"x_loaded{u}") for u in range(2)]
        stored = [sem(f"stored{u}") for u in range(2)]
        h_done, h_copied, ht_done, relu_ready = sem("h_done"), sem("h_copied"), sem("ht_done"), sem("relu_ready")
        b1_ready, y_done, y_ready, row_used = (sem(q) for q in ("b1_ready", "y_done", "y_ready", "row_used"))
        row_kept = sem("row_kept")
        stats_ready, mv_ready, var_ready, rstd_ready, shift_ready, result_ready = (
            sem(q) for q in ("stats_ready", "mv_ready", "var_ready", "rstd_ready", "shift_ready", "result_ready"))
        block = start_block()
        R_LOADS, W_LOADS = 8, NE + 2

        def tiles_in_pairs(eng, step, lo, hi):
            with eng.Fori(lo // 2, hi // 2) as it:
                step(2 * it, 0)
                step(2 * it + 1, 1)

        @block.sync
        def _(sp):
            sp.dma_start(wr[:], a["ffn_Wr"].rearrange("(k p) e -> p k e", p=P)).then_inc(r_loaded, 16)
            sp.dma_start(br[:], a["ffn_br"].rearrange("(o e) -> o e", o=1).broadcast_to([P, NE])).then_inc(r_loaded, 16)
            sp.dma_start(order[:], a["expert_order"]).then_inc(r_loaded, 16)
            sp.dma_start(edges[:], a["tile_edges"]).then_inc(r_loaded, 16)
            sp.dma_start(index[:], a["tile_index"]).then_inc(r_loaded, 16)
            sp.dma_start(mask_strict[:], a["mask_strict"]).then_inc(r_loaded, 16)
            sp.dma_start(token[:], a["token_number"]).then_inc(r_loaded, 16)
            sp.dma_start(empty[:], a["empty_row"]).then_inc(r_loaded, 16)
            sp.wait_ge(r_loaded, 16 * R_LOADS)
            sp.dma_start(xs_dram.rearrange("(n p) d -> p n d", p=P),
                         empty[:].unsqueeze(1).broadcast_to([P, TILES, XW])).then_inc(emptied, 16)
            sp.dma_start(b1[:], a["ffn_b1_cols"]).then_inc(w_loaded, 16)
            sp.dma_start(b2[:], a["ffn_b2"].rearrange("(o e) d -> o e d", o=1).broadcast_to([P, NE, D])).then_inc(w_loaded, 16)
            for e in range(NE):
                sp.dma_start(w2[:, e, :, :], a["ffn_W2"][e, :, :].rearrange("(f p) d -> p f d", p=P)).then_inc(w_loaded, 16)

            def load(j, u):
                start = j * P if isinstance(j, int) else sp.snap(j * P)
                if not (isinstance(j, int) and j < 2):
                    sp.wait_ge(xt_done, j - 1)
                    sp.wait_ge(row_kept, j - 1)
                sp.dma_start(x_in[u][:], xs_dram[ds(start, P), :]).then_inc(x_loaded[u], 16)

            sp.wait_ge(scattered, 16 * NT)
            load(0, 0)
            load(1, 1)
            tiles_in_pairs(sp, load, 2, TILES - 1)
            load(TILES - 1, 0)
            sp.wait_ge(stored[0], 16 * (TILES // 2 + 1))
            sp.wait_ge(stored[1], 16 * (TILES // 2))

        @block.tensor
        def _(pe):
            pe.wait_ge(r_loaded, 16 * R_LOADS)

            def logits(g):
                pe.wait_ge(rt_copied, g + 1)
                for n in (2 * g, 2 * g + 1):
                    for k in range(KD):
                        last = nc.tensor.matmul(ps_l[:, n, :], xr[g % 2][:, n % 2, k, :], wr[:, k, :],
                                                start=(k == 0), stop=(k == KD - 1), skip_group_check=True)
                return last

            for g in range(NT // 2):
                if g >= 2:
                    pe.wait_ge(rt_copied, g - 1)
                for n in (2 * g, 2 * g + 1):
                    for k in range(KD):
                        last = nc.tensor.transpose(ps_r[g % 2][:, n % 2, k, :], x2_all[:, n, k * P:(k + 1) * P], ident[:])
                last.then_inc(rt_done, 1)
                if g:
                    logits(g - 1)
            logits(NT // 2 - 1).then_inc(logits_done, 1)
            pe.wait_ge(onehot_ready, 1)
            pe.wait_ge(ones_ready, 1)
            flat = onehot[:].rearrange("p n e -> p (n e)")
            nc.tensor.matmul(ps_h[0][:, 0:NT * NE], mask_strict[:], flat, start=True, stop=True)
            nc.tensor.matmul(ps_h[1][:, 0:NT * NE], ones[:], flat, start=True, stop=True).then_inc(counts_done, 1)

            def x_transposes(j, u):
                pe.wait_ge(x_loaded[u], 8 * (j - u) + 16)
                if not (isinstance(j, int) and j == 0):
                    pe.wait_ge(xt_copied, j)
                for k in range(KD):
                    last = nc.tensor.transpose(ps_x[:, 0, k, :], x_in[u][:, k * P:(k + 1) * P], ident[:])
                last.then_inc(xt_done, 1)

            def up(j, e):
                pe.wait_ge(xt_copied, j + 1)
                for i in range(2):
                    if not (isinstance(j, int) and j == 0):
                        pe.wait_ge(h_copied, 2 * j + i - 1)
                    for k in range(KD):
                        last = nc.tensor.matmul(ps_h[i][:], x_t[:, k, :],
                                                w1[:, ds(e, 1), k, i * 512:(i + 1) * 512].rearrange("p o f -> p (o f)"),
                                                start=(k == 0), stop=(k == KD - 1))
                    last.then_inc(h_done, 1)

            def h_transposes(j):
                for i in range(2):
                    pe.wait_ge(h_copied, 2 * j + i + 1)
                    if not (isinstance(j, int) and j == 0):
                        pe.wait_ge(relu_ready, 8 * j + 4 * i - 4)
                    for f in range(4):
                        last = nc.tensor.transpose(ps_ht[i][:, f, :], h[:, (4 * i + f) * P:(4 * i + f + 1) * P], ident[:])
                    last.then_inc(ht_done, 1)

            def down(j, e):
                pe.wait_ge(relu_ready, 8 * j + 8)
                if not (isinstance(j, int) and j == 0):
                    pe.wait_ge(y_ready, j)
                for f in range(FT):
                    last = nc.tensor.matmul(ps_y[:], h_t[:, f, :], w2[:, ds(e, 1), f, :].rearrange("p o d -> p (o d)"),
                                            start=(f == 0), stop=(f == FT - 1))
                last.then_inc(y_done, 1)

            def expert_of(j):
                return pe.value_load(expert[0:1, ds(j, 1)], min_val=0, max_val=NE - 1)

            pe.wait_ge(expert_ready, 1)
            e0 = expert_of(0)
            pe.wait_ge(w_loaded, 16 * W_LOADS)
            x_transposes(0, 0)
            up(0, e0)
            h_transposes(0)
            x_transposes(1, 1)

            def step(j, u):
                e_up, e_down = expert_of(j + 1), expert_of(j)
                up(j + 1, e_up)
                down(j, e_down)
                h_transposes(j + 1)
                x_transposes(j + 2, u)

            step(0, 0)
            step(1, 1)
            tiles_in_pairs(pe, step, 2, TILES - 3)
            step(TILES - 3, 0)
            j = TILES - 2
            e_up, e_down = expert_of(j + 1), expert_of(j)
            up(j + 1, e_up)
            down(j, e_down)
            h_transposes(j + 1)
            down(j + 1, e_up)

        @block.scalar
        def _(act):
            for g in range(NT // 2):
                if g >= 2:
                    act.wait_ge(rt_done, g)
                act.wait_ge(rt_done, g + 1)
                nc.scalar.activation(xr[g % 2][:], ps_r[g % 2][:], ACT.Copy).then_inc(rt_copied, 1)
            act.wait_ge(diff_ready, 1)
            nc.scalar.activation(ex[:], ex[:], ACT.Exp).then_inc(ex_ready, 1)

            def x_copy(j):
                act.wait_ge(xt_done, j + 1)
                nc.scalar.activation(x_t[:], ps_x[:, 0, :, :], ACT.Copy).then_inc(xt_copied, 1)

            def keep(j, u):
                act.wait_ge(x_loaded[u], 8 * (j - u) + 16)
                if not (isinstance(j, int) and j < 2):
                    act.wait_ge(row_used, 2 * j - 2)
                nc.scalar.activation(row[u][:], x_in[u][:], ACT.Copy).then_inc(row_kept, 1)

            def h_copies(j):
                for i in range(2):
                    act.wait_ge(h_done, 2 * j + i + 1)
                    nc.scalar.activation(h[:, i * 512:(i + 1) * 512], ps_h[i][:], ACT.Copy).then_inc(h_copied, 1)

            x_copy(0)
            h_copies(0)
            keep(0, 0)
            x_copy(1)
            keep(1, 1)

            def step(j, u):
                h_copies(j + 1)
                x_copy(j + 2)
                keep(j + 2, u)

            tiles_in_pairs(act, step, 0, TILES - 3)
            step(TILES - 3, 0)
            h_copies(TILES - 1)

        @block.vector
        def _(dve):
            V = nc.vector
            made = [0]

            def then(ins):
                made[0] += 1
                ins.then_inc(route, 1)
                dve.wait_ge(route, made[0])

            def over_experts(t):
                return t.unsqueeze(2).broadcast_to([P, NT, NE])

            def over_tiles(t):
                return t.unsqueeze(1).broadcast_to([P, NT, NE])

            V.memset(ones[:], 1.0).then_inc(ones_ready, 1)
            dve.wait_ge(ones_ready, 1)
            dve.wait_ge(r_loaded, 16 * R_LOADS)
            dve.wait_ge(logits_done, 1)
            then(V.tensor_tensor(logit[:], ps_l[:], over_tiles(br[:]), ALU.add))
            then(V.tensor_reduce(top[:], logit[:], AX, ALU.max))
            V.tensor_tensor(ex[:], logit[:], over_experts(top[:]), ALU.subtract).then_inc(diff_ready, 1)
            then(V.tensor_tensor(onehot[:], logit[:], over_experts(top[:]), ALU.is_equal))
            then(V.tensor_tensor(onehot[:], onehot[:], over_tiles(order[:]), ALU.mult))
            then(V.tensor_reduce(top[:], onehot[:], AX, ALU.max))
            V.tensor_tensor(onehot[:], onehot[:], over_experts(top[:]), ALU.is_equal).then_inc(onehot_ready, 1)
            dve.wait_ge(ex_ready, 1)
            then(V.tensor_reduce(gate[:], ex[:], AX, ALU.add))
            V.reciprocal(x_rows[:, :, GATE], gate[:]).then_inc(row_ready, 1)
            V.tensor_scalar(x_rows[:, :, NUMBER], token[:], 1.0, None, ALU.mult).then_inc(row_ready, 1)
            dve.wait_ge(counts_done, 1)
            then(V.tensor_copy(rank[:].rearrange("p n e -> p (n e)"), ps_h[0][:, 0:NT * NE]))
            then(V.tensor_copy(tot[:].rearrange("p n e -> p (n e)"), ps_h[1][:, 0:NT * NE]))
            for e in range(NE):
                then(V.tensor_tensor_scan(incl[:, :, e], ones[:, 0:NT], tot[:, :, e], 0.0, ALU.mult, ALU.add))
            then(V.tensor_tensor(over[:], incl[:, NT - 1, :].unsqueeze(2).broadcast_to([P, NE, NT]),
                                 edges[:].unsqueeze(1).broadcast_to([P, NE, NT]), ALU.is_gt))
            then(V.tensor_reduce(tiles[:], over[:], AX, ALU.add))
            then(V.tensor_tensor_scan(tend[:], ones[:, 0:NE], tiles[:], 0.0, ALU.mult, ALU.add))
            then(V.tensor_tensor(tstart[:], tend[:], tiles[:], ALU.subtract))
            then(V.tensor_tensor(starts[:], index[:].unsqueeze(2).broadcast_to([P, TILES, NE]),
                                 tstart[:].unsqueeze(1).broadcast_to([P, TILES, NE]), ALU.is_ge))
            then(V.tensor_reduce(expert_f[:], starts[:], AX, ALU.add))
            V.tensor_scalar(expert[:], expert_f[:], -1.0, None, ALU.add).then_inc(expert_ready, 1)
            then(V.tensor_tensor(rank[:], rank[:], incl[:], ALU.add))
            then(V.tensor_tensor(rank[:], rank[:], tot[:], ALU.subtract))
            then(V.tensor_scalar(tstart[:], tstart[:], float(P), None, ALU.mult))
            then(V.tensor_tensor(rank[:], rank[:], over_tiles(tstart[:]), ALU.add))
            then(V.tensor_tensor(rank[:], rank[:], onehot[:], ALU.mult))
            then(V.tensor_reduce(pos_f[:], rank[:], AX, ALU.add))
            V.tensor_copy(pos[:], pos_f[:]).then_inc(pos_ready, 1)
            dve.wait_ge(expert_ready, 1)
            dve.wait_ge(w_loaded, 16 * W_LOADS)

            def expert_of(j):
                return dve.value_load(expert[0:1, ds(j, 1)], min_val=0, max_val=NE - 1)

            def relus(j, e):
                if not (isinstance(j, int) and j == 0):
                    dve.wait_ge(relu_ready, 8 * j)
                V.tensor_scalar(b1_now[:], b1[:, ds(e, 1), :].rearrange("p o f -> p (o f)"), 1.0, None,
                                ALU.mult).then_inc(b1_ready, 1)
                dve.wait_ge(b1_ready, j + 1)
                for i in range(2):
                    dve.wait_ge(ht_done, 2 * j + i + 1)
                    for f in range(4):
                        V.tensor_scalar(h_t[:, 4 * i + f, :], ps_ht[i][:, f, :], b1_now[:, 4 * i + f:4 * i + f + 1], 0.0,
                                        ALU.add, ALU.max).then_inc(relu_ready, 1)

            held = (w_loaded, 16 * W_LOADS)

            def y_out(j, e):
                dve.wait_ge(y_done, j + 1)
                V.tensor_tensor(y[:], ps_y[:], b2[:, ds(e, 1), :].rearrange("p o d -> p (o d)"), ALU.add).then_inc(y_ready, 1)

            def total(j, u):
                if not (isinstance(j, int) and j < 2):
                    dve.wait_ge(stored[u], 8 * (j - u))
                dve.wait_ge(row_kept, j + 1)
                V.tensor_scalar(number[u][:], row[u][:, NUMBER:NUMBER + 1], 1.0, None, ALU.mult).then_inc(row_used, 1)
                dve.wait_ge(y_ready, j + 1)
                V.scalar_tensor_tensor(result[u][:], y[:], row[u][:, GATE:GATE + 1], row[u][:, 0:D],
                                       ALU.mult, ALU.add).then_inc(row_used, 1)
                dve.wait_ge(row_used, 2 * j + 2)
                V.bn_stats(stats[:], result[u][:]).then_inc(stats_ready, 1)
                wait_apart(dve, stats_ready, j + 1, held)
                V.bn_aggr(mv[:], stats[:]).then_inc(mv_ready, 1)
                dve.wait_ge(mv_ready, j + 1)
                V.tensor_scalar(var[:], mv[:, 1:2], EPS, None, ALU.add).then_inc(var_ready, 1)

            def normed(j, u):
                dve.wait_ge(rstd_ready, j + 1)
                V.scalar_tensor_tensor(shift[:], mv[:, 0:1], -1.0, rstd[:], ALU.mult, ALU.mult).then_inc(shift_ready, 1)
                dve.wait_ge(shift_ready, j + 1)
                V.tensor_scalar(result[u][:], result[u][:], rstd[:], shift[:], ALU.mult, ALU.add).then_inc(result_ready, 1)

            relus(0, expert_of(0))

            def step(j, u):
                e_down, e_up = expert_of(j), expert_of(j + 1)
                y_out(j, e_down)
                relus(j + 1, e_up)
                total(j, u)
                normed(j, u)

            step(0, 0)
            step(1, 1)
            tiles_in_pairs(dve, step, 2, TILES - 1)
            y_out(TILES - 1, expert_of(TILES - 1))
            total(TILES - 1, 0)
            normed(TILES - 1, 0)

        @block.gpsimd
        def _(pool):
            nc.gpsimd.memset(half[:], -0.5).then_inc(half_ready, 1)
            pool.wait_ge(half_ready, 1)
            pool.wait_ge(emptied, 16)
            pool.wait_ge(pos_ready, 1)
            pool.wait_ge(row_ready, 2)
            for n in range(NT):
                nc.gpsimd.indirect_dma_start(out=xs_dram, out_offset=bass.IndirectOffsetOnAxis(ap=pos[:, n:n + 1], axis=0),
                                             in_=x_rows[:, n, :], in_offset=None).then_inc(scattered, 16)
            for j in range(TILES):
                pool.wait_ge(var_ready, j + 1)
                nc.gpsimd.tensor_tensor(rstd[:], var[:], half[:], ALU.pow).then_inc(rstd_ready, 1)
                pool.wait_ge(result_ready, j + 1)
                nc.gpsimd.indirect_dma_start(out=out, out_offset=bass.IndirectOffsetOnAxis(ap=number[j % 2][:], axis=0),
                                             in_=result[j % 2][:], in_offset=None,
                                             bounds_check=B * T - 1, oob_is_err=False).then_inc(stored[j % 2], 16)


def constants():
    import numpy as np
    i = np.arange(P)
    row, colm = i[:, None], i[None, :]
    c = {"ident": np.eye(P), "mask_incl": row <= colm, "mask_strict": row < colm}
    keep = np.ones((P, NT, H))
    keep[:, CB - 1::CB, :] = 0
    c["keep"] = keep.reshape(P, NT * H)

    def joins(b):
        return (row // (2 * b) == colm // (2 * b)) & (row // b % 2 == 1) & (colm // b % 2 == 0)

    c["mask_one"] = joins(1).T | (row == colm)
    c["mask_levels"] = np.stack([joins(2 << lev) | (row == colm) for lev in range(LEVELS)], axis=1)

    c["expert_order"] = np.tile(np.arange(NE, 0, -1), (P, 1))
    c["tile_edges"] = np.tile(P * np.arange(NT), (P, 1))
    c["tile_index"] = np.tile(np.arange(TILES), (P, 1))
    c["token_number"] = row + P * np.arange(NT)[None, :]
    c["empty_row"] = np.hstack([np.zeros((P, D + 1)), B * T + row])
    p, m64, m128 = np.arange(P)[:, None], np.arange(64)[None, :], np.arange(P)[None, :]

    def angle(f, t):
        return 2 * np.pi * ((f * t) % T) / T

    re0, im0 = np.cos(angle(4 * m64, p)), -np.sin(angle(4 * m64, p))
    im0[:, 0] = np.cos(angle(T // 2, p))[:, 0]
    re2, im2 = np.cos(angle(4 * m64 + 2, p)), -np.sin(angle(4 * m64 + 2, p))
    c1, s1 = np.cos(angle(4 * m128 + 1, p)), np.sin(angle(4 * m128 + 1, p))
    c["dft_fwd"] = np.concatenate([re0, im0, re2, im2, c1, -s1, -s1, -c1], axis=1)
    weight = np.where(m64.T == 0, 1.0, 2.0) / T
    z0re, z0im = weight * re0.T, weight * im0.T
    z2re, z2im = 2 / T * re2.T, 2 / T * im2.T
    even_re = np.concatenate([np.hstack([z0re, z0re]), np.hstack([z2re, -z2re])])
    even_im = np.concatenate([np.hstack([z0im, z0im]), np.hstack([z2im, -z2im])])
    odd_re = 2 / T * np.hstack([c1.T, -s1.T])
    odd_im = 2 / T * np.hstack([-s1.T, -c1.T])
    c["dft_inv"] = np.stack([even_re, even_im, odd_re, odd_im], axis=1)
    return {k: np.ascontiguousarray(v, np.float32) for k, v in c.items()}


def program(nc, a, out):
    qkv_dram = nc.dram_tensor("qkv_dram", (B * T, 3 * HW), F32, kind="Internal").ap()
    scal_dram = nc.dram_tensor("scal_dram", (NT, P, NSC * H), F32, kind="Internal").ap()
    grow_dram = nc.dram_tensor("grow_dram", (NT * H, P), F32, kind="Internal").ap()
    o_dram = nc.dram_tensor("o_dram", (B * T, HW), F32, kind="Internal").ap()
    xs_dram = nc.dram_tensor("xs_dram", (TILES * P, XW), F32, kind="Internal").ap()
    with ExitStack() as ctx:
        ident = ctx.enter_context(nc.sbuf_tensor("ident", [P, P], F32))
        ident_loaded = ctx.enter_context(nc.semaphore("ident_loaded"))
        with nc.Block() as block:
            @block.sync
            def _(sp):
                sp.dma_start(ident[:], a["ident"]).then_inc(ident_loaded, 16)
                sp.wait_ge(ident_loaded, 16)
        project_stage(nc, a, ident, qkv_dram, scal_dram, grow_dram)
        delta_stage(nc, a, ident, qkv_dram, scal_dram, grow_dram, o_dram)
        x_rows = ctx.enter_context(nc.sbuf_tensor("x_rows", [P, NT, XW], F32))
        ffn_stage(nc, a, ident, o_dram, x_rows)
        expert_w1 = ctx.enter_context(nc.sbuf_tensor("expert_w1", [P, NE, KD, F], F32))
        xattn_stage(nc, a, ident, x_rows, expert_w1)
        experts_stage(nc, a, ident, x_rows, expert_w1, out, xs_dram)


def kernel(**inputs):
    import numpy as np
    import concourse.bacc as bacc
    from concourse.bass_utils import run_bass_kernel_spmd

    nc = bacc.Bacc("TRN2", target_bir_lowering=False, num_devices=1)
    arrays = {}
    for name, v in inputs.items():
        v = np.ascontiguousarray(v)
        if name in ("x", "ctx_1024"):
            v = v.reshape(B * T, D)
        name = name.replace("L0_attn_", "").replace("L0_", "")
        if name == "ffn_b1":
            name, v = "ffn_b1_cols", np.ascontiguousarray(v.reshape(NE, FT, P).transpose(2, 0, 1))
        arrays[name] = v
    arrays.update(constants())
    a, feed = {}, {}
    for name, v in arrays.items():
        feed[f"in_{name}"] = v
        a[name] = nc.dram_tensor(f"in_{name}", v.shape, mybir.dt.from_np(v.dtype), kind="ExternalInput").ap()
    out = nc.dram_tensor("out", (B * T, D), F32, kind="ExternalOutput").ap()
    program(nc, a, out)
    r = run_bass_kernel_spmd(nc, [feed], core_ids=[0])
    return r.results[0]["out"].reshape(B, T, D)
```

```python
from contextlib import ExitStack

import concourse.bass as bass
from concourse import mybir

P = 128
B, T, D = 4, 512, 256
NT = B * T // P
CB = T // P
H, HD = 8, 128
HW = H * HD
TOP, LOW = slice(0, P // 2), slice(P // 2, P)
GH = 4
NG = H // GH
F = 1024
KD = D // P
FT = F // P
LEVELS = 6
NE = 8
TILES = NT + NE - 1
XW = D + 2
GATE, NUMBER = D, D + 1
EARLY = (B - 2) * CB
NSC = 5
EPS = 1e-5

MASK_SHAPES = {"mask_levels": [P, LEVELS - 1, P],
               "mask_incl": [P, P],
               "mask_strict": [P, P],
               "mask_one": [P, P]}
ROUTING_SHAPES = {"wr": [P, KD, NE], "br": [P, NE],
                  "order": [P, NE],
                  "edges": [P, NT],
                  "index": [P, TILES],
                  "mask_strict": [P, P],
                  "token": [P, NT],
                  "empty": [P, XW]}
FFN_SHAPES = {"Wo": [P, H, D], "W1": [P, KD, F], "W2": [P, FT, D], "b1": [P, FT], "b2": [P, D],
              "ln2_w": [P, KD], "ln2_b": [P, KD]}

F32 = mybir.dt.float32
I32 = mybir.dt.int32
ALU = mybir.AluOpType
ACT = mybir.ActivationFunctionType
AX = mybir.AxisListType.X
ds = bass.ds


def tensors(nc, ctx, prefix):
    def sb(name, shape, dt=F32):
        return ctx.enter_context(nc.sbuf_tensor(prefix + name, shape, dt))

    def ps(name, shape):
        return ctx.enter_context(nc.psum_tensor(prefix + name, shape, F32))

    numbers = []

    def sem(name):
        s = ctx.enter_context(nc.semaphore(prefix + name))
        numbers.append(s.num)
        return s

    def clear():
        runs = []
        for n in sorted(numbers):
            if runs and runs[-1][1] == n:
                runs[-1][1] = n + 1
            else:
                runs.append([n, n + 1])
        with nc.Block() as block:
            @block.sync
            def _(sp):
                for lo, hi in runs:
                    sp.sem_clear(range(lo, hi))

    def start_block():
        ctx.callback(clear)
        return ctx.enter_context(nc.Block())

    return sb, ps, sem, start_block


def wait_apart(eng, sem, value, held):
    if not isinstance(value, int):
        value = eng.to_reg(value)
    eng.wait_ge(*held)
    eng.wait_ge(sem, value)


def project_stage(nc, a, ident, x_rows, scalars, masks, qkv_dram, grow_dram):
    x_all = x_rows[:, :, 0:D]
    with ExitStack() as ctx:
        sb, ps, sem, start_block = tensors(nc, ctx, "pj_")
        w_qkv = sb("w_qkv", [P, KD, 3 * HW])
        w_gate = sb("w_gate", [P, KD, 2 * H])
        ln_w = sb("ln_w", [P, KD])
        ln_b = sb("ln_b", [P, KD])
        stats = sb("stats", [P, NT, 6])
        meanvar = sb("meanvar", [P, NT, 2])
        rstd = sb("rstd", [P, NT])
        shift = sb("shift", [P, NT])
        z = sb("z", [P, 2, D])
        n_t = sb("n_t", [P, 2, KD, P])
        sig = sb("sig", [P, 6, 512])
        act = sb("act", [P, 2, 3 * HW])
        sq = sb("sq", [P, 2 * HW])
        ss = sb("ss", [P, 2 * H])
        rn = sb("rn", [P, 2, 2 * H])
        half = sb("half", [P, 2 * H])
        gates = sb("gates", [P, NT, 2 * H])
        cumul = sb("cumul", [P, P])
        ones = sb("ones", [P, P])
        keep = sb("keep", [P, NT * H])
        beta = sb("beta", [P, NT * H])
        la = sb("la", [P, NT * H])
        tmp = sb("tmp", [P, NT * H])
        gsum = sb("gsum", [P, NT * H])
        gtot = sb("gtot", [P, NT * H])
        grow = sb("grow", [P, P])
        ps_t = [ps(f"t{u}", [P, 512]) for u in range(2)]
        ps_p = [ps(f"p{j}", [P, 512]) for j in range(6)]

        masks_loaded = sem("masks_loaded")
        rest_loaded, ln_loaded = sem("rest_loaded"), sem("ln_loaded")
        qkv_loaded = [sem(f"w_{c}_loaded") for c in "qkv"]
        x_loaded, w_loaded, g_loaded = sem("x_loaded"), sem("w_loaded"), sem("g_loaded")
        stats_done, aggr_done, ln_done, shift_done = sem("stats_done"), sem("aggr_done"), sem("ln_done"), sem("shift_done")
        z_ready, zt_done, nt_ready = sem("z_ready"), sem("zt_done"), sem("nt_ready")
        chunk_done, gate_done, gate_read = sem("chunk_done"), sem("gate_done"), sem("gate_read")
        sig_ready, act_ready = sem("sig_ready"), sem("act_ready")
        sq_ready, ss_ready, rn_ready, unit_ready = sem("sq_ready"), sem("ss_ready"), sem("rn_ready"), sem("unit_ready")
        stored = [sem(f"stored{u}") for u in range(2)]
        pow_ready, half_ready = sem("pow_ready"), sem("half_ready")
        const_ready, chain, la_ready = sem("const_ready"), sem("chain"), sem("la_ready")
        beta_ready, ex_ready, ln1p_ready = sem("beta_ready"), sem("ex_ready"), sem("ln1p_ready")
        sums_done, gsum_ready, grow_done, grow_ready = sem("sums_done"), sem("gsum_ready"), sem("grow_done"), sem("grow_ready")
        ediff_ready, eg_ready, out_stored = sem("ediff_ready"), sem("eg_ready"), sem("out_stored")
        block = start_block()

        @block.sync
        def _(sp):
            x_tiles = a["x"].rearrange("(n p) d -> p n d", p=P)
            sp.dma_start(x_all[:, 0:2, :], x_tiles[:, 0:2, :]).then_inc(x_loaded, 16)
            sp.dma_start(ln_w[:], a["ln1_w"].rearrange("(k p) -> p k", p=P),
                         allow_slow_non_contiguous=True).then_inc(ln_loaded, 16)
            sp.dma_start(ln_b[:], a["ln1_b"].rearrange("(k p) -> p k", p=P),
                         allow_slow_non_contiguous=True).then_inc(ln_loaded, 16)
            for j, w in enumerate(("Wq", "Wk", "Wv")):
                sp.dma_start(w_qkv[:, :, j * HW:(j + 1) * HW],
                             a[w].rearrange("(k p) m -> p k m", p=P)).then_inc(qkv_loaded[j], 16)
                if j == 0:
                    sp.dma_start(x_all[:, 2:NT, :], x_tiles[:, 2:NT, :]).then_inc(rest_loaded, 16)
            sp.dma_start(w_gate[:, :, 0:H], a["Wb"].rearrange("(k p) m -> p k m", p=P)).then_inc(w_loaded, 16)
            sp.dma_start(w_gate[:, :, H:2 * H], a["Wa"].rearrange("(k p) m -> p k m", p=P)).then_inc(w_loaded, 16)
            sp.dma_start(cumul[:], a["mask_incl"]).then_inc(g_loaded, 16)
            sp.dma_start(keep[:], a["keep"]).then_inc(g_loaded, 16)
            for name, mask in masks.items():
                sp.dma_start(mask[:], a[name]).then_inc(masks_loaded, 16)
            with sp.Fori(0, NT // 2) as it:
                for u in range(2):
                    row = sp.snap(it * 2 * P + u * P)
                    sp.wait_ge(unit_ready, 2 * it + u + 1)
                    sp.dma_start(qkv_dram[ds(row, P), :], act[:, u, :]).then_inc(stored[u], 16)
            sp.wait_ge(grow_ready, 1)
            sp.dma_start(grow_dram, grow[:]).then_inc(out_stored, 16)
            for u in range(2):
                sp.wait_ge(stored[u], 16 * (NT // 2))
            sp.wait_ge(out_stored, 16)
            sp.wait_ge(masks_loaded, 16 * len(masks))

        @block.vector
        def _(dve):
            dve.wait_ge(x_loaded, 16)
            def moments(lo, hi):
                for n in range(lo, hi):
                    nc.vector.bn_stats(stats[:, n, :], x_all[:, n, :]).then_inc(stats_done, 1)
                for n in range(lo, hi):
                    dve.wait_ge(stats_done, n + 1)
                    nc.vector.bn_aggr(meanvar[:, n, :], stats[:, n, :]).then_inc(aggr_done, 1)

            def shifts(lo, hi, done):
                dve.wait_ge(ln_done, done)
                nc.vector.scalar_tensor_tensor(shift[:, lo:hi], meanvar[:, lo:hi, 0], -1.0, rstd[:, lo:hi],
                                               ALU.mult, ALU.mult).then_inc(shift_done, 1)
                dve.wait_ge(shift_done, done)

            moments(0, 2)
            shifts(0, 2, 1)
            for u in range(2):
                nc.vector.tensor_scalar(z[:, u, :], x_all[:, u, :], rstd[:, u:u + 1], shift[:, u:u + 1],
                                        ALU.mult, ALU.add).then_inc(z_ready, 1)
            nc.vector.memset(ones[:], 1.0).then_inc(const_ready, 1)
            dve.wait_ge(rest_loaded, 16)
            moments(2, NT)
            shifts(2, NT, 2)

            def tile(it, u, more):
                n = 2 * it + u
                if more:
                    dve.wait_ge(zt_done, n + 1)
                    nc.vector.tensor_scalar(z[:, u, :], x_all[:, ds(n + 2, 1), :].rearrange("p a d -> p (a d)"),
                                            rstd[:, ds(n + 2, 1)], shift[:, ds(n + 2, 1)],
                                            ALU.mult, ALU.add).then_inc(z_ready, 1)
                for j in range(6):
                    dve.wait_ge(sig_ready, 6 * n + j + 1)
                    if j == 0 and not (isinstance(it, int) and it == 0):
                        dve.wait_ge(stored[u], 16 * it)
                    nc.vector.tensor_tensor(act[:, u, j * 512:(j + 1) * 512], ps_p[j][:], sig[:, j, :],
                                            ALU.mult).then_inc(act_ready, 1)
                dve.wait_ge(gate_done, n + 1)
                nc.vector.tensor_scalar(gates[:, ds(n, 1), :].rearrange("p a c -> p (a c)"), ps_t[u][:, 256:256 + 2 * H],
                                        1.0, None, ALU.mult).then_inc(gate_read, 1)
                dve.wait_ge(sq_ready, n + 1)
                nc.vector.tensor_reduce(ss[:], sq[:].rearrange("p (h d) -> p h d", d=HD), AX, ALU.add).then_inc(ss_ready, 1)
                dve.wait_ge(ss_ready, n + 1)
                nc.vector.tensor_scalar(rn[:, u, :], ss[:], 1e-6, None, ALU.add).then_inc(rn_ready, 1)

            for u in range(2):
                tile(0, u, True)
            with dve.Fori(1, NT // 2 - 1) as it:
                for u in range(2):
                    tile(it, u, True)
            for u in range(2):
                tile(NT // 2 - 1, u, False)

            dve.wait_ge(gate_read, NT)
            nc.vector.scalar_tensor_tensor(tmp[:].rearrange("p (n h) -> p n h", h=H), gates[:, :, H:2 * H], -1.0,
                                           gates[:, :, H:2 * H], ALU.mult, ALU.max).then_inc(chain, 1)
            nc.vector.tensor_scalar(la[:].rearrange("p (n h) -> p n h", h=H), gates[:, :, H:2 * H], 0.0, None,
                                    ALU.min).then_inc(la_ready, 1)
            dve.wait_ge(ln1p_ready, 1)
            dve.wait_ge(la_ready, 1)
            nc.vector.tensor_tensor(la[:], la[:], tmp[:], ALU.subtract).then_inc(la_ready, 1)
            dve.wait_ge(sums_done, 1)
            nc.vector.tensor_copy(gsum[:], ps_p[0][:, 0:P]).then_inc(gsum_ready, 1)
            nc.vector.tensor_copy(gtot[:], ps_p[1][:, 0:P]).then_inc(gsum_ready, 1)
            dve.wait_ge(gsum_ready, 2)
            nc.vector.tensor_tensor(tmp[:], gtot[:], gsum[:], ALU.subtract).then_inc(ediff_ready, 1)
            dve.wait_ge(grow_done, 1)
            nc.vector.tensor_copy(grow[:], ps_p[2][:, 0:P]).then_inc(grow_ready, 1)

            def col(c):
                return scalars[:, :, c, :]

            def nh(t):
                return t[:].rearrange("p (n h) -> p n h", h=H)

            dve.wait_ge(beta_ready, 1)
            dve.wait_ge(g_loaded, 32)
            nc.vector.tensor_scalar(col(0), nh(beta), 1.0, None, ALU.mult).then_inc(chain, 1)
            nc.vector.tensor_scalar(col(1), nh(beta), -1.0, None, ALU.mult).then_inc(chain, 1)
            nc.vector.tensor_scalar(col(2), nh(gsum), 1.0, None, ALU.mult).then_inc(chain, 1)
            dve.wait_ge(eg_ready, 2)
            nc.vector.tensor_tensor(col(3), nh(gtot), nh(keep), ALU.mult).then_inc(chain, 1)
            nc.vector.tensor_tensor(col(4), nh(tmp), nh(keep), ALU.mult).then_inc(chain, 1)
            dve.wait_ge(chain, 6)

        @block.gpsimd
        def _(pool):
            nc.gpsimd.memset(half[:], -0.5).then_inc(half_ready, 1)
            pool.wait_ge(half_ready, 1)
            for i, (lo, hi) in enumerate(((0, 2), (2, NT))):
                pool.wait_ge(aggr_done, hi)
                nc.gpsimd.tensor_scalar(rstd[:, lo:hi], meanvar[:, lo:hi, 1], EPS, None, ALU.add).then_inc(half_ready, 1)
                pool.wait_ge(half_ready, i + 2)
                nc.gpsimd.tensor_tensor(rstd[:, lo:hi], rstd[:, lo:hi], half[:, lo:hi], ALU.pow).then_inc(ln_done, 1)
            with pool.Fori(0, NT // 2) as it:
                for u in range(2):
                    n = 2 * it + u
                    qk = act[:, u, 0:2 * HW]
                    pool.wait_ge(rn_ready, n + 1)
                    nc.gpsimd.tensor_tensor(rn[:, u, :], rn[:, u, :], half[:], ALU.pow).then_inc(pow_ready, 1)
                    pool.wait_ge(pow_ready, n + 1)
                    nc.gpsimd.tensor_tensor(qk.rearrange("p (h d) -> p h d", d=HD),
                                            qk.rearrange("p (h d) -> p h d", d=HD),
                                            rn[:, u, :].unsqueeze(2).broadcast_to([P, 2 * H, HD]),
                                            ALU.mult).then_inc(unit_ready, 1)

        @block.scalar
        def _(act_e):
            act_e.wait_ge(ln_loaded, 32)

            def normed(n, u):
                act_e.wait_ge(zt_done, n + 1)
                for k in range(KD):
                    nc.scalar.activation(n_t[:, u, k, :], ps_t[u][:, k * P:(k + 1) * P], ACT.Identity,
                                         bias=ln_b[:, k:k + 1], scale=ln_w[:, k:k + 1]).then_inc(nt_ready, 1)

            def sigmoids(n, u, first=False, last=False):
                for j in range(6):
                    if j == 3 and not last:
                        normed(n + 1, 1 - u)
                    act_e.wait_ge(chunk_done, 6 * n + j + 1)
                    nc.scalar.activation(sig[:, j, :], ps_p[j][:], ACT.Sigmoid).then_inc(sig_ready, 1)
                act_e.wait_ge(act_ready, 6 * n + 4)
                if not first:
                    act_e.wait_ge(ss_ready, n)
                nc.scalar.activation(sq[:], act[:, u, 0:2 * HW], ACT.Square).then_inc(sq_ready, 1)

            normed(0, 0)
            sigmoids(0, 0, first=True)
            sigmoids(1, 1)
            with act_e.Fori(1, NT // 2 - 1) as it:
                sigmoids(2 * it, 0)
                sigmoids(2 * it + 1, 1)
            sigmoids(NT - 2, 0)
            sigmoids(NT - 1, 1, last=True)
            act_e.wait_ge(gate_read, NT)
            nc.scalar.activation(beta[:].rearrange("p (n h) -> p n h", h=H), gates[:, :, 0:H],
                                 ACT.Sigmoid).then_inc(beta_ready, 1)
            act_e.wait_ge(chain, 1)
            nc.scalar.activation(tmp[:], tmp[:], ACT.Exp, scale=-1.0).then_inc(ex_ready, 1)
            act_e.wait_ge(ex_ready, 1)
            nc.scalar.activation(tmp[:], tmp[:], ACT.Ln, bias=1.0).then_inc(ln1p_ready, 1)
            act_e.wait_ge(ediff_ready, 1)
            nc.scalar.activation(gtot[:], gtot[:], ACT.Exp).then_inc(eg_ready, 1)
            nc.scalar.activation(tmp[:], tmp[:], ACT.Exp).then_inc(eg_ready, 1)

        @block.tensor
        def _(pe):

            def transposes(n, u):
                pe.wait_ge(z_ready, n + 1)
                for k in range(KD):
                    last = nc.tensor.transpose(ps_t[u][:, k * P:(k + 1) * P], z[:, u, k * P:(k + 1) * P], ident[:])
                last.then_inc(zt_done, 1)

            def products(it, u, first, between):
                n = 2 * it + u
                for j in range(6):
                    if j == 3:
                        between()
                    if j == 0:
                        pe.wait_ge(nt_ready, 2 * n + 2)
                    if first and j % 2 == 0:
                        pe.wait_ge(qkv_loaded[j // 2], 16)
                    if not first:
                        pe.wait_ge(act_ready, 6 * n - 6 + j + 1)
                    for k in range(KD):
                        last = nc.tensor.matmul(ps_p[j][:], n_t[:, u, k, :], w_qkv[:, k, j * 512:(j + 1) * 512],
                                                start=(k == 0), stop=(k == KD - 1))
                    last.then_inc(chunk_done, 1)
                if first:
                    pe.wait_ge(w_loaded, 32)
                for k in range(KD):
                    last = nc.tensor.matmul(ps_t[u][:, 256:256 + 2 * H], n_t[:, u, k, :], w_gate[:, k, :],
                                            start=(k == 0), stop=(k == KD - 1))
                last.then_inc(gate_done, 1)

            def tile(it, u, first=False, last=False):
                n = 2 * it + u

                def next_transposes():
                    if not last:
                        if not first:
                            pe.wait_ge(gate_read, n)
                        transposes(n + 1, 1 - u)

                products(it, u, first, next_transposes)

            transposes(0, 0)
            tile(0, 0, first=True)
            tile(0, 1)
            with pe.Fori(1, NT // 2 - 1) as it:
                for u in range(2):
                    tile(it, u)
            tile(NT // 2 - 1, 0)
            tile(NT // 2 - 1, 1, last=True)
            pe.wait_ge(la_ready, 2)
            pe.wait_ge(g_loaded, 32)
            pe.wait_ge(const_ready, 1)
            nc.tensor.matmul(ps_p[0][:, 0:P], cumul[:], la[:], start=True, stop=True)
            nc.tensor.matmul(ps_p[1][:, 0:P], ones[:], la[:], start=True, stop=True).then_inc(sums_done, 1)
            pe.wait_ge(gsum_ready, 2)
            nc.tensor.transpose(ps_p[2][:, 0:P], gsum[:], ident[:]).then_inc(grow_done, 1)


def delta_stage(nc, a, ident, scalars, masks, ffn_weights, qkv_dram, grow_dram, o_dram):
    with ExitStack() as ctx:
        sb, ps, sem, start_block = tensors(nc, ctx, "dl_")
        qkv = [sb(f"qkv{u}", [P, 3, H, HD]) for u in range(2)]
        k_rows = sb("k_rows", [P, H, HD])
        gb = [sb(f"gb{u}", [P, H, P]) for u in range(2)]
        BETA, NBETA, GSUM, GEND, WDECAY = range(NSC)
        mask_levels, mask_incl, mask_strict, mask_one = (
            masks[c] for c in ("mask_levels", "mask_incl", "mask_strict", "mask_one"))

        def pair(name, slots=2):
            return [[sb(f"{name}{u}{g}", [P, GH, P]) for g in range(NG)] for u in range(slots)]

        k_t, q_t, kg_t, qg_t = pair("k_t", 1) * 2, pair("q_t", 1) * 2, pair("kg_t"), pair("qg_t")
        n_mat_t, attn_t, tinv, tinv_t = pair("n_mat_t"), pair("attn_t"), pair("tinv"), pair("tinv_t")
        eg, edec, eb = pair("eg", 1)[0], pair("edec", 1)[0], pair("eb", 1)[0]
        ymat, rhs, w, w2, sdec, state = (pair(s, 1)[0] for s in ("ymat", "rhs", "w", "w2", "sdec", "state"))
        o_sb = pair("o_sb", 1)[0]
        bank = [ps(f"m{i}", [P, GH, P]) for i in range(4)]
        xb = [ps(f"x{g}", [P, GH, P]) for g in range(NG)]
        tb = [ps(f"t{g}", [P, GH, P]) for g in range(NG)]

        loaded = [sem(f"loaded{u}") for u in range(2)]
        ffn_loaded, state_zero = sem("ffn_loaded"), sem("state_zero")
        kt_done, qt_done, kk_done, kq_done, tinv2_done = (sem(s) for s in ("kt_done", "qt_done", "kk_done", "kq_done", "tinv2_done"))
        x_done, t_done, tt_done = sem("x_done"), sem("t_done"), sem("tt_done")
        ks_done, y_done, o_done, kw_done = sem("ks_done"), sem("y_done"), sem("o_done"), sem("kw_done")
        eg_ready, edec_ready, kt_copied, qt_copied, tinv2_copied = (
            sem(s) for s in ("eg_ready", "edec_ready", "kt_copied", "qt_copied", "tinv2_copied"))
        t_copied, tt_copied, o_copied = sem("t_copied"), sem("tt_copied"), sem("o_copied")
        kg_ready, qg_ready, diff_ready, a_ready, attn_ready, tinv2t_ready = (
            sem(s) for s in ("kg_ready", "qg_ready", "diff_ready", "a_ready", "attn_ready", "tinv2t_ready"))
        ymat_ready, r_ready, w_ready, s_ready = sem("ymat_ready"), sem("r_ready"), sem("w_ready"), sem("s_ready")
        nbm_ready, eb_ready, n_ready, incl_ready = sem("nbm_ready"), sem("eb_ready"), sem("n_ready"), sem("incl_ready")
        k_kept = sem("k_kept")
        w2_ready, sdec_ready, o_stored = sem("w2_ready"), sem("sdec_ready"), sem("o_stored")
        block = start_block()

        def scalars_of(n, c, lo, hi):
            return scalars[:, ds(n, 1), c, lo:hi].rearrange("p a h -> p (a h)")

        def per_head(n, c, g):
            return scalars_of(n, c, g * GH, (g + 1) * GH).unsqueeze(2).broadcast_to([P, GH, P])

        def per_group(m):
            return m.unsqueeze(1).broadcast_to([P, GH, P])

        def schedule(eng, prep, invert, update):
            def step(n, u, first, last):
                invert(n, u, lambda part: None if first else update(n - 1, 1 - u, part),
                       lambda part: None if last else prep(n + 1, 1 - u, part))

            for part in range(3):
                prep(0, 0, part)
            step(0, 0, True, False)
            step(1, 1, False, False)
            with eng.Fori(1, NT // 2 - 1) as j:
                step(2 * j, 0, False, False)
                step(2 * j + 1, 1, False, False)
            step(NT - 2, 0, False, False)
            step(NT - 1, 1, False, True)
            for part in range(3):
                update(NT - 1, 1, part)

        def static(n):
            return isinstance(n, int)

        @block.sync
        def _(sp):
            def load(n, u, reuse):
                row = sp.snap(n * P) if reuse and not static(n) else n * P
                if reuse:
                    sp.wait_ge(r_ready, 2 * n - 2)
                    sp.wait_ge(k_kept, n - 1)
                sp.dma_start(qkv[u][:], qkv_dram[ds(row, P), :].rearrange("p (c h d) -> p c h d", c=3, h=H)).then_inc(loaded[u], 16)
                sp.dma_start(gb[u][:], grow_dram[ds(n * H, H), :].partition_broadcast(P)).then_inc(loaded[u], 16)

            def store(n):
                row = n * P if static(n) else sp.snap(n * P)
                for g in range(NG):
                    sp.wait_ge(o_copied, 2 * n + g + 1)
                    sp.dma_start(o_dram[ds(row, P), g * GH * P:(g + 1) * GH * P].rearrange("p (h t) -> p h t", h=GH),
                                 o_sb[g][:]).then_inc(o_stored, 16)

            load(0, 0, False)
            load(1, 1, False)
            for w in ("Wo", "W1", "W2"):
                sp.dma_start(ffn_weights[w][:], a[w].rearrange("(k p) m -> p k m", p=P)).then_inc(ffn_loaded, 16)
            sp.dma_start(ffn_weights["b2"][:], a["b2"].rearrange("(o d) -> o d", o=1).broadcast_to([P, D])).then_inc(ffn_loaded, 16)
            for w in ("b1", "ln2_w", "ln2_b"):
                sp.dma_start(ffn_weights[w][:], a[w].rearrange("(k p) -> p k", p=P),
                             allow_slow_non_contiguous=True).then_inc(ffn_loaded, 16)
            load(2, 0, True)
            store(0)
            with sp.Fori(1, NT // 2 - 1) as j:
                load(2 * j + 1, 1, True)
                store(2 * j - 1)
                load(2 * j + 2, 0, True)
                store(2 * j)
            load(NT - 1, 1, True)
            store(NT - 3)
            store(NT - 2)
            store(NT - 1)
            sp.wait_ge(o_stored, 32 * NT)
            sp.wait_ge(ffn_loaded, 16 * len(ffn_weights))

        @block.tensor
        def _(pe):
            held = (state_zero, NG)

            def four(out, lhs, rhs_, **flags):
                for h in range(GH):
                    last = nc.tensor.matmul(out[:, h, :], lhs(h), rhs_(h), start=flags.get("start", True),
                                            stop=flags.get("stop", True), skip_group_check=True)
                return last

            def four_transposed(out, src):
                for h in range(GH):
                    last = nc.tensor.transpose(out[:, h, :], src[:, h, :], ident[:])
                return last

            def prep(n, u, part):
                if part == 0:
                    pe.wait_ge(loaded[u], 32 * (n // 2 + 1) if static(n) else 16 * n + (32 if u == 0 else 16))
                    for g in range(NG):
                        k_bank, q_bank = bank[2 * g], bank[2 * g + 1]
                        if not (static(n) and n < 2):
                            if g == 0:
                                pe.wait_ge(o_copied, 2 * n - 2)
                            else:
                                pe.wait_ge(s_ready, 2 * n - 2)
                        elif n == 1:
                            pe.wait_ge(attn_ready, g + 1)
                        four_transposed(k_bank, qkv[u][:, 1, g * GH:(g + 1) * GH, :]).then_inc(kt_done, 1)
                        four_transposed(q_bank, qkv[u][:, 0, g * GH:(g + 1) * GH, :]).then_inc(qt_done, 1)
                elif part == 1:
                    for g in range(NG):
                        kk, kq = bank[2 * g], bank[2 * g + 1]
                        pe.wait_ge(kt_copied, 2 * n + g + 1)
                        four(kk, lambda h: k_t[u][g][:, h, :], lambda h: k_t[u][g][:, h, :]).then_inc(kk_done, 1)
                        pe.wait_ge(qt_copied, 2 * n + g + 1)
                        four(kq, lambda h: k_t[u][g][:, h, :], lambda h: q_t[u][g][:, h, :]).then_inc(kq_done, 1)
                else:
                    for g in range(NG):
                        pe.wait_ge(tinv2t_ready, 2 * n + g + 1)
                        four_transposed(bank[2 * g], tinv_t[u][g]).then_inc(tinv2_done, 1)

            def invert(n, u, update_, prep_):
                for lev in range(LEVELS):
                    for g in range(NG):
                        if lev == 0:
                            pe.wait_ge(tinv2_copied, 2 * n + g + 1)
                            pe.wait_ge(n_ready, 2 * n + g + 1)
                        else:
                            pe.wait_ge(t_copied, 10 * n + 2 * (lev - 1) + g + 1)
                            four_transposed(tb[g], tinv[u][g]).then_inc(tt_done, 1)
                        if lev < LEVELS - 1:
                            four(xb[g], lambda h: n_mat_t[u][g][:, h, :], lambda h: tinv[u][g][:, h, :]).then_inc(x_done, 1)
                        else:
                            four(xb[g][LOW, :, TOP], lambda h: n_mat_t[u][g][TOP, h, LOW],
                                 lambda h: tinv[u][g][TOP, h, TOP]).then_inc(x_done, 1)
                    if lev < 3:
                        update_(lev)
                    else:
                        prep_(lev - 3)
                    for g in range(NG):
                        if not (static(n) and n == 0 and lev == 0):
                            pe.wait_ge(tt_copied, 12 * n + 2 * (lev - 1) + g + 1)
                        if lev < LEVELS - 1:
                            pe.wait_ge(ymat_ready, 12 * n + 2 * lev + g + 1)
                        else:
                            wait_apart(pe, ymat_ready, 12 * n + 2 * lev + g + 1, held)
                        if lev < LEVELS - 1:
                            four(tb[g], lambda h: tinv_t[u][g][:, h, :], lambda h: ymat[g][:, h, :]).then_inc(t_done, 1)
                        else:
                            four(tb[g][TOP, :, LOW], lambda h: ymat[g][LOW, h, TOP],
                                 lambda h: tinv_t[u][g][LOW, h, LOW]).then_inc(tt_done, 1)

            def update(n, u, part):
                for g in range(NG):
                    if part == 0:
                        if not (static(n) and n == NT - 1):
                            if g == 0:
                                pe.wait_ge(tinv2_copied, 2 * n + 3)
                            else:
                                pe.wait_ge(attn_ready, 2 * n + 3)
                        if static(n) and n == 0:
                            pe.wait_ge(state_zero, 2)
                        else:
                            pe.wait_ge(s_ready, 2 * n - 1 + g)
                        pe.wait_ge(kg_ready, 2 * n + g + 1)
                        four(bank[g], lambda h: kg_t[u][g][:, h, :], lambda h: state[g][:, h, :]).then_inc(ks_done, 1)
                    elif part == 1:
                        pe.wait_ge(r_ready, 2 * n + g + 1)
                        pe.wait_ge(tt_copied, 12 * n + 11 + g)
                        if not (static(n) and n == NT - 1):
                            if g == 0:
                                pe.wait_ge(tinv2_copied, 2 * n + 4)
                            else:
                                pe.wait_ge(attn_ready, 2 * n + 4)
                        four(bank[2 + g], lambda h: tinv_t[u][g][:, h, :], lambda h: rhs[g][:, h, :]).then_inc(y_done, 1)
                    else:
                        pe.wait_ge(w_ready, 2 * n + g + 1)
                        pe.wait_ge(incl_ready, 2 * n + g + 1)
                        pe.wait_ge(qg_ready, 2 * n + g + 1)
                        for h in range(GH):
                            nc.tensor.matmul(bank[g][:, h, :], state[g][:, h, :], qg_t[u][g][:, h, :],
                                             start=True, stop=False, skip_group_check=True)
                            last = nc.tensor.matmul(bank[g][:, h, :], w[g][:, h, :], attn_t[u][g][:, h, :],
                                                    start=False, stop=True, skip_group_check=True)
                        last.then_inc(o_done, 1)
                if part == 2:
                    for g in range(NG):
                        pe.wait_ge(k_kept, n + 1)
                        pe.wait_ge(w2_ready, 2 * n + g + 1)
                        four(bank[2 + g], lambda h: k_rows[:, g * GH + h, :],
                             lambda h: w2[g][:, h, :]).then_inc(kw_done, 1)

            pe.wait_ge(*held)
            schedule(pe, prep, invert, update)

        @block.scalar
        def _(act):
            def prep(n, u, part):
                if part == 0:
                    act.wait_ge(loaded[u], 32 * (n // 2 + 1) if static(n) else 16 * n + (32 if u == 0 else 16))
                    for g in range(NG):
                        heads = slice(g * GH, (g + 1) * GH)
                        if not (static(n) and n == 0):
                            act.wait_ge(qg_ready, 2 * n - 1 + g)
                        nc.scalar.activation(eg[g][:], gb[u][:, heads, :], ACT.Exp).then_inc(eg_ready, 1)
                    for g in range(NG):
                        act.wait_ge(kt_done, 2 * n + g + 1)
                        nc.scalar.activation(k_t[u][g][:], bank[2 * g][:], ACT.Copy).then_inc(kt_copied, 1)
                        act.wait_ge(qt_done, 2 * n + g + 1)
                        nc.scalar.activation(q_t[u][g][:], bank[2 * g + 1][:], ACT.Copy).then_inc(qt_copied, 1)
                        act.wait_ge(diff_ready, 8 * n + 4 * g + 4)
                        nc.scalar.activation(edec[g][:], edec[g][:], ACT.Exp).then_inc(edec_ready, 1)
                elif part == 2:
                    for g in range(NG):
                        act.wait_ge(tinv2_done, 2 * n + g + 1)
                        nc.scalar.activation(tinv[u][g][:], bank[2 * g][:], ACT.Copy).then_inc(tinv2_copied, 1)

            def invert(n, u, update_, prep_):
                for lev in range(LEVELS):
                    if lev < 3:
                        update_(lev)
                    else:
                        prep_(lev - 3)
                    if lev < LEVELS - 1:
                        for g in range(NG):
                            act.wait_ge(t_done, 10 * n + 2 * lev + g + 1)
                            nc.scalar.activation(tinv[u][g][:], tb[g][:], ACT.Copy).then_inc(t_copied, 1)
                    for g in range(NG):
                        act.wait_ge(tt_done, 12 * n + 2 * lev + g + 1)
                        if lev < LEVELS - 1:
                            nc.scalar.activation(tinv_t[u][g][:], tb[g][:], ACT.Copy).then_inc(tt_copied, 1)
                        else:
                            nc.scalar.activation(tinv_t[u][g][TOP, :, LOW], tb[g][TOP, :, LOW], ACT.Copy).then_inc(tt_copied, 1)

            def update(n, u, part):
                if part != 2:
                    return
                for g in range(NG):
                    if not (static(n) and n == 0):
                        act.wait_ge(o_stored, 32 * n)
                    act.wait_ge(o_done, 2 * n + g + 1)
                    nc.scalar.activation(o_sb[g][:], bank[g][:], ACT.Copy).then_inc(o_copied, 1)

            schedule(act, prep, invert, update)

        @block.vector
        def _(dve):
            for g in range(NG):
                nc.vector.memset(state[g][:], 0.0).then_inc(state_zero, 1)

            def prep(n, u, part):
                if part == 0:
                    dve.wait_ge(loaded[u], 32 * (n // 2 + 1) if static(n) else 16 * n + (32 if u == 0 else 16))
                    for g in range(NG):
                        if not (static(n) and n == 0):
                            dve.wait_ge(eb_ready, 2 * n - 1 + g)
                            dve.wait_ge(attn_ready, 2 * n - 1 + g)
                        for h in range(GH):
                            hh = g * GH + h
                            nc.vector.tensor_scalar(edec[g][:, h, :], gb[u][:, hh, :], scalars_of(n, GSUM, hh, hh + 1), 0.0,
                                                    ALU.subtract, ALU.min).then_inc(diff_ready, 1)
                    for g in range(NG):
                        dve.wait_ge(eg_ready, 2 * n + g + 1)
                        dve.wait_ge(kt_copied, 2 * n + g + 1)
                        nc.vector.tensor_tensor(kg_t[u][g][:], k_t[u][g][:], eg[g][:], ALU.mult).then_inc(kg_ready, 1)
                        dve.wait_ge(qt_copied, 2 * n + g + 1)
                        nc.vector.tensor_tensor(qg_t[u][g][:], q_t[u][g][:], eg[g][:], ALU.mult).then_inc(qg_ready, 1)
                elif part == 1:
                    for g in range(NG):
                        dve.wait_ge(kk_done, 2 * n + g + 1)
                        dve.wait_ge(eb_ready, 2 * n + g + 1)
                        nc.vector.tensor_tensor(n_mat_t[u][g][:], bank[2 * g][:], eb[g][:], ALU.mult).then_inc(a_ready, 1)
                        dve.wait_ge(kq_done, 2 * n + g + 1)
                        nc.vector.tensor_tensor(attn_t[u][g][:], bank[2 * g + 1][:], edec[g][:], ALU.mult).then_inc(attn_ready, 1)
                    for g in range(NG):
                        dve.wait_ge(n_ready, 2 * n + g + 1)
                        nc.vector.tensor_tensor(tinv_t[u][g][:], n_mat_t[u][g][:], per_group(mask_one[:]),
                                                ALU.mult).then_inc(tinv2t_ready, 1)

            def invert(n, u, update_, prep_):
                for lev in range(LEVELS):
                    for g in range(NG):
                        dve.wait_ge(x_done, 12 * n + 2 * lev + g + 1)
                        if lev < LEVELS - 1:
                            nc.vector.tensor_tensor(ymat[g][:], xb[g][:], per_group(mask_levels[:, lev, :]),
                                                    ALU.mult).then_inc(ymat_ready, 1)
                        else:
                            nc.vector.tensor_scalar(ymat[g][LOW, :, TOP], xb[g][LOW, :, TOP], 1.0, None,
                                                    ALU.mult).then_inc(ymat_ready, 1)
                    if lev < 3:
                        update_(lev)
                    else:
                        prep_(lev - 3)

            def update(n, u, part):
                for g in range(NG):
                    if part == 0:
                        dve.wait_ge(ks_done, 2 * n + g + 1)
                        nc.vector.tensor_tensor(rhs[g][:], qkv[u][:, 2, g * GH:(g + 1) * GH, :], bank[g][:],
                                                ALU.subtract).then_inc(r_ready, 1)
                    elif part == 1:
                        dve.wait_ge(y_done, 2 * n + g + 1)
                        nc.vector.tensor_tensor(w[g][:], bank[2 + g][:], per_head(n, BETA, g), ALU.mult).then_inc(w_ready, 1)
                    else:
                        dve.wait_ge(kw_done, 2 * n + g + 1)
                        dve.wait_ge(sdec_ready, 2 * n + g + 1)
                        nc.vector.tensor_tensor(state[g][:], sdec[g][:], bank[2 + g][:], ALU.add).then_inc(s_ready, 1)

            schedule(dve, prep, invert, update)

        @block.gpsimd
        def _(pool):
            def prep(n, u, part):
                if part == 0:
                    for g in range(NG):
                        pool.wait_ge(loaded[u], 32 * (n // 2 + 1) if static(n) else 16 * n + (32 if u == 0 else 16))
                        if not (static(n) and n == 0):
                            pool.wait_ge(a_ready, 2 * n - 1 + g)
                        nc.gpsimd.tensor_tensor(eb[g][:], per_group(mask_strict[:]), per_head(n, NBETA, g),
                                                ALU.mult).then_inc(nbm_ready, 1)
                elif part == 1:
                    for g in range(NG):
                        pool.wait_ge(edec_ready, 2 * n + g + 1)
                        pool.wait_ge(nbm_ready, 2 * n + g + 1)
                        nc.gpsimd.tensor_tensor(eb[g][:], eb[g][:], edec[g][:], ALU.mult).then_inc(eb_ready, 1)
                    for g in range(NG):
                        pool.wait_ge(a_ready, 2 * n + g + 1)
                        nc.gpsimd.tensor_tensor(n_mat_t[u][g][:], n_mat_t[u][g][:], per_group(ident[:]),
                                                ALU.add).then_inc(n_ready, 1)
                else:
                    for g in range(NG):
                        pool.wait_ge(attn_ready, 2 * n + g + 1)
                        nc.gpsimd.tensor_tensor(attn_t[u][g][:], attn_t[u][g][:], per_group(mask_incl[:]),
                                                ALU.mult).then_inc(incl_ready, 1)

            def invert(n, u, update_, prep_):
                for part in range(3):
                    update_(part)
                for part in range(3):
                    prep_(part)

            def update(n, u, part):
                for g in range(NG):
                    if part == 0:
                        if static(n) and n == 0:
                            pool.wait_ge(state_zero, 2)
                        else:
                            pool.wait_ge(s_ready, 2 * n - 1 + g)
                        nc.gpsimd.tensor_tensor(sdec[g][:], state[g][:], per_head(n, GEND, g), ALU.mult).then_inc(sdec_ready, 1)
                        if g == NG - 1:
                            if not (static(n) and n == 0):
                                wait_apart(pool, kw_done, 2 * n, (state_zero, NG))
                            nc.gpsimd.tensor_copy(k_rows[:], qkv[u][:, 1, :, :]).then_inc(k_kept, 1)
                    elif part == 1:
                        pool.wait_ge(w_ready, 2 * n + g + 1)
                        nc.gpsimd.tensor_tensor(w2[g][:], w[g][:], per_head(n, WDECAY, g), ALU.mult).then_inc(w2_ready, 1)

            schedule(pool, prep, invert, update)


def ffn_stage(nc, ident, o_dram, x_rows, weights):
    x_all = x1_all = x_rows[:, :, 0:D]
    wo, w1, w2, b1, b2, ln_w, ln_b = (weights[c] for c in ("Wo", "W1", "W2", "b1", "b2", "ln2_w", "ln2_b"))
    with ExitStack() as ctx:
        sb, ps, sem, start_block = tensors(nc, ctx, "ff_")
        xb_all = sb("xb_all", [P, NT, D])
        half = sb("half", [P, 1])
        o_t = [sb(f"o_t{u}", [P, H, P]) for u in range(2)]
        x1 = sb("x1", [P, D])
        z = sb("z", [P, D])
        h_t = sb("h_t", [P, KD, P])
        g_t = sb("g_t", [P, FT, P])
        base = [sb(f"base{u}", [P, D]) for u in range(2)]
        total = sb("total", [P, D])
        stats = [sb(f"stats{c}", [P, 6]) for c in range(2)]
        mv = [sb(f"mv{c}", [P, 2]) for c in range(2)]
        var = [sb(f"var{c}", [P, 1]) for c in range(2)]
        rstd = [sb(f"rstd{c}", [P, 1]) for c in range(2)]
        shift = [sb(f"shift{c}", [P, 1]) for c in range(2)]
        ps_at = ps("at", [P, D])
        ps_z = ps("z_ps", [P, KD, P])
        ps_f1 = [ps(f"f1{i}", [P, 4, P]) for i in range(2)]
        ps_f2 = ps("f2", [P, D])

        half_ready, xb_ready = sem("half_ready"), sem("xb_ready")
        o_loaded = [sem(f"o_loaded{u}") for u in range(2)]
        attn_done, x1_ready = sem("attn_done"), sem("x1_ready")
        z_ready, zt_done, ht_ready = sem("z_ready"), sem("zt_done"), sem("ht_ready")
        f1_done, gelu_ready, f2_done, total_ready = sem("f1_done"), sem("gelu_ready"), sem("f2_done"), sem("total_ready")
        base_ready, out_ready = sem("base_ready"), sem("out_ready")
        stats_ready = [sem(f"stats_ready{c}") for c in range(2)]
        mv_ready = [sem(f"mv_ready{c}") for c in range(2)]
        var_ready = [sem(f"var_ready{c}") for c in range(2)]
        rstd_ready = [sem(f"rstd_ready{c}") for c in range(2)]
        shift_ready = [sem(f"shift_ready{c}") for c in range(2)]
        block = start_block()

        def schedule(eng, prologue, step):
            prologue()
            step(0, 0)
            step(1, 1)
            with eng.Fori(1, NT // 2 - 1) as j:
                step(2 * j, 0)
                step(2 * j + 1, 1)
            step(NT - 2, 0)
            step(NT - 1, 1)

        def has(n, k):
            return not isinstance(n, int) or n + k < NT

        @block.sync
        def _(sp):
            def load(n, u):
                row = n * P if isinstance(n, int) else sp.snap(n * P)
                if not (isinstance(n, int) and n < 2):
                    sp.wait_ge(attn_done, n - 1)
                sp.dma_start(o_t[u][:], o_dram[ds(row, P), :].rearrange("p (h t) -> p h t", h=H)).then_inc(o_loaded[u], 16)

            load(0, 0)
            load(1, 1)
            with sp.Fori(1, NT // 2) as j:
                load(2 * j, 0)
                load(2 * j + 1, 1)

        @block.tensor
        def _(pe):
            def attn(n, u):
                pe.wait_ge(o_loaded[u], 16 * (n // 2 + 1) if isinstance(n, int) else 8 * n + (16 if u == 0 else 8))
                if not (isinstance(n, int) and n == 0):
                    pe.wait_ge(x1_ready, n)
                for h in range(H):
                    last = nc.tensor.matmul(ps_at[:], o_t[u][:, h, :], wo[:, h, :], start=(h == 0), stop=(h == H - 1))
                last.then_inc(attn_done, 1)

            def z_transposes(n):
                pe.wait_ge(z_ready, n + 1)
                if not (isinstance(n, int) and n == 0):
                    pe.wait_ge(ht_ready, 2 * n)
                for k in range(KD):
                    last = nc.tensor.transpose(ps_z[:, k, :], z[:, k * P:(k + 1) * P], ident[:])
                last.then_inc(zt_done, 1)

            def ffn1(n):
                pe.wait_ge(ht_ready, 2 * n + 2)
                for f in range(FT):
                    if f % 4 == 0 and not (isinstance(n, int) and n == 0):
                        pe.wait_ge(gelu_ready, 8 * n - 4 + f)
                    for k in range(KD):
                        last = nc.tensor.matmul(ps_f1[f // 4][:, f % 4, :], w1[:, k, f * P:(f + 1) * P], h_t[:, k, :],
                                                start=(k == 0), stop=(k == KD - 1), skip_group_check=True)
                    if f % 4 == 3:
                        last.then_inc(f1_done, 1)

            def ffn2(n):
                pe.wait_ge(gelu_ready, 8 * n + 8)
                if not (isinstance(n, int) and n == 0):
                    pe.wait_ge(total_ready, n)
                for f in range(FT):
                    last = nc.tensor.matmul(ps_f2[:], g_t[:, f, :], w2[:, f, :], start=(f == 0), stop=(f == FT - 1))
                last.then_inc(f2_done, 1)

            def prologue():
                attn(0, 0)
                attn(1, 1)
                z_transposes(0)

            def step(n, u):
                ffn1(n)
                if has(n, 2):
                    attn(n + 2, u)
                if has(n, 1):
                    z_transposes(n + 1)
                ffn2(n)

            schedule(pe, prologue, step)

        @block.scalar
        def _(act):
            def h_copies(n):
                act.wait_ge(zt_done, n + 1)
                for k in range(KD):
                    nc.scalar.activation(h_t[:, k, :], ps_z[:, k, :], ACT.Identity,
                                         bias=ln_b[:, k:k + 1], scale=ln_w[:, k:k + 1]).then_inc(ht_ready, 1)

            def gelus(n):
                for f in range(FT):
                    if f % 4 == 0:
                        act.wait_ge(f1_done, 2 * n + f // 4 + 1)
                    nc.scalar.activation(g_t[:, f, :], ps_f1[f // 4][:, f % 4, :], ACT.Gelu,
                                         bias=b1[:, f:f + 1]).then_inc(gelu_ready, 1)

            def prologue():
                h_copies(0)

            def step(n, u):
                gelus(n)
                if has(n, 1):
                    h_copies(n + 1)

            schedule(act, prologue, step)

        @block.vector
        def _(dve):
            def moments(c, n, t):
                nc.vector.bn_stats(stats[c][:], t).then_inc(stats_ready[c], 1)
                wait_apart(dve, stats_ready[c], n + 1, (xb_ready, 1))
                nc.vector.bn_aggr(mv[c][:], stats[c][:]).then_inc(mv_ready[c], 1)
                dve.wait_ge(mv_ready[c], n + 1)
                nc.vector.tensor_scalar(var[c][:], mv[c][:, 1:2], EPS, None, ALU.add).then_inc(var_ready[c], 1)
                dve.wait_ge(rstd_ready[c], n + 1)
                nc.vector.scalar_tensor_tensor(shift[c][:], mv[c][:, 0:1], -1.0, rstd[c][:], ALU.mult,
                                               ALU.mult).then_inc(shift_ready[c], 1)
                dve.wait_ge(shift_ready[c], n + 1)

            def tile_of(t, n):
                return t[:, ds(n, 1), :].rearrange("p a d -> p (a d)")

            def after_attn(n, u):
                if not (isinstance(n, int) and n == 0):
                    dve.wait_ge(base_ready, n)
                dve.wait_ge(attn_done, n + 1)
                nc.vector.tensor_tensor(x1[:], ps_at[:], tile_of(x_all, n), ALU.add).then_inc(x1_ready, 1)
                dve.wait_ge(x1_ready, n + 1)
                moments(0, n, x1[:])
                if not (isinstance(n, int) and n == 0):
                    dve.wait_ge(zt_done, n)
                nc.vector.tensor_scalar(z[:], x1[:], rstd[0][:], shift[0][:], ALU.mult, ALU.add).then_inc(z_ready, 1)
                nc.vector.tensor_tensor(base[u][:], x1[:], tile_of(xb_all, n), ALU.add).then_inc(base_ready, 1)

            def after_ffn(n, u):
                dve.wait_ge(base_ready, n + 1)
                if not (isinstance(n, int) and n == 0):
                    dve.wait_ge(out_ready, n)
                dve.wait_ge(f2_done, n + 1)
                nc.vector.tensor_tensor(total[:], ps_f2[:], base[u][:], ALU.add).then_inc(total_ready, 1)
                dve.wait_ge(total_ready, n + 1)
                moments(1, n, total[:])
                nc.vector.tensor_scalar(tile_of(x1_all, n), total[:], rstd[1][:], shift[1][:], ALU.mult,
                                        ALU.add).then_inc(out_ready, 1)

            def prologue():
                nc.vector.tensor_tensor(xb_all[:], x_all[:], b2[:].unsqueeze(1).broadcast_to([P, NT, D]),
                                        ALU.add).then_inc(xb_ready, 1)
                dve.wait_ge(xb_ready, 1)
                after_attn(0, 0)
                after_attn(1, 1)

            def step(n, u):
                after_ffn(n, u)
                if has(n, 2):
                    after_attn(n + 2, u)

            schedule(dve, prologue, step)

        @block.gpsimd
        def _(pool):
            nc.gpsimd.memset(half[:], -0.5).then_inc(half_ready, 1)
            pool.wait_ge(half_ready, 1)

            def power(c, n):
                pool.wait_ge(var_ready[c], n + 1)
                nc.gpsimd.tensor_tensor(rstd[c][:], var[c][:], half[:], ALU.pow).then_inc(rstd_ready[c], 1)

            def prologue():
                power(0, 0)
                power(0, 1)

            def step(n, u):
                power(1, n)
                if has(n, 2):
                    power(0, n + 2)

            schedule(pool, prologue, step)


NF = 4
TOPK = 12
FAR = -3.0e38


def xattn_stage(nc, a, ident, x_rows, expert_w1, routing, logit, xs_dram):
    x1_all = x2_all = x_rows[:, :, 0:D]
    with ExitStack() as ctx:
        sb, ps, sem, start_block = tensors(nc, ctx, "xa_")
        fwd = sb("fwd", [P, 768])
        inv = sb("inv", [P, NF, 256])
        wts = {c: sb(f"w{c}", [P, KD, D]) for c in "qkvo"}
        dc_bias = sb("dc_bias", [1, 3, D])
        bo = sb("bo", [P, D])
        half = sb("half", [P, 4])
        ctx_in = sb("ctx_in", [P, CB, D])
        comb = {c: sb(f"comb_{c}", [P, 4, D]) for c in "xc"}
        fold = {c: sb(f"fold_{c}", [P, 2, D]) for c in "xc"}
        spec = {c: sb(f"spec_{c}", [P, KD, T]) for c in "xc"}
        proj = {c: sb(f"proj_{c}", [P, 2, 2, D]) for c in "qkv"}
        wspec = sb("wspec", [P, 2, 2, D])
        prod = {c: sb(f"prod_{c}", [P, 2, 2, D]) for c in "qv"}
        m = [sb(f"m{i}", [P, 2, D]) for i in range(4)]
        half_sums = [sb(f"half_sums{c}", [P, T]) for c in range(KD)]
        corr = [sb(f"corr{c}", [P, T]) for c in range(KD)]
        corr8 = [sb(f"corr8_{c}", [P, T]) for c in range(KD)]
        top = [sb(f"top{c}", [P, 16]) for c in range(KD)]
        nmax = [sb(f"nmax{c}", [P, 1]) for c in range(KD)]
        texp = [sb(f"texp{c}", [P, TOPK]) for c in range(KD)]
        tsum = [sb(f"tsum{c}", [P, 1]) for c in range(KD)]
        rsum = [sb(f"rsum{c}", [P, 1]) for c in range(KD)]
        dfold = [sb(f"dfold{c}", [P, 2, P]) for c in range(KD)]
        dcomb = [sb(f"dcomb{c}", [P, 4, P]) for c in range(KD)]
        dcomb_t = sb("dcomb_t", [P, 4, D])
        agg_t = [sb(f"agg_t{c}", [P, T]) for c in range(KD)]
        xbo = sb("xbo", [P, CB, D])
        stats, mv = sb("stats", [P, CB, 6]), sb("mv", [P, CB, 2])
        var, rstd, shift = sb("var", [P, CB]), sb("rstd", [P, CB]), sb("shift", [P, CB])
        tbank = [ps(f"t{i}", [P, T]) for i in range(2)]
        pbank = [ps(f"p{i}", [P, 2, D]) for i in range(4)]
        cbank = [ps(f"c{i}", [P, T]) for i in range(2)]

        fwd_loaded, bias_loaded = sem("fwd_loaded"), sem("bias_loaded")
        wr_loaded, lx_done, lx_copied = sem("wr_loaded"), sem("lx_done"), sem("lx_copied")
        logits_done, logits_kept = sem("logits_done"), sem("logits_kept")
        w1_loaded, empty_loaded, emptied = sem("w1_loaded"), sem("empty_loaded"), sem("emptied")
        loaded, ctx_loaded, half_ready, bias_ready = sem("loaded"), sem("ctx_loaded"), sem("half_ready"), sem("bias_ready")
        fold_ready = {c: sem(f"fold_{c}") for c in "xc"}
        comb_ready = {c: sem(f"comb_{c}") for c in "xc"}
        dft_done = {c: sem(f"dft_{c}") for c in "xc"}
        spec_ready = {c: sem(f"spec_{c}") for c in "xc"}
        proj_done = {c: sem(f"projd_{c}") for c in "qkv"}
        proj_ready = {c: sem(f"projr_{c}") for c in "qkv"}
        dc_ready = {c: sem(f"dc_{c}") for c in "qkv"}
        mul_ready = {c: sem(f"mul_{c}") for c in "qv"}
        add_ready = {c: sem(f"add_{c}") for c in "qv"}
        prod_ready = {c: sem(f"prod_{c}") for c in "qv"}
        corr_done, sums_ready, corr_ready = sem("corr_done"), sem("sums_ready"), sem("corr_ready")
        top8_ready, corr8_ready, top16_ready = sem("top8_ready"), sem("corr8_ready"), sem("top16_ready")
        taken_ready, nmax_ready, exp_ready, texp_ready = sem("taken_ready"), sem("nmax_ready"), sem("exp_ready"), sem("texp_ready")
        far_ready = sem("far_ready")
        rsum_ready, weight_ready, scaled_ready = sem("rsum_ready"), sem("weight_ready"), sem("scaled_ready")
        dfold_ready, dcomb_ready = sem("dfold_ready"), sem("dcomb_ready")
        dt_done, dt_copied, wspec_done, wspec_ready = sem("dt_done"), sem("dt_copied"), sem("wspec_done"), sem("wspec_ready")
        agg_done, agg_sums, agg_ready = sem("agg_done"), sem("agg_sums"), sem("agg_ready")
        out_done, xbo_ready, res_ready = sem("out_done"), sem("xbo_ready"), sem("res_ready")
        stats_ready, mv_ready, var_ready, rstd_ready, shift_ready, x2_ready = (
            sem(q) for q in ("stats_ready", "mv_ready", "var_ready", "rstd_ready", "shift_ready", "x2_ready"))
        block = start_block()

        def schedule(eng, front, body, parts=(0, 1, 2)):
            for part in parts:
                front(0, part)
            body(0, lambda part: front(1, part))
            with eng.Fori(1, B - 1) as b:
                body(b, lambda part: front(b + 1, part))
            body(B - 1, lambda part: None)

        def ahead(b):
            return 0 if isinstance(b, int) and b == B - 1 else 1

        def wait_past(eng, sem_, value):
            if not (isinstance(value, int) and value == 0):
                eng.wait_ge(sem_, value)

        def final(b):
            return isinstance(b, int) and b == B - 1

        def early_x(g):
            return spec["x"][:, g % 2, :].rearrange("p (n k t) -> p n k t", n=2, k=KD)

        def first(b):
            return isinstance(b, int) and b == 0

        RE0, IM0, RE2, IM2 = (slice(64 * i, 64 * i + 64) for i in range(4))
        A_COLS, B_COLS = slice(256, 512), slice(512, 768)

        @block.sync
        def _(sp):
            def load(b):
                row = 0 if first(b) else sp.snap(b * T)
                if not first(b):
                    sp.wait_ge(fold_ready["c"], 2 * b)
                sp.dma_start(ctx_in[:], a["ctx_1024"][ds(row, T), :].rearrange("(j p) d -> p j d", p=P)).then_inc(ctx_loaded, 16)

            sp.dma_start(fwd[:], a["dft_fwd"]).then_inc(fwd_loaded, 16)
            load(0)
            for i, c in enumerate("qkv"):
                sp.dma_start(dc_bias[:, i, :], a[f"xattn_b{c}"].rearrange("(o d) -> o d", o=1)).then_inc(bias_loaded, 16)
            for c in "qkvo":
                sp.dma_start(wts[c][:], a[f"xattn_W{c}"].rearrange("(k p) m -> p k m", p=P)).then_inc(loaded, 16)
            sp.dma_start(inv[:], a["dft_inv"]).then_inc(loaded, 16)
            sp.dma_start(bo[:], a["xattn_bo"].rearrange("(o d) -> o d", o=1).broadcast_to([P, D])).then_inc(loaded, 16)
            sp.dma_start(routing["wr"][:], a["ffn_Wr"].rearrange("(k p) e -> p k e", p=P)).then_inc(wr_loaded, 16)
            sp.dma_start(routing["br"][:], a["ffn_br"].rearrange("(o e) -> o e", o=1).broadcast_to([P, NE])).then_inc(w1_loaded, 16)
            for name in ("order", "edges", "index", "mask_strict", "token"):
                sp.dma_start(routing[name][:], a[name]).then_inc(w1_loaded, 16)
            sp.dma_start(routing["empty"][:], a["empty"]).then_inc(empty_loaded, 16)
            for e in range(NE):
                sp.dma_start(expert_w1[:, e, :, :], a["ffn_W1"][e, :, :].rearrange("(k p) f -> p k f", p=P)).then_inc(w1_loaded, 16)
            with sp.Fori(1, B) as b:
                load(b)
            sp.wait_ge(empty_loaded, 16)
            sp.dma_start(xs_dram.rearrange("(n p) d -> p n d", p=P),
                         routing["empty"][:].unsqueeze(1).broadcast_to([P, TILES, XW])).then_inc(emptied, 16)
            sp.wait_ge(w1_loaded, 16 * (NE + len(routing) - 2))
            sp.wait_ge(emptied, 16)

        @block.tensor
        def _(pe):
            def dft(c, b):
                pe.wait_ge(comb_ready[c], 2 * b + 2)
                for k in range(KD):
                    bank = tbank[k]
                    if c == "c":
                        pe.wait_ge(spec_ready["x"], 2 * b + k + 1)
                    elif not first(b):
                        pe.wait_ge(spec_ready["c"], 2 * b)
                        wait_past(pe, dt_copied, 2 * b - 2)

                    def mm(lo, hi, q, cols, start=True, stop=True):
                        return nc.tensor.matmul(bank[:, lo:hi], comb[c][:, q, k * P:(k + 1) * P], fwd[:, cols],
                                                start=start, stop=stop, skip_group_check=True)
                    mm(0, 64, 0, RE0)
                    mm(128, 192, 0, IM0)
                    mm(64, 128, 1, RE2)
                    mm(192, 256, 1, IM2)
                    mm(256, 512, 2, A_COLS, stop=False)
                    mm(256, 512, 3, B_COLS, start=False).then_inc(dft_done[c], 1)

            def project(c, b):
                src = "x" if c == "q" else "c"
                banks = pbank[0:2] if c == "q" else pbank[2:4]
                pe.wait_ge(spec_ready[src], 2 * b + 2)
                for half_ in range(2):
                    for reim in range(2):
                        ft = 2 * half_ + reim
                        for k in range(KD):
                            last = nc.tensor.matmul(banks[half_][:, reim, :], spec[src][:, k, ft * P:(ft + 1) * P],
                                                    wts[c][:, k, :], start=(k == 0), stop=(k == KD - 1),
                                                    skip_group_check=True)
                    last.then_inc(proj_done[c], 1)

            def inverse(key, done):
                for k in range(KD):
                    for ft in range(NF):
                        half_, reim = divmod(ft, 2)
                        last = nc.tensor.matmul(cbank[k][:, 256 * half_:256 * half_ + 256],
                                                prod[key][:, half_, reim, k * P:(k + 1) * P], inv[:, ft, :],
                                                start=(reim == 0), stop=(reim == 1), skip_group_check=True)
                    last.then_inc(done, 1)

            def front(b, part):
                if part == 0:
                    dft("x", b)
                    dft("c", b)
                    if first(b):
                        pe.wait_ge(loaded, 16 * 6)
                    if not first(b):
                        pe.wait_ge(proj_ready["q"], 2 * b)
                        wait_past(pe, res_ready, 2 * b - 2)
                    project("q", b)
                    if not first(b):
                        pe.wait_ge(proj_ready["v"], 2 * b)
                    project("k", b)
                elif part == 1:
                    pe.wait_ge(prod_ready["q"], b + 1)
                    if not first(b):
                        pe.wait_ge(sums_ready, 2 * b)
                        wait_past(pe, agg_sums, 2 * b - 2)
                    inverse("q", corr_done)
                else:
                    pe.wait_ge(proj_ready["k"], 2 * b + 2)
                    project("v", b)

            def early_logits():
                pe.wait_ge(wr_loaded, 16)
                pe.wait_ge(x2_ready, EARLY)
                pe.wait_ge(proj_ready["v"], 2 * B)
                pe.wait_ge(agg_sums, 2 * B - 2)

                def logits_of(g):
                    pe.wait_ge(lx_copied, g + 1)
                    for n in (2 * g, 2 * g + 1):
                        for k in range(KD):
                            end = nc.tensor.matmul(cbank[0][:, n * NE:(n + 1) * NE], early_x(g)[:, n % 2, k, :],
                                                   routing["wr"][:, k, :], start=(k == 0), stop=(k == KD - 1),
                                                   skip_group_check=True)
                    return end

                for g in range(EARLY // 2):
                    if g >= 2:
                        pe.wait_ge(lx_copied, g - 1)
                    for n in (2 * g, 2 * g + 1):
                        for k in range(KD):
                            end = nc.tensor.transpose(pbank[2 + g % 2][:, n % 2, k * P:(k + 1) * P],
                                                      x2_all[:, n, k * P:(k + 1) * P], ident[:])
                    end.then_inc(lx_done, 1)
                    if g:
                        logits_of(g - 1)
                logits_of(EARLY // 2 - 1).then_inc(logits_done, 1)

            def body(b, front_):
                front_(0)
                if final(b):
                    early_logits()
                for k in range(KD):
                    pe.wait_ge(dcomb_ready, 4 * b + 2 * k + 2)
                    pe.wait_ge(spec_ready["c"], 2 * (b + ahead(b)) + 2)
                    for q in range(4):
                        last = nc.tensor.transpose(tbank[k][:, q * P:(q + 1) * P], dcomb[k][:, q, :], ident[:])
                    last.then_inc(dt_done, 1)
                pe.wait_ge(dt_copied, 2 * b + 2)
                pe.wait_ge(proj_ready["q"], 2 * (b + ahead(b)) + 2)

                def mm(out, cols, q, start=True, stop=True):
                    return nc.tensor.matmul(out, fwd[:, cols], dcomb_t[:, q, :], start=start, stop=stop,
                                            skip_group_check=True)
                mm(pbank[0][0:64, 0, :], RE0, 0)
                mm(pbank[0][64:128, 0, :], RE2, 1)
                mm(pbank[0][0:64, 1, :], IM0, 0)
                mm(pbank[0][64:128, 1, :], IM2, 1).then_inc(wspec_done, 1)
                for reim in range(2):
                    mm(pbank[1][:, reim, :], slice(256 + P * reim, 256 + P * (reim + 1)), 2, stop=False)
                    last = mm(pbank[1][:, reim, :], slice(512 + P * reim, 512 + P * (reim + 1)), 3, start=False)
                last.then_inc(wspec_done, 1)
                front_(2)
                front_(1)
                pe.wait_ge(prod_ready["v"], b + 1)
                pe.wait_ge(sums_ready, 2 * (b + ahead(b)) + 2)
                if final(b):
                    pe.wait_ge(logits_kept, 1)
                inverse("v", agg_done)
                pe.wait_ge(agg_ready, 4 * b + 4)
                pe.wait_ge(wspec_ready, 2 * b + 2)
                for tt in range(CB):
                    for k in range(KD):
                        last = nc.tensor.matmul(pbank[tt // 2][:, tt % 2, :], agg_t[k][:, tt * P:(tt + 1) * P],
                                                wts["o"][:, k, :], start=(k == 0), stop=(k == KD - 1),
                                                skip_group_check=True)
                    if tt % 2:
                        last.then_inc(out_done, 1)

            pe.wait_ge(fwd_loaded, 16)
            schedule(pe, front, body)

        @block.scalar
        def _(act):
            def copy(out, in_, done):
                nc.scalar.activation(out, in_, ACT.Copy).then_inc(done, 1)

            def front(b, part):
                if part == 0:
                    for c in "xc":
                        for k in range(KD):
                            act.wait_ge(dft_done[c], 2 * b + k + 1)
                            copy(spec[c][:, k, :], tbank[k][:], spec_ready[c])
                elif part == 3:
                    if not first(b):
                        act.wait_ge(mul_ready["q"], 4 * b)
                    for c in "qk":
                        for i in range(2):
                            act.wait_ge(proj_done[c], 2 * b + i + 1)
                            copy(proj[c][:, i, :, :], pbank[i + (0 if c == "q" else 2)][:], proj_ready[c])
                elif part == 1:
                    for k in range(KD):
                        act.wait_ge(corr_done, 2 * b + k + 1)
                        if not first(b):
                            act.wait_ge(corr_ready, 4 * b)
                            wait_past(act, agg_ready, 4 * b - 4)
                        copy(half_sums[k][:], cbank[k][:], sums_ready)
                else:
                    for i in range(2):
                        act.wait_ge(proj_done["v"], 2 * b + i + 1)
                        if not first(b):
                            act.wait_ge(prod_ready["v"], b)
                        copy(proj["v"][:, i, :, :], pbank[2 + i][:], proj_ready["v"])

            def body(b, front_):
                front_(0)
                for k in range(KD):
                    act.wait_ge(nmax_ready, 2 * b + k + 1)
                    nc.scalar.activation(texp[k][:], top[k][:, 0:TOPK], ACT.Exp, bias=nmax[k][:],
                                         accum_out=tsum[k][:]).then_inc(texp_ready, 1)
                    act.wait_ge(corr8_ready, 2 * b + k + 1)
                    nc.scalar.activation(corr[k][:], corr[k][:], ACT.Exp, bias=nmax[k][:]).then_inc(exp_ready, 1)
                    act.wait_ge(taken_ready, 2 * b + k + 1)
                    nc.scalar.activation(corr8[k][:], corr8[k][:], ACT.Exp, bias=nmax[k][:]).then_inc(exp_ready, 1)
                    if final(b):
                        for g in range(k * EARLY // 4, (k + 1) * EARLY // 4):
                            act.wait_ge(lx_done, g + 1)
                            copy(early_x(g), pbank[2 + g % 2][:].rearrange("p n (k t) -> p n k t", k=KD), lx_copied)
                front_(3)
                for k in range(KD):
                    act.wait_ge(dt_done, 2 * b + k + 1)
                    copy(dcomb_t[:, :, k * P:(k + 1) * P], tbank[k][:].rearrange("p (q t) -> p q t", q=4), dt_copied)
                wait_past(act, mul_ready["v"], 4 * b)
                for i in range(2):
                    act.wait_ge(wspec_done, 2 * b + i + 1)
                    copy(wspec[:, i, :, :], pbank[i][:], wspec_ready)
                front_(1)
                front_(2)
                for k in range(KD):
                    act.wait_ge(agg_done, 2 * b + k + 1)
                    act.wait_ge(corr_ready, 4 * (b + ahead(b)) + 4)
                    copy(half_sums[k][:], cbank[k][:], agg_sums)

            act.wait_ge(bias_loaded, 16 * 3)
            nc.scalar.activation(dc_bias[:], dc_bias[:], ACT.Copy, scale=float(T)).then_inc(bias_ready, 1)
            schedule(act, front, body, (0, 3, 1, 2))

        @block.vector
        def _(dve):
            V = nc.vector
            held = (loaded, 16 * 6)

            def bias_at_dc(c, b):
                i = "qkv".index(c)
                dve.wait_ge(proj_ready[c], 2 * b + 2)
                V.tensor_tensor(proj[c][0:1, 0, 0, :], proj[c][0:1, 0, 0, :], dc_bias[0:1, i, :], ALU.add).then_inc(dc_ready[c], 1)
                dve.wait_ge(dc_ready[c], b + 1)

            def multiply(key, b, p, q):
                re, im = (lambda t: t[:, :, 0, :]), (lambda t: t[:, :, 1, :])
                for i, (x, y) in enumerate(((re(p), re(q)), (im(p), im(q)), (im(p), re(q)), (re(p), im(q)))):
                    V.tensor_tensor(m[i][:], x, y, ALU.mult).then_inc(mul_ready[key], 1)
                dve.wait_ge(mul_ready[key], 4 * b + 4)
                V.tensor_tensor(prod[key][:, :, 0, :], m[0][:], m[1][:], ALU.add).then_inc(add_ready[key], 1)
                V.tensor_tensor(prod[key][:, :, 1, :], m[2][:], m[3][:], ALU.subtract).then_inc(add_ready[key], 1)
                dve.wait_ge(add_ready[key], 2 * b + 2)
                V.tensor_copy(prod[key][0:1, 0, 0, :], m[0][0:1, 0, :])
                V.tensor_copy(prod[key][0:1, 0, 1, :], m[1][0:1, 0, :]).then_inc(prod_ready[key], 1)

            def unfold(out, sums, done, k):
                V.tensor_tensor(out[:, 0:256], sums[:, 0:256], sums[:, 256:512], ALU.add).then_inc(done, 1)
                V.tensor_tensor(out[:, 256:512], sums[:, 0:256], sums[:, 256:512], ALU.subtract).then_inc(done, 1)

            def front(b, part):
                if part == 1:
                    bias_at_dc("q", b)
                    bias_at_dc("k", b)
                    multiply("q", b, proj["q"], proj["k"])
                elif part == 2:
                    for k in range(KD):
                        dve.wait_ge(sums_ready, 2 * b + k + 1)
                        unfold(corr[k], half_sums[k], corr_ready, k)

            def largest(b, k):
                wait_apart(dve, corr_ready, 4 * b + 2 * k + 2, held)
                V.max(top[k][:, 0:8], corr[k][:]).then_inc(top8_ready, 1)
                wait_apart(dve, top8_ready, 2 * b + k + 1, held)
                V.match_replace(corr8[k][:], top[k][:, 0:8], corr[k][:], FAR).then_inc(corr8_ready, 1)
                wait_apart(dve, corr8_ready, 2 * b + k + 1, held)
                V.max(top[k][:, 8:16], corr8[k][:]).then_inc(top16_ready, 1)
                dve.wait_ge(top16_ready, 2 * b + k + 1)
                V.tensor_scalar(nmax[k][:], top[k][:, 0:1], -1.0, None, ALU.mult).then_inc(nmax_ready, 1)
                V.memset(top[k][:, TOPK:16], FAR).then_inc(far_ready, 1)
                wait_apart(dve, far_ready, 2 * b + k + 1, held)
                V.match_replace(corr8[k][:], top[k][:, 8:16], corr8[k][:], FAR).then_inc(taken_ready, 1)

            def weights(b):
                for k in range(KD):
                    dve.wait_ge(texp_ready, 2 * b + k + 1)
                    V.reciprocal(rsum[k][:], tsum[k][:]).then_inc(rsum_ready, 1)
                for k in range(KD):
                    dve.wait_ge(exp_ready, 4 * b + 2 * k + 2)
                    V.tensor_tensor(corr[k][:], corr[k][:], corr8[k][:], ALU.subtract).then_inc(weight_ready, 1)
                dve.wait_ge(rsum_ready, 2 * b + 2)
                for k in range(KD):
                    dve.wait_ge(weight_ready, 2 * b + k + 1)
                    V.tensor_scalar(corr[k][:], corr[k][:], rsum[k][:], None, ALU.mult).then_inc(scaled_ready, 1)
                for k in range(KD):
                    dve.wait_ge(scaled_ready, 2 * b + k + 1)
                    quarters = corr[k][:].rearrange("p (j t) -> p j t", j=4)
                    V.tensor_tensor(dfold[k][:], quarters[:, 0:2, :], quarters[:, 2:4, :], ALU.add).then_inc(dfold_ready, 1)
                    V.tensor_tensor(dcomb[k][:, 2:4, :], quarters[:, 0:2, :], quarters[:, 2:4, :], ALU.subtract).then_inc(dfold_ready, 1)
                for k in range(KD):
                    dve.wait_ge(dfold_ready, 4 * b + 2 * k + 2)
                    V.tensor_tensor(dcomb[k][:, 0, :], dfold[k][:, 0, :], dfold[k][:, 1, :], ALU.add).then_inc(dcomb_ready, 1)
                    V.tensor_tensor(dcomb[k][:, 1, :], dfold[k][:, 0, :], dfold[k][:, 1, :], ALU.subtract).then_inc(dcomb_ready, 1)

            def residual(b):
                dve.wait_ge(xbo_ready, b + 1)
                for i in range(2):
                    dve.wait_ge(out_done, 2 * b + i + 1)
                    V.tensor_tensor(xbo[:, 2 * i:2 * i + 2, :], pbank[i][:], xbo[:, 2 * i:2 * i + 2, :], ALU.add).then_inc(res_ready, 1)

            def layernorm(b):
                for j in range(CB):
                    dve.wait_ge(res_ready, 2 * b + j // 2 + 1)
                    V.bn_stats(stats[:, j, :], xbo[:, j, :]).then_inc(stats_ready, 1)
                for j in range(CB):
                    wait_apart(dve, stats_ready, 4 * b + j + 1, held)
                    V.bn_aggr(mv[:, j, :], stats[:, j, :]).then_inc(mv_ready, 1)
                dve.wait_ge(mv_ready, 4 * b + 4)
                V.tensor_scalar(var[:], mv[:, :, 1], EPS, None, ALU.add).then_inc(var_ready, 1)

            def normed(b):
                dve.wait_ge(rstd_ready, b + 1)
                V.scalar_tensor_tensor(shift[:], mv[:, :, 0], -1.0, rstd[:], ALU.mult, ALU.mult).then_inc(shift_ready, 1)
                dve.wait_ge(shift_ready, b + 1)
                for j in range(CB):
                    V.tensor_scalar(x2_all[:, ds(b * CB + j, 1), :].rearrange("p a d -> p (a d)"), xbo[:, j, :],
                                    rstd[:, j:j + 1], shift[:, j:j + 1], ALU.mult, ALU.add).then_inc(x2_ready, 1)

            def body(b, front_):
                largest(b, 0)
                if not first(b):
                    residual(b - 1)
                largest(b, 1)
                if not first(b):
                    layernorm(b - 1)
                weights(b)
                if not first(b):
                    normed(b - 1)
                if final(b):
                    dve.wait_ge(logits_done, 1)
                    V.tensor_copy(logit[:, 0:EARLY, :].rearrange("p n e -> p (n e)"),
                                  cbank[0][:, 0:EARLY * NE]).then_inc(logits_kept, 1)
                front_(1)
                bias_at_dc("v", b)
                dve.wait_ge(wspec_ready, 2 * b + 2)
                dve.wait_ge(prod_ready["q"], b + ahead(b) + 1)
                multiply("v", b, proj["v"], wspec)
                front_(2)
                for k in range(KD):
                    dve.wait_ge(agg_sums, 2 * b + k + 1)
                    unfold(agg_t[k], half_sums[k], agg_ready, k)

            dve.wait_ge(loaded, 16 * 6)
            dve.wait_ge(bias_ready, 1)
            schedule(dve, front, body)
            residual(B - 1)
            layernorm(B - 1)
            normed(B - 1)

        @block.gpsimd
        def _(pool):
            G = nc.gpsimd
            G.memset(half[:], -0.5).then_inc(half_ready, 1)
            pool.wait_ge(half_ready, 1)

            def four_quarters(c, b, src):
                G.tensor_tensor(fold[c][:], src[:, 0:2, :], src[:, 2:4, :], ALU.add).then_inc(fold_ready[c], 1)
                G.tensor_tensor(comb[c][:, 2:4, :], src[:, 0:2, :], src[:, 2:4, :], ALU.subtract).then_inc(fold_ready[c], 1)
                pool.wait_ge(fold_ready[c], 2 * b + 2)
                G.tensor_tensor(comb[c][:, 0, :], fold[c][:, 0, :], fold[c][:, 1, :], ALU.add).then_inc(comb_ready[c], 1)
                G.tensor_tensor(comb[c][:, 1, :], fold[c][:, 0, :], fold[c][:, 1, :], ALU.subtract).then_inc(comb_ready[c], 1)

            def combine(b):
                for c in "xc":
                    if not first(b):
                        pool.wait_ge(dft_done[c], 2 * b)
                    if c == "c":
                        pool.wait_ge(ctx_loaded, 16 * b + 16)
                    four_quarters(c, b, x1_all[:, ds(b * CB, CB), :] if c == "x" else ctx_in)

            def residual(b):
                if not first(b):
                    pool.wait_ge(x2_ready, CB * b)
                G.tensor_tensor(xbo[:], x1_all[:, ds(b * CB, CB), :], bo[:].unsqueeze(1).broadcast_to([P, CB, D]),
                                ALU.add).then_inc(xbo_ready, 1)

            def inverse_deviation(b):
                pool.wait_ge(var_ready, b + 1)
                G.tensor_tensor(rstd[:], var[:], half[:], ALU.pow).then_inc(rstd_ready, 1)

            combine(0)
            combine(1)
            pool.wait_ge(loaded, 16 * 6)
            residual(0)
            with pool.Fori(0, B - 2) as b:
                combine(b + 2)
                inverse_deviation(b)
                residual(b + 1)
            inverse_deviation(B - 2)
            residual(B - 1)
            inverse_deviation(B - 1)




def experts_stage(nc, a, ident, x_rows, w1, routing, logit, out, xs_dram):
    x2_all = x_rows[:, :, 0:D]
    wr, br, order, edges, index, mask_strict, token = (
        routing[c] for c in ("wr", "br", "order", "edges", "index", "mask_strict", "token"))
    with ExitStack() as ctx:
        sb, ps, sem, start_block = tensors(nc, ctx, "ex_")
        w2 = sb("w2", [P, NE, FT, D])
        b1 = sb("b1", [P, NE, FT])
        b2 = sb("b2", [P, NE, D])
        ones = sb("ones", [P, P])
        half = sb("half", [P, 1])
        xr = [sb(f"xr{i}", [P, 2, KD, P]) for i in range(2)]
        ex, onehot = sb("exps", [P, NT, NE]), sb("onehot", [P, NT, NE])
        rank, tot, incl = sb("rank", [P, NT, NE]), sb("tot", [P, NT, NE]), sb("incl", [P, NT, NE])
        top, gate = sb("top", [P, NT]), sb("gate", [P, NT])
        over = sb("over", [P, NE, NT])
        tiles, tend, tstart = sb("tiles", [P, NE]), sb("tend", [P, NE]), sb("tstart", [P, NE])
        row_start = sb("row_start", [P, NE])
        starts = sb("starts", [P, TILES, NE])
        expert_f, expert = sb("expert_f", [P, TILES]), sb("expert", [P, TILES], I32)
        pos_f, pos = sb("pos_f", [P, NT]), sb("pos", [P, NT], I32)
        x_in = [sb(f"x_in{u}", [P, XW]) for u in range(2)]
        row = [sb(f"row{u}", [P, XW]) for u in range(2)]
        x_t = sb("x_t", [P, KD, P])
        h = sb("h", [P, F])
        h_t = sb("h_t", [P, FT, P])
        b1_now = sb("b1_now", [P, FT])
        y = sb("y", [P, D])
        number = [sb(f"number{u}", [P, 1], I32) for u in range(2)]
        result = [sb(f"result{u}", [P, D]) for u in range(2)]
        stats, mv = sb("stats", [P, 6]), sb("mv", [P, 2])
        var, rstd, shift = sb("var", [P, 1]), sb("rstd", [P, 1]), sb("shift", [P, 1])
        ps_r = [ps(f"r{i}", [P, 2, KD, P]) for i in range(2)]
        ps_l = ps("l", [P, NT, NE])
        ps_h = [ps(f"h_ps{i}", [P, 512]) for i in range(2)]
        ps_ht = [ps(f"ht{i}", [P, 4, P]) for i in range(2)]
        ps_y = ps("y_ps", [P, D])
        ps_x = ps_r[0]

        b_loaded = sem("b_loaded")
        w_loaded, ones_ready, half_ready, row_ready = (
            sem(q) for q in ("w_loaded", "ones_ready", "half_ready", "row_ready"))
        logit_ready = sem("logit_ready")
        rt_done, rt_copied, logits_done = sem("rt_done"), sem("rt_copied"), sem("logits_done")
        route, diff_ready, ex_ready, onehot_ready = sem("route"), sem("diff_ready"), sem("ex_ready"), sem("onehot_ready")
        counts_done, pos_ready, expert_ready = sem("counts_done"), sem("pos_ready"), sem("expert_ready")
        scattered, xt_done, xt_copied = sem("scattered"), sem("xt_done"), sem("xt_copied")
        x_loaded = [sem(f"x_loaded{u}") for u in range(2)]
        stored = [sem(f"stored{u}") for u in range(2)]
        h_done, h_copied, ht_done, relu_ready = sem("h_done"), sem("h_copied"), sem("ht_done"), sem("relu_ready")
        b1_ready, y_done, y_ready, row_used = (sem(q) for q in ("b1_ready", "y_done", "y_ready", "row_used"))
        row_kept = sem("row_kept")
        stats_ready, mv_ready, var_ready, rstd_ready, shift_ready, result_ready = (
            sem(q) for q in ("stats_ready", "mv_ready", "var_ready", "rstd_ready", "shift_ready", "result_ready"))
        block = start_block()

        def tiles_in_pairs(eng, step, lo, hi):
            with eng.Fori(lo // 2, hi // 2) as it:
                step(2 * it, 0)
                step(2 * it + 1, 1)

        @block.sync
        def _(sp):
            sp.dma_start(b1[:], a["ffn_b1_cols"]).then_inc(b_loaded, 16)
            sp.dma_start(b2[:], a["ffn_b2"].rearrange("(o e) d -> o e d", o=1).broadcast_to([P, NE, D])).then_inc(b_loaded, 16)
            for e in range(NE):
                sp.dma_start(w2[:, e, :, :], a["ffn_W2"][e, :, :].rearrange("(f p) d -> p f d", p=P)).then_inc(w_loaded, 16)

            def load(j, u):
                start = j * P if isinstance(j, int) else sp.snap(j * P)
                if not (isinstance(j, int) and j < 2):
                    sp.wait_ge(xt_done, j - 1)
                    sp.wait_ge(row_kept, j - 1)
                sp.dma_start(x_in[u][:], xs_dram[ds(start, P), :]).then_inc(x_loaded[u], 16)

            sp.wait_ge(scattered, 16 * NT)
            load(0, 0)
            load(1, 1)
            tiles_in_pairs(sp, load, 2, TILES - 1)
            load(TILES - 1, 0)
            sp.wait_ge(stored[0], 16 * (TILES // 2 + 1))
            sp.wait_ge(stored[1], 16 * (TILES // 2))

        @block.tensor
        def _(pe):
            pairs = (NT - EARLY) // 2


            def logits(g):
                pe.wait_ge(rt_copied, g + 1)
                for n in (EARLY + 2 * g, EARLY + 2 * g + 1):
                    for k in range(KD):
                        last = nc.tensor.matmul(ps_l[:, n, :], xr[g % 2][:, n % 2, k, :], wr[:, k, :],
                                                start=(k == 0), stop=(k == KD - 1), skip_group_check=True)
                return last

            for g in range(pairs):
                if g >= 2:
                    pe.wait_ge(rt_copied, g - 1)
                for n in (EARLY + 2 * g, EARLY + 2 * g + 1):
                    for k in range(KD):
                        last = nc.tensor.transpose(ps_r[g % 2][:, n % 2, k, :], x2_all[:, n, k * P:(k + 1) * P], ident[:])
                last.then_inc(rt_done, 1)
                if g:
                    logits(g - 1)
            logits(pairs - 1).then_inc(logits_done, 1)
            pe.wait_ge(onehot_ready, 1)
            pe.wait_ge(ones_ready, 1)
            flat = onehot[:].rearrange("p n e -> p (n e)")
            nc.tensor.matmul(ps_h[0][:, 0:NT * NE], mask_strict[:], flat, start=True, stop=True)
            nc.tensor.matmul(ps_h[1][:, 0:NT * NE], ones[:], flat, start=True, stop=True).then_inc(counts_done, 1)

            def x_transposes(j, u):
                pe.wait_ge(x_loaded[u], 8 * (j - u) + 16)
                if not (isinstance(j, int) and j == 0):
                    pe.wait_ge(xt_copied, j)
                for k in range(KD):
                    last = nc.tensor.transpose(ps_x[:, 0, k, :], x_in[u][:, k * P:(k + 1) * P], ident[:])
                last.then_inc(xt_done, 1)

            def up(j, e):
                pe.wait_ge(xt_copied, j + 1)
                for i in range(2):
                    if not (isinstance(j, int) and j == 0):
                        pe.wait_ge(h_copied, 2 * j + i - 1)
                    for k in range(KD):
                        last = nc.tensor.matmul(ps_h[i][:], x_t[:, k, :],
                                                w1[:, ds(e, 1), k, i * 512:(i + 1) * 512].rearrange("p o f -> p (o f)"),
                                                start=(k == 0), stop=(k == KD - 1))
                    last.then_inc(h_done, 1)

            def h_transposes(j):
                for i in range(2):
                    pe.wait_ge(h_copied, 2 * j + i + 1)
                    if not (isinstance(j, int) and j == 0):
                        pe.wait_ge(relu_ready, 8 * j + 4 * i - 4)
                    for f in range(4):
                        last = nc.tensor.transpose(ps_ht[i][:, f, :], h[:, (4 * i + f) * P:(4 * i + f + 1) * P], ident[:])
                    last.then_inc(ht_done, 1)

            def down(j, e):
                pe.wait_ge(relu_ready, 8 * j + 8)
                if not (isinstance(j, int) and j == 0):
                    pe.wait_ge(y_ready, j)
                for f in range(FT):
                    last = nc.tensor.matmul(ps_y[:], h_t[:, f, :], w2[:, ds(e, 1), f, :].rearrange("p o d -> p (o d)"),
                                            start=(f == 0), stop=(f == FT - 1))
                last.then_inc(y_done, 1)

            def expert_of(j):
                return pe.value_load(expert[0:1, ds(j, 1)], min_val=0, max_val=NE - 1)

            pe.wait_ge(expert_ready, 1)
            e0 = expert_of(0)
            x_transposes(0, 0)
            up(0, e0)
            x_transposes(1, 1)
            h_transposes(0)

            def step(j, u):
                e_up, e_down = expert_of(j + 1), expert_of(j)
                up(j + 1, e_up)
                x_transposes(j + 2, u)
                down(j, e_down)
                h_transposes(j + 1)

            pe.wait_ge(w_loaded, 16 * NE)
            step(0, 0)
            step(1, 1)
            tiles_in_pairs(pe, step, 2, TILES - 3)
            step(TILES - 3, 0)
            j = TILES - 2
            e_up, e_down = expert_of(j + 1), expert_of(j)
            up(j + 1, e_up)
            down(j, e_down)
            h_transposes(j + 1)
            down(j + 1, e_up)

        @block.scalar
        def _(act):
            for g in range((NT - EARLY) // 2):
                if g >= 2:
                    act.wait_ge(rt_done, g)
                act.wait_ge(rt_done, g + 1)
                nc.scalar.activation(xr[g % 2][:], ps_r[g % 2][:], ACT.Copy).then_inc(rt_copied, 1)
            act.wait_ge(diff_ready, 1)
            nc.scalar.activation(ex[:], ex[:], ACT.Exp).then_inc(ex_ready, 1)

            def x_copy(j):
                act.wait_ge(xt_done, j + 1)
                nc.scalar.activation(x_t[:], ps_x[:, 0, :, :], ACT.Copy).then_inc(xt_copied, 1)

            def keep(j, u):
                act.wait_ge(x_loaded[u], 8 * (j - u) + 16)
                if not (isinstance(j, int) and j < 2):
                    act.wait_ge(row_used, 2 * j - 2)
                nc.scalar.activation(row[u][:], x_in[u][:], ACT.Copy).then_inc(row_kept, 1)

            def h_copies(j):
                for i in range(2):
                    act.wait_ge(h_done, 2 * j + i + 1)
                    nc.scalar.activation(h[:, i * 512:(i + 1) * 512], ps_h[i][:], ACT.Copy).then_inc(h_copied, 1)

            x_copy(0)
            h_copies(0)
            keep(0, 0)
            x_copy(1)
            keep(1, 1)

            def step(j, u):
                h_copies(j + 1)
                x_copy(j + 2)
                keep(j + 2, u)

            tiles_in_pairs(act, step, 0, TILES - 3)
            step(TILES - 3, 0)
            h_copies(TILES - 1)

        @block.vector
        def _(dve):
            V = nc.vector
            made = [0]

            def then(ins):
                made[0] += 1
                ins.then_inc(route, 1)
                dve.wait_ge(route, made[0])

            def over_experts(t):
                return t.unsqueeze(2).broadcast_to([P, NT, NE])

            def over_tiles(t):
                return t.unsqueeze(1).broadcast_to([P, NT, NE])

            V.memset(ones[:], 1.0).then_inc(ones_ready, 1)
            dve.wait_ge(ones_ready, 1)
            V.tensor_tensor(logit[:, 0:EARLY, :], logit[:, 0:EARLY, :],
                            br[:].unsqueeze(1).broadcast_to([P, EARLY, NE]), ALU.add).then_inc(logit_ready, 1)
            dve.wait_ge(logits_done, 1)
            late = slice(EARLY, NT)
            V.tensor_tensor(logit[:, late, :], ps_l[:, late, :],
                            br[:].unsqueeze(1).broadcast_to([P, NT - EARLY, NE]), ALU.add).then_inc(logit_ready, 1)
            dve.wait_ge(logit_ready, 2)
            then(V.tensor_reduce(top[:], logit[:], AX, ALU.max))
            V.tensor_tensor(ex[:], logit[:], over_experts(top[:]), ALU.subtract).then_inc(diff_ready, 1)
            then(V.tensor_tensor(onehot[:], logit[:], over_experts(top[:]), ALU.is_equal))
            then(V.tensor_tensor(onehot[:], onehot[:], over_tiles(order[:]), ALU.mult))
            then(V.tensor_reduce(top[:], onehot[:], AX, ALU.max))
            V.tensor_tensor(onehot[:], onehot[:], over_experts(top[:]), ALU.is_equal).then_inc(onehot_ready, 1)
            dve.wait_ge(ex_ready, 1)
            then(V.tensor_reduce(gate[:], ex[:], AX, ALU.add))
            V.reciprocal(x_rows[:, :, GATE], gate[:]).then_inc(row_ready, 1)
            V.tensor_scalar(x_rows[:, :, NUMBER], token[:], 1.0, None, ALU.mult).then_inc(row_ready, 1)
            dve.wait_ge(counts_done, 1)
            then(V.tensor_copy(rank[:].rearrange("p n e -> p (n e)"), ps_h[0][:, 0:NT * NE]))
            then(V.tensor_copy(tot[:].rearrange("p n e -> p (n e)"), ps_h[1][:, 0:NT * NE]))
            for e in range(NE):
                then(V.tensor_tensor_scan(incl[:, :, e], ones[:, 0:NT], tot[:, :, e], 0.0, ALU.mult, ALU.add))
            then(V.tensor_tensor(over[:], incl[:, NT - 1, :].unsqueeze(2).broadcast_to([P, NE, NT]),
                                 edges[:].unsqueeze(1).broadcast_to([P, NE, NT]), ALU.is_gt))
            then(V.tensor_reduce(tiles[:], over[:], AX, ALU.add))
            then(V.tensor_tensor_scan(tend[:], ones[:, 0:NE], tiles[:], 0.0, ALU.mult, ALU.add))
            then(V.tensor_tensor(tstart[:], tend[:], tiles[:], ALU.subtract))
            then(V.tensor_tensor(rank[:], rank[:], incl[:], ALU.add))
            then(V.tensor_tensor(rank[:], rank[:], tot[:], ALU.subtract))
            then(V.tensor_scalar(row_start[:], tstart[:], float(P), None, ALU.mult))
            then(V.tensor_tensor(rank[:], rank[:], over_tiles(row_start[:]), ALU.add))
            then(V.tensor_tensor(rank[:], rank[:], onehot[:], ALU.mult))
            then(V.tensor_reduce(pos_f[:], rank[:], AX, ALU.add))
            V.tensor_copy(pos[:], pos_f[:]).then_inc(pos_ready, 1)
            then(V.tensor_tensor(starts[:], index[:].unsqueeze(2).broadcast_to([P, TILES, NE]),
                                 tstart[:].unsqueeze(1).broadcast_to([P, TILES, NE]), ALU.is_ge))
            then(V.tensor_reduce(expert_f[:], starts[:], AX, ALU.add))
            V.tensor_scalar(expert[:], expert_f[:], -1.0, None, ALU.add).then_inc(expert_ready, 1)
            dve.wait_ge(expert_ready, 1)
            dve.wait_ge(b_loaded, 32)

            def expert_of(j):
                return dve.value_load(expert[0:1, ds(j, 1)], min_val=0, max_val=NE - 1)

            def relus(j, e):
                if not (isinstance(j, int) and j == 0):
                    dve.wait_ge(relu_ready, 8 * j)
                V.tensor_scalar(b1_now[:], b1[:, ds(e, 1), :].rearrange("p o f -> p (o f)"), 1.0, None,
                                ALU.mult).then_inc(b1_ready, 1)
                dve.wait_ge(b1_ready, j + 1)
                for i in range(2):
                    dve.wait_ge(ht_done, 2 * j + i + 1)
                    for f in range(4):
                        V.tensor_scalar(h_t[:, 4 * i + f, :], ps_ht[i][:, f, :], b1_now[:, 4 * i + f:4 * i + f + 1], 0.0,
                                        ALU.add, ALU.max).then_inc(relu_ready, 1)

            held = (b_loaded, 32)

            def y_out(j, e):
                dve.wait_ge(y_done, j + 1)
                V.tensor_tensor(y[:], ps_y[:], b2[:, ds(e, 1), :].rearrange("p o d -> p (o d)"), ALU.add).then_inc(y_ready, 1)

            def total(j, u):
                if not (isinstance(j, int) and j < 2):
                    dve.wait_ge(stored[u], 8 * (j - u))
                dve.wait_ge(row_kept, j + 1)
                V.tensor_scalar(number[u][:], row[u][:, NUMBER:NUMBER + 1], 1.0, None, ALU.mult).then_inc(row_used, 1)
                dve.wait_ge(y_ready, j + 1)
                V.scalar_tensor_tensor(result[u][:], y[:], row[u][:, GATE:GATE + 1], row[u][:, 0:D],
                                       ALU.mult, ALU.add).then_inc(row_used, 1)
                dve.wait_ge(row_used, 2 * j + 2)
                V.bn_stats(stats[:], result[u][:]).then_inc(stats_ready, 1)
                wait_apart(dve, stats_ready, j + 1, held)
                V.bn_aggr(mv[:], stats[:]).then_inc(mv_ready, 1)
                dve.wait_ge(mv_ready, j + 1)
                V.tensor_scalar(var[:], mv[:, 1:2], EPS, None, ALU.add).then_inc(var_ready, 1)

            def normed(j, u):
                dve.wait_ge(rstd_ready, j + 1)
                V.scalar_tensor_tensor(shift[:], mv[:, 0:1], -1.0, rstd[:], ALU.mult, ALU.mult).then_inc(shift_ready, 1)
                dve.wait_ge(shift_ready, j + 1)
                V.tensor_scalar(result[u][:], result[u][:], rstd[:], shift[:], ALU.mult, ALU.add).then_inc(result_ready, 1)

            relus(0, expert_of(0))

            def step(j, u):
                e_down, e_up = expert_of(j), expert_of(j + 1)
                y_out(j, e_down)
                relus(j + 1, e_up)
                total(j, u)
                normed(j, u)

            step(0, 0)
            step(1, 1)
            tiles_in_pairs(dve, step, 2, TILES - 1)
            y_out(TILES - 1, expert_of(TILES - 1))
            total(TILES - 1, 0)
            normed(TILES - 1, 0)

        @block.gpsimd
        def _(pool):
            nc.gpsimd.memset(half[:], -0.5).then_inc(half_ready, 1)
            pool.wait_ge(half_ready, 1)
            pool.wait_ge(pos_ready, 1)
            pool.wait_ge(row_ready, 2)
            for n in range(NT):
                nc.gpsimd.indirect_dma_start(out=xs_dram, out_offset=bass.IndirectOffsetOnAxis(ap=pos[:, n:n + 1], axis=0),
                                             in_=x_rows[:, n, :], in_offset=None).then_inc(scattered, 16)
            for j in range(TILES):
                pool.wait_ge(var_ready, j + 1)
                nc.gpsimd.tensor_tensor(rstd[:], var[:], half[:], ALU.pow).then_inc(rstd_ready, 1)
                pool.wait_ge(result_ready, j + 1)
                nc.gpsimd.indirect_dma_start(out=out, out_offset=bass.IndirectOffsetOnAxis(ap=number[j % 2][:], axis=0),
                                             in_=result[j % 2][:], in_offset=None,
                                             bounds_check=B * T - 1, oob_is_err=False).then_inc(stored[j % 2], 16)


def constants():
    import numpy as np
    i = np.arange(P)
    row, colm = i[:, None], i[None, :]
    c = {"ident": np.eye(P), "mask_incl": row <= colm, "mask_strict": row < colm}
    keep = np.ones((P, NT, H))
    keep[:, CB - 1::CB, :] = 0
    c["keep"] = keep.reshape(P, NT * H)

    def joins(b):
        return (row // (2 * b) == colm // (2 * b)) & (row // b % 2 == 1) & (colm // b % 2 == 0)

    c["mask_one"] = joins(1).T | (row == colm)
    c["mask_levels"] = np.stack([joins(2 << lev) | (row == colm) for lev in range(LEVELS - 1)], axis=1)

    c["order"] = np.tile(np.arange(NE, 0, -1), (P, 1))
    c["edges"] = np.tile(P * np.arange(NT), (P, 1))
    c["index"] = np.tile(np.arange(TILES), (P, 1))
    c["token"] = row + P * np.arange(NT)[None, :]
    c["empty"] = np.hstack([np.zeros((P, D + 1)), B * T + row])
    p, m64, m128 = np.arange(P)[:, None], np.arange(64)[None, :], np.arange(P)[None, :]

    def angle(f, t):
        return 2 * np.pi * ((f * t) % T) / T

    re0, im0 = np.cos(angle(4 * m64, p)), -np.sin(angle(4 * m64, p))
    im0[:, 0] = np.cos(angle(T // 2, p))[:, 0]
    re2, im2 = np.cos(angle(4 * m64 + 2, p)), -np.sin(angle(4 * m64 + 2, p))
    c1, s1 = np.cos(angle(4 * m128 + 1, p)), np.sin(angle(4 * m128 + 1, p))
    c["dft_fwd"] = np.concatenate([re0, im0, re2, im2, c1, -s1, -s1, -c1], axis=1)
    weight = np.where(m64.T == 0, 1.0, 2.0) / T
    z0re, z0im = weight * re0.T, weight * im0.T
    z2re, z2im = 2 / T * re2.T, 2 / T * im2.T
    even_re = np.concatenate([np.hstack([z0re, z0re]), np.hstack([z2re, -z2re])])
    even_im = np.concatenate([np.hstack([z0im, z0im]), np.hstack([z2im, -z2im])])
    odd_re = 2 / T * np.hstack([c1.T, -s1.T])
    odd_im = 2 / T * np.hstack([-s1.T, -c1.T])
    c["dft_inv"] = np.stack([even_re, even_im, odd_re, odd_im], axis=1)
    return {k: np.ascontiguousarray(v, np.float32) for k, v in c.items()}


def program(nc, a, out):
    def dram(name, shape):
        return nc.dram_tensor(name, shape, F32, kind="Internal").ap()

    qkv_dram, grow_dram = dram("qkv_dram", (B * T, 3 * HW)), dram("grow_dram", (NT * H, P))
    o_dram, xs_dram = dram("o_dram", (NT * P, H * P)), dram("xs_dram", (TILES * P, XW))
    with ExitStack() as ctx:
        def keep(stack, name, shape):
            return stack.enter_context(nc.sbuf_tensor(name, shape, F32))

        ident = keep(ctx, "ident", [P, P])
        x_rows = keep(ctx, "x_rows", [P, NT, XW])
        ident_loaded = ctx.enter_context(nc.semaphore("ident_loaded"))
        with nc.Block() as block:
            @block.sync
            def _(sp):
                sp.dma_start(ident[:], a["ident"]).then_inc(ident_loaded, 16)
                sp.wait_ge(ident_loaded, 16)
        with ExitStack() as until_ffn:
            ffn_weights = {name: keep(until_ffn, f"ffn_{name}", shape) for name, shape in FFN_SHAPES.items()}
            with ExitStack() as until_delta:
                masks = {name: keep(until_delta, name, shape) for name, shape in MASK_SHAPES.items()}
                scalars = keep(until_delta, "scalars", [P, NT, NSC, H])
                project_stage(nc, a, ident, x_rows, scalars, masks, qkv_dram, grow_dram)
                delta_stage(nc, a, ident, scalars, masks, ffn_weights, qkv_dram, grow_dram, o_dram)
            ffn_stage(nc, ident, o_dram, x_rows, ffn_weights)
        expert_w1 = keep(ctx, "expert_w1", [P, NE, KD, F])
        routing = {name: keep(ctx, f"routing_{name}", shape) for name, shape in ROUTING_SHAPES.items()}
        logit = keep(ctx, "logit", [P, NT, NE])
        xattn_stage(nc, a, ident, x_rows, expert_w1, routing, logit, xs_dram)
        experts_stage(nc, a, ident, x_rows, expert_w1, routing, logit, out, xs_dram)


def kernel(**inputs):
    import numpy as np
    import concourse.bacc as bacc
    from concourse.bass_utils import run_bass_kernel_spmd

    nc = bacc.Bacc("TRN2", target_bir_lowering=False, num_devices=1)
    arrays = {}
    for name, v in inputs.items():
        v = np.ascontiguousarray(v)
        if name in ("x", "ctx_1024"):
            v = v.reshape(B * T, D)
        name = name.replace("L0_attn_", "").replace("L0_", "")
        if name == "ffn_b1":
            name, v = "ffn_b1_cols", np.ascontiguousarray(v.reshape(NE, FT, P).transpose(2, 0, 1))
        arrays[name] = v
    arrays.update(constants())
    a, feed = {}, {}
    for name, v in arrays.items():
        feed[f"in_{name}"] = v
        a[name] = nc.dram_tensor(f"in_{name}", v.shape, mybir.dt.from_np(v.dtype), kind="ExternalInput").ap()
    out = nc.dram_tensor("out", (B * T, D), F32, kind="ExternalOutput").ap()
    program(nc, a, out)
    r = run_bass_kernel_spmd(nc, [feed], core_ids=[0])
    return r.results[0]["out"].reshape(B, T, D)
```
